# Optimizing a Trainium2 kernel written in Bass

```python
import numpy as np
import jax
import jax.numpy as jnp

def _softmax(x, axis=-1):
    return jax.nn.softmax(x, axis=axis)

def _gelu(x):
    return jax.nn.gelu(x, approximate=True)

def _silu(x):
    return jax.nn.silu(x)

def _sigmoid(x):
    return jax.nn.sigmoid(x)

def _layernorm(x, axis=-1, eps=1e-05):
    m = jnp.mean(x, axis=axis, keepdims=True)
    v = jnp.var(x, axis=axis, keepdims=True)
    return (x - m) / jnp.sqrt(v + eps)

def _scatter_add(tgt, idx, src, axis=0):
    return tgt.at[idx].add(src)

def _segment_sum(src, seg, n):
    return jax.ops.segment_sum(src, seg, n)
kernel_name = 'mk_gnn_resnorm_d4_gnn_r8_ef6fef'

def setup_inputs(seed: int=0):
    np.random.seed(seed)
    _w = jnp.asarray

    def _rec_inputs():
        import jax
        import jax.numpy as jnp
        _gk = jax.random.key(seed)
        x = -0.0003713 + 1 * jax.random.normal(jax.random.fold_in(_gk, 1), (6250, 128), jnp.float32)
        _s = jax.random.randint(jax.random.fold_in(_gk, 2), (100000,), 0, 6250, jnp.int32)
        _d = jax.random.randint(jax.random.fold_in(_gk, 3), (100000,), 0, 6250, jnp.int32)
        _loop = jnp.arange(6250, dtype=jnp.int32)
        src = jnp.concatenate([_s, _d, _loop])
        dst = jnp.concatenate([_d, _s, _loop])
        _o = jnp.argsort(dst, stable=True)
        src = src[_o]
        dst = dst[_o]
        edge_type_3 = jax.random.randint(jax.random.fold_in(_gk, 13), (206250,), 0, 3, jnp.int32)
        node_type_3 = jax.random.randint(jax.random.fold_in(_gk, 14), (6250,), 0, 3, jnp.int32)
        return (x, src, dst, edge_type_3, node_type_3)
    x, src, dst, edge_type_3, node_type_3 = _rec_inputs()

    def _L0_gnn_setup():
        import jax, jax.numpy as jnp
        import numpy as np
        N_NODES = 12500
        N_EDGES = 200000
        EMB_DIM = 128
        BN_EPS = 1e-05
        key = jax.random.key(seed)
        k = jax.random.split(key, 5)
        x = jax.random.normal(k[0], (N_NODES, EMB_DIM), dtype=jnp.float32)
        src = jax.random.randint(k[1], (N_EDGES,), 0, N_NODES)
        dst = jax.random.randint(k[2], (N_EDGES,), 0, N_NODES)
        W = jax.random.normal(k[3], (EMB_DIM, EMB_DIM), dtype=jnp.float32) / np.float32(np.sqrt(EMB_DIM))
        b = jnp.zeros((EMB_DIM,), dtype=jnp.float32)
        gamma = jnp.ones((EMB_DIM,), dtype=jnp.float32)
        beta = jnp.zeros((EMB_DIM,), dtype=jnp.float32)
        return {'x': x, 'src': src, 'dst': dst, 'W': W, 'b': b, 'gamma': gamma, 'beta': beta}
    _L0_gnn_all = _L0_gnn_setup()
    _L0_gnn_in = {k: v for k, v in _L0_gnn_all.items() if k in ('W', 'b', 'gamma', 'beta')}
    del _L0_gnn_all

    def _L1_gnn_setup():
        import jax, jax.numpy as jnp
        import numpy as np
        N_NODES = 6250
        N_EDGES = 100000
        D = 128
        T = 3
        NODE_IN = D + T * D
        key = jax.random.key(seed)
        ks = jax.random.split(key, 8)
        scale = 0.05
        return {'node_feature': jax.random.normal(ks[0], (N_NODES, D), jnp.float32), 'W_e': jax.random.normal(ks[1], (T, D, D), jnp.float32) * scale, 'b_e': jnp.zeros((T, D), jnp.float32), 'W_n': jax.random.normal(ks[2], (T, D, NODE_IN), jnp.float32) * scale, 'b_n': jnp.zeros((T, D), jnp.float32), 'edge_src': jax.random.randint(ks[3], (N_EDGES,), 0, N_NODES, jnp.int32), 'edge_dst': jax.random.randint(ks[4], (N_EDGES,), 0, N_NODES, jnp.int32), 'edge_type': jax.random.randint(ks[5], (N_EDGES,), 0, T, jnp.int32), 'node_type': jax.random.randint(ks[6], (N_NODES,), 0, T, jnp.int32)}
    _L1_gnn_all = _L1_gnn_setup()
    _L1_gnn_in = {k: v for k, v in _L1_gnn_all.items() if k in ('W_e', 'b_e', 'W_n', 'b_n')}
    del _L1_gnn_all

    def _L2_gnn_setup():
        import jax, jax.numpy as jnp
        import numpy as np
        N, E, D = (12500, 80000, 128)
        BN_EPS = 1e-05

        def _batchnorm(h, gamma, beta):
            mean = jnp.mean(h, axis=0)
            var = jnp.var(h, axis=0)
            return gamma * (h - mean) * jax.lax.rsqrt(var + BN_EPS) + beta
        key = jax.random.key(seed)
        ks = jax.random.split(key, 8)
        x = jax.random.normal(ks[0], (N, D), dtype=jnp.float32)
        edge_index = jax.random.randint(ks[1], (2, E), 0, N, dtype=jnp.int64)
        s = 1.0 / np.sqrt(D)
        W1 = jax.random.uniform(ks[2], (D, D), jnp.float32, -s, s)
        b1 = jax.random.uniform(ks[3], (D,), jnp.float32, -s, s)
        W2 = jax.random.uniform(ks[4], (D, D), jnp.float32, -s, s)
        b2 = jax.random.uniform(ks[5], (D,), jnp.float32, -s, s)
        return {'x': x, 'edge_index': edge_index, 'eps': jnp.array([0.1], dtype=jnp.float32), 'W1': W1, 'b1': b1, 'g1': jnp.ones((D,), jnp.float32), 'beta1': jnp.zeros((D,), jnp.float32), 'W2': W2, 'b2': b2, 'g2': jnp.ones((D,), jnp.float32), 'beta2': jnp.zeros((D,), jnp.float32)}
    _L2_gnn_all = _L2_gnn_setup()
    _L2_gnn_in = {k: v for k, v in _L2_gnn_all.items() if k in ('eps', 'W1', 'b1', 'g1', 'beta1', 'W2', 'b2', 'g2', 'beta2')}
    del _L2_gnn_all

    def _L3_gnn_setup():
        import jax, jax.numpy as jnp
        import numpy as np
        N_NODES = 1250
        N_EDGES = 80000
        DIM = 128

        def _sage_conv(h, src, dst, lw, lb, rw, n_nodes):
            msg = h[src]
            summed = jax.ops.segment_sum(msg, dst, num_segments=n_nodes)
            cnt = jax.ops.segment_sum(jnp.ones_like(dst, dtype=h.dtype), dst, num_segments=n_nodes)
            agg = summed / jnp.maximum(cnt, 1.0)[:, None]
            return agg @ lw.T + lb + h @ rw.T
        key = jax.random.key(seed)
        ks = jax.random.split(key, 10)
        s = 1.0 / np.sqrt(DIM)
        return {'x': jax.random.normal(ks[0], (N_NODES, DIM), dtype=jnp.float32), 'edge_index': jax.random.randint(ks[1], (2, N_EDGES), 0, N_NODES, dtype=jnp.int64), 'fc_w': jax.random.normal(ks[2], (DIM, DIM), dtype=jnp.float32) * s, 'fc_b': jax.random.normal(ks[3], (DIM,), dtype=jnp.float32) * s, 'f_lw': jax.random.normal(ks[4], (DIM, DIM), dtype=jnp.float32) * s, 'f_lb': jax.random.normal(ks[5], (DIM,), dtype=jnp.float32) * s, 'f_rw': jax.random.normal(ks[6], (DIM, DIM), dtype=jnp.float32) * s, 'n_lw': jax.random.normal(ks[7], (DIM, DIM), dtype=jnp.float32) * s, 'n_lb': jax.random.normal(ks[8], (DIM,), dtype=jnp.float32) * s, 'n_rw': jax.random.normal(ks[9], (DIM, DIM), dtype=jnp.float32) * s}
    _L3_gnn_all = _L3_gnn_setup()
    _L3_gnn_in = {k: v for k, v in _L3_gnn_all.items() if k in ('fc_w', 'fc_b', 'f_lw', 'f_lb', 'f_rw', 'n_lw', 'n_lb', 'n_rw')}
    del _L3_gnn_all
    return {'x': x, 'src': src, 'dst': dst, 'edge_type_3': edge_type_3, 'node_type_3': node_type_3, 'L0_gnn_W': _L0_gnn_in['W'], 'L0_gnn_b': _L0_gnn_in['b'], 'L0_gnn_gamma': _L0_gnn_in['gamma'], 'L0_gnn_beta': _L0_gnn_in['beta'], 'L1_gnn_W_e': _L1_gnn_in['W_e'], 'L1_gnn_b_e': _L1_gnn_in['b_e'], 'L1_gnn_W_n': _L1_gnn_in['W_n'], 'L1_gnn_b_n': _L1_gnn_in['b_n'], 'L2_gnn_eps': _L2_gnn_in['eps'], 'L2_gnn_W1': _L2_gnn_in['W1'], 'L2_gnn_b1': _L2_gnn_in['b1'], 'L2_gnn_g1': _L2_gnn_in['g1'], 'L2_gnn_beta1': _L2_gnn_in['beta1'], 'L2_gnn_W2': _L2_gnn_in['W2'], 'L2_gnn_b2': _L2_gnn_in['b2'], 'L2_gnn_g2': _L2_gnn_in['g2'], 'L2_gnn_beta2': _L2_gnn_in['beta2'], 'L3_gnn_fc_w': _L3_gnn_in['fc_w'], 'L3_gnn_fc_b': _L3_gnn_in['fc_b'], 'L3_gnn_f_lw': _L3_gnn_in['f_lw'], 'L3_gnn_f_lb': _L3_gnn_in['f_lb'], 'L3_gnn_f_rw': _L3_gnn_in['f_rw'], 'L3_gnn_n_lw': _L3_gnn_in['n_lw'], 'L3_gnn_n_lb': _L3_gnn_in['n_lb'], 'L3_gnn_n_rw': _L3_gnn_in['n_rw']}

def reference(x, src, dst, edge_type_3, node_type_3, L0_gnn_W, L0_gnn_b, L0_gnn_gamma, L0_gnn_beta, L1_gnn_W_e, L1_gnn_b_e, L1_gnn_W_n, L1_gnn_b_n, L2_gnn_eps, L2_gnn_W1, L2_gnn_b1, L2_gnn_g1, L2_gnn_beta1, L2_gnn_W2, L2_gnn_b2, L2_gnn_g2, L2_gnn_beta2, L3_gnn_fc_w, L3_gnn_fc_b, L3_gnn_f_lw, L3_gnn_f_lb, L3_gnn_f_rw, L3_gnn_n_lw, L3_gnn_n_lb, L3_gnn_n_rw):
    import jax
    import jax.numpy as jnp

    def _L0_gnn_ref(x, src, dst, W, b, gamma, beta):
        import jax, jax.numpy as jnp
        import numpy as np
        N_NODES = 12500
        N_EDGES = 200000
        EMB_DIM = 128
        BN_EPS = 1e-05
        n = x.shape[0]
        ones = jnp.ones(src.shape, dtype=x.dtype)
        deg_out = jnp.maximum(jax.ops.segment_sum(ones, src, num_segments=n), 1.0)
        deg_in = jnp.maximum(jax.ops.segment_sum(ones, dst, num_segments=n), 1.0)
        norm_src = jax.lax.rsqrt(deg_out)
        norm_dst = jax.lax.rsqrt(deg_in)
        h = x * norm_src[:, None] @ W
        agg = jax.ops.segment_sum(h[src], dst, num_segments=n)
        h = agg * norm_dst[:, None] + b
        mean = jnp.mean(h, axis=0)
        var = jnp.var(h, axis=0)
        h = (h - mean) * jax.lax.rsqrt(var + BN_EPS) * gamma + beta
        h = jax.nn.relu(h)
        return h + x

    def _L1_gnn_ref(node_feature, W_e, b_e, W_n, b_n, edge_src, edge_dst, edge_type, node_type):
        import jax, jax.numpy as jnp
        import numpy as np
        N_NODES = 6250
        N_EDGES = 100000
        D = 128
        T = 3
        NODE_IN = D + T * D
        N, Din = node_feature.shape
        n_types = W_e.shape[0]
        out_dim = W_e.shape[1]
        src = node_feature[edge_src]
        parts = [jax.nn.relu(node_feature)]
        for t in range(n_types):
            msg = jax.nn.relu(src @ W_e[t].T + b_e[t])
            msg = jnp.where((edge_type == t)[:, None], msg, jnp.zeros((), msg.dtype))
            parts.append(jax.ops.segment_sum(msg, edge_dst, num_segments=N))
        agg = jnp.concatenate(parts, axis=1)
        updated = jnp.zeros((N, out_dim), node_feature.dtype)
        for t in range(n_types):
            o = agg @ W_n[t].T + b_n[t]
            updated = jnp.where((node_type == t)[:, None], o, updated)
        return updated + node_feature

    def _L2_gnn_ref(x, edge_index, eps, W1, b1, g1, beta1, W2, b2, g2, beta2):
        import jax, jax.numpy as jnp
        import numpy as np
        N, E, D = (12500, 80000, 128)
        BN_EPS = 1e-05

        def _batchnorm(h, gamma, beta):
            mean = jnp.mean(h, axis=0)
            var = jnp.var(h, axis=0)
            return gamma * (h - mean) * jax.lax.rsqrt(var + BN_EPS) + beta
        src, dst = (edge_index[0], edge_index[1])
        aggr = jax.ops.segment_sum(x[src], dst, num_segments=x.shape[0])
        h = (1.0 + eps) * x + aggr
        h = jax.nn.relu(_batchnorm(h @ W1.T + b1, g1, beta1))
        h = jax.nn.relu(_batchnorm(h @ W2.T + b2, g2, beta2))
        return h

    def _L3_gnn_ref(x, edge_index, fc_w, fc_b, f_lw, f_lb, f_rw, n_lw, n_lb, n_rw):
        import jax, jax.numpy as jnp
        import numpy as np
        N_NODES = 1250
        N_EDGES = 80000
        DIM = 128

        def _sage_conv(h, src, dst, lw, lb, rw, n_nodes):
            msg = h[src]
            summed = jax.ops.segment_sum(msg, dst, num_segments=n_nodes)
            cnt = jax.ops.segment_sum(jnp.ones_like(dst, dtype=h.dtype), dst, num_segments=n_nodes)
            agg = summed / jnp.maximum(cnt, 1.0)[:, None]
            return agg @ lw.T + lb + h @ rw.T
        n_nodes = x.shape[0]
        src, dst = (edge_index[0], edge_index[1])
        inp = x @ fc_w.T + fc_b
        h = jax.nn.relu(_sage_conv(x, src, dst, f_lw, f_lb, f_rw, n_nodes))
        h = _sage_conv(h, src, dst, n_lw, n_lb, n_rw, n_nodes)
        return jax.nn.relu(h + inp)
    edge_index = jnp.stack([src, dst])
    x = _layernorm(x + _L0_gnn_ref(x, src, dst, L0_gnn_W, L0_gnn_b, L0_gnn_gamma, L0_gnn_beta), axis=-1)
    x = _layernorm(x + _L1_gnn_ref(x, L1_gnn_W_e, L1_gnn_b_e, L1_gnn_W_n, L1_gnn_b_n, src, dst, edge_type_3, node_type_3), axis=-1)
    x = _layernorm(x + _L2_gnn_ref(x, edge_index, L2_gnn_eps, L2_gnn_W1, L2_gnn_b1, L2_gnn_g1, L2_gnn_beta1, L2_gnn_W2, L2_gnn_b2, L2_gnn_g2, L2_gnn_beta2), axis=-1)
    x = _layernorm(x + _L3_gnn_ref(x, edge_index, L3_gnn_fc_w, L3_gnn_fc_b, L3_gnn_f_lw, L3_gnn_f_lb, L3_gnn_f_rw, L3_gnn_n_lw, L3_gnn_n_lb, L3_gnn_n_rw), axis=-1)
    return x

_drawn_inputs = setup_inputs


def setup_inputs(seed=0):
    import zlib

    import numpy as np

    out = dict(_drawn_inputs(seed))
    spreads = {'L0_gnn_b': (0.0, 0.1),
     'L0_gnn_gamma': (1.0, 0.2),
     'L0_gnn_beta': (0.0, 0.1),
     'L1_gnn_b_e': (0.0, 0.1),
     'L1_gnn_b_n': (0.0, 0.1),
     'L2_gnn_g1': (1.0, 0.2),
     'L2_gnn_beta1': (0.0, 0.1),
     'L2_gnn_g2': (1.0, 0.2),
     'L2_gnn_beta2': (0.0, 0.1)}
    factors = {}
    for name, (base, spread) in spreads.items():
        noise = np.random.default_rng([zlib.crc32(name.encode()), seed]).standard_normal(out[name].shape)
        drawn = base * np.exp(spread * noise) if base else spread * noise
        out[name] = jnp.asarray(drawn.astype(out[name].dtype))
    for name, factor in factors.items():
        out[name] = (out[name] * factor).astype(out[name].dtype)
    return out
```

```python
import concourse.bass as bass
from concourse import mybir
from contextlib import ExitStack


class Chain:

    def __init__(self, eng, sem):
        self.eng, self.sem, self.done, self.turn = eng, sem, 0, 0

    def link(self, ins):
        ins.then_inc(self.sem, 1)
        self.done += 1
        self.eng.wait_ge(self.sem, self.turn + self.done)

    def enter(self, i, per_turn):
        self.before, self.per, self.turn = self.done, per_turn, i * per_turn

    def leave(self, turns):
        assert self.done - self.before == self.per, (self.done - self.before, self.per)
        self.done, self.turn = self.before + turns * self.per, 0


def gnn_resnorm_kernel(nc, x, edges, dst, node_type, mats, cols, rows, eps2, out):
    fp32, bf16, fp16 = mybir.dt.float32, mybir.dt.bfloat16, mybir.dt.float16
    fp8, u8, i32 = mybir.dt.float8e4, mybir.dt.uint8, mybir.dt.int32
    ALU, ACT, AX = mybir.AluOpType, mybir.ActivationFunctionType, mybir.AxisListType

    N, D = x.shape
    E = edges.shape[0]
    T = 3
    P = 128
    NT = -(-N // P)
    NP = NT * P
    LASTN = N - (NT - 1) * P
    GT = 4
    NG = -(-NT // GT)
    WN = 2
    WE = 128
    SBW = P // WN
    NH = -(-NT // 2)
    HC = NT * WN
    KINDS = T + 1
    AC = KINDS * HC
    BW = 8
    NB = SBW // BW
    UNITS = ((0, 3), (3, 6), (6, 8))
    UPB = len(UNITS) * NB
    HEADS = 375
    HROW = E // HEADS
    assert HEADS * HROW == E and NT % 2 == 1 and len(UNITS) * NB % 2 == 0
    CI = 7
    NC = NT // CI
    PARTS = 3
    BN_EPS = LN_EPS = 1e-5
    MAXCOUNT = 16.0

    EARLY = ["W"] + [f"We{t}" for t in range(T)] + [f"Wn{k}{t}" for k in range(T + 1) for t in range(T)]
    LATE = ["W1", "W2", "fc", "f_lw", "f_rw", "n_lw", "n_rw"]
    MAT = {n: i for i, n in enumerate(EARLY)} | {n: i for i, n in enumerate(LATE)}
    COL = {n: i for i, n in enumerate(
        ["b", "gamma", "beta", "b1", "g1", "beta1", "b2", "g2", "beta2", "f_lb", "n_lb", "fc_b"])}
    ALL = T
    PASSES = [ALL, 0, 1, 2, ALL, ALL, ALL]
    NPASS = len(PASSES)

    adj = nc.dram_tensor("adjacency", (KINDS, NT, P, NT * P), u8, kind="Internal").ap()

    ctx = ExitStack()
    with ctx:
        def sb(name, shape, dt):
            return ctx.enter_context(nc.sbuf_tensor(name, shape, dt))

        def sem(name):
            return ctx.enter_context(nc.semaphore(name))

        x_nm = sb("x_nm", [P, NT, D], fp32)
        feat = sb("feat", [P, 2, NP], fp32)
        xT, hT = feat[:, 0, :], feat[:, 1, :]
        stage = [feat[:, s, :].bitcast(fp8).rearrange("p (k i d) -> p k i d", k=KINDS, d=P) for s in range(2)]
        deg_row = sb("deg_row", [P, NP], fp32)
        z = sb("z", [P, NT, D], fp32)
        z_row = z[:, :, :].rearrange("p i d -> p (i d)")
        work = sb("work", [P, PARTS * NT * D // 2], fp32)
        parts = work[:, :].bitcast(bf16).rearrange("p (s i d) -> p s i d", s=PARTS, d=D)
        ring = sb("ring", [P, NC, GT, CI * P], u8)
        wts = sb("wts", [P, len(EARLY), D], fp32)
        cvec = sb("cvec", [P, len(COL)], fp32)
        rvec = sb("rvec", [1, 2, T * D], fp32)
        eps_c = sb("eps_c", [P, 1], fp32)
        ident = sb("ident", [P, P], fp32)
        ones = sb("ones", [P, P], fp32)
        ones_b = sb("ones_b", [P, P], bf16)
        agg_s = sb("agg_s", [P, GT * P], fp32)
        tmp = sb("tmp", [P, 2, GT * P], fp32)
        res = sb("res", [P, GT * P], fp32)
        nt_i = sb("nt_i", [P, NT], i32)
        nt_m = sb("nt_m", [P, T, NT], fp32)
        deg_out = sb("deg_out", [P, NT], fp32)
        stats = sb("stats", [P, max(NG, GT), 6], fp32)
        mv = sb("mv", [P, NT, 2], fp32)
        bn_a = sb("bn_a", [P, 8], fp32)
        start_i = sb("start_i", [P, NH + 1], i32)
        next_i = sb("next_i", [P, 1], i32)

        at = [0]

        def scratch(words):
            at[0] += words
            assert at[0] <= work.shape[1]
            return work[:, at[0] - words:at[0]]
        onehot = scratch(BW * (AC + P)).bitcast(bf16).rearrange("p (s n) -> p s n", s=2)
        OH_T, OH_A, OH_L = T * HC * BW, AC * BW, (AC + P) * BW
        keysT = scratch(T * P // 2).bitcast(fp16).rearrange("p (a w) -> p a w", a=3)
        g3 = scratch(3 * WE).bitcast(i32)
        deg_acc, deg_max = scratch(HC), scratch(HC)
        bnd = scratch(NH)
        cnt, cnt2, row_f, nvalid = (scratch(NH) for _ in range(4))
        bnd_i, row_i = scratch(NH).bitcast(i32), scratch(NH).bitcast(i32)
        g3v = g3.rearrange("p (e a) -> p a e", a=3)
        lo_i, hi_i, dl, ge0, valid, key = (scratch(WE) for _ in range(6))
        kw = scratch(3 * WE).rearrange("p (a e) -> p a e", a=3)
        iota_r = scratch(AC * BW // 2).bitcast(fp16)
        f_flat = feat[:, :, :].rearrange("p a n -> p (a n)")
        iota_i = f_flat[:, 0:AC * BW].bitcast(i32)
        NR = 5
        o = AC * BW
        rowg = f_flat[:, o:o + NR * HROW].bitcast(i32).rearrange("p (s n) -> p s n", s=NR)
        o += NR * HROW
        junk = f_flat[:, o:o + HROW]
        o += HROW
        head_i = f_flat[0:1, o:o + HEADS].bitcast(i32)
        head_f = f_flat[0:1, o + HEADS:o + 2 * HEADS]

        ps = ctx.enter_context(nc.psum_tensor("ps", [P, 8, 512], fp32))
        A_BANK, DEG_BANK, MISC = (0, 3), 6, 7
        AGG, PROJ, SRC, TR = (0, 1), 2, (2, 3), (6, 7)

        made = {}

        def S(signal, phase=""):
            name = f"{signal}{phase}"
            if name not in made:
                made[name] = ctx.enter_context(nc.semaphore(name))
            return made[name]

        block = ctx.enter_context(nc.Block())

        def gw(g):
            return min(GT * P, NP - g * GT * P)

        def cols_of(g):
            return slice(g * GT * P, g * GT * P + gw(g))

        def tiles_of(g):
            return range(GT * g, min(GT * (g + 1), NT))

        def bank(i, w=512):
            return ps[:, i, 0:w]

        def nodes(buf, g):
            return buf[:, GT * g:min(GT * (g + 1), NT), :].rearrange("p i d -> p (i d)")

        def in_turns(eng, one):
            one(0, 0, GT * P)
            one(1, 1, GT * P)
            with eng.Fori(0, (NG - 3) // 2) as k:
                one(2 * k + 2, 0, GT * P)
                one(2 * k + 3, 1, GT * P)
            one(NG - 1, 0, gw(NG - 1))

        def hold(eng, signal, value):
            eng.wait_ge(signal, value)
            if not isinstance(value, int):
                eng.sem_inc(S("holds"), 1)

        def wait_sums(eng, p, g):
            eng.wait_ge(S("chunk_used"), NC * (NG * p + g + 1))

        @block.sync
        def _(sp):
            with nc.allow_non_contiguous_dma(reason="single integers"):
                sp.dma_start(head_i, dst.rearrange("(r c) -> c r", c=HROW)[0:1, :]).then_inc(S("heads_in"), 16)
            sp.dma_start(x_nm[:, 0:NT - 1, :], x[0:(NT - 1) * P, :].rearrange("(i p) d -> p i d", p=P)).then_inc(S("x_in"), 16)
            sp.wait_ge(S("consts"), 2)
            sp.dma_start(x_nm[0:LASTN, NT - 1, :], x[(NT - 1) * P:N, :]).then_inc(S("xtail_in"), 16)
            sp.dma_start(wts[:, :, :], mats[:, 0:len(EARLY) * D].rearrange("p (m d) -> p m d", d=D)).then_inc(S("mats_in"), 16)
            sp.dma_start(cvec[:, :], cols).then_inc(S("cols_in"), 16)
            sp.dma_start(rvec[:, :, :], rows.unsqueeze(0)).then_inc(S("rows_in"), 16)
            sp.dma_start(eps_c[:, :], eps2.unsqueeze(0).to_broadcast([P, 1])).then_inc(S("eps_in"), 16)
            with nc.allow_non_contiguous_dma(reason="single integers"):
                sp.dma_start(nt_i[:, 0:NT - 1], node_type[0:(NT - 1) * P].rearrange("(i p) -> p i", p=P)).then_inc(S("nt_in"), 16)
                sp.dma_start(nt_i[0:LASTN, NT - 1:NT], node_type[(NT - 1) * P:N].unsqueeze(1)).then_inc(S("nttail_in"), 16)

            def store(s, block_i):
                hold(sp, S("evacuated"), (block_i + 1) * UPB)
                sp.dma_start(adj[:, bass.ds(block_i, 1), :, :].rearrange("k o p n -> p (k o) n"),
                             stage[s].rearrange("p k i d -> p k (i d)").bitcast(u8)).then_inc(S("stored", s), 16)
            store(0, 0)
            with sp.Fori(0, NH - 1) as k:
                store(1, 2 * k + 1)
                store(0, 2 * k + 2)
            sp.wait_ge(S("stored", 0), 16 * NH)
            sp.wait_ge(S("stored", 1), 16 * NH)

            def load(p, g, width, first=False):
                for c in range(NC):
                    if not first:
                        hold(sp, S("chunk_used"), NC * (NG * p + g - 1) + c + 1)
                    sp.dma_start(ring[:, c, 0:width, :],
                                 adj[PASSES[p], bass.ds(GT * g, width), :, c * CI * P:(c + 1) * CI * P]
                                 .rearrange("b p n -> p b n")).then_inc(S("chunk_in", c), 16)
            for p in range(NPASS):
                load(p, 0, GT, first=(p == 0))
                if p == T + 1:
                    sp.wait_ge(S("proj_used", T), NG)
                    sp.dma_start(wts[:, 0:len(LATE), :], mats[:, len(EARLY) * D:].rearrange("p (m d) -> p m d", d=D)
                                 ).then_inc(S("late_mats_in"), 16)
                with sp.Fori(1, NG - 1) as g:
                    load(p, g, GT)
                load(p, NG - 1, NT - GT * (NG - 1))

            for g in range(NG):
                sp.wait_ge(S("x_ready", 3), g + 1)
                if g < NG - 1:
                    sp.dma_start(out[g * GT * P:(g + 1) * GT * P, :].rearrange("(i p) d -> p i d", p=P),
                                 x_nm[:, GT * g:GT * (g + 1), :]).then_inc(S("out_stored"), 16)
                else:
                    sp.dma_start(out[(NT - 1) * P:N, :], x_nm[0:LASTN, NT - 1, :]).then_inc(S("out_stored"), 16)
            sp.wait_ge(S("out_stored"), 16 * NG)

        @block.gpsimd
        def _(pool):
            consts = S("consts")
            pool.memset(x_nm[:, NT - 1, :], 0.0).then_inc(consts, 1)
            pool.memset(nt_i[:, NT - 1:NT], 0).then_inc(consts, 1)
            pool.iota(bnd_i[:, :], pattern=[[P * WN, NH]], base=0, channel_multiplier=WN).then_inc(consts, 1)
            pool.memset(ones[:, :], 1.0).then_inc(consts, 1)
            pool.iota(iota_i, pattern=[[1, AC], [0, BW]], base=1, channel_multiplier=0).then_inc(consts, 1)
            pool.memset(ones_b[:, :], 1.0).then_inc(consts, 1)
            pool.memset(ident[:, :], 0.0).then_inc(consts, 1)
            pool.wait_ge(consts, 7)
            pool.affine_select(out=ident[:, :], in_=ident[:, :], compare_op=ALU.not_equal, fill=1.0,
                               base=0, pattern=[[-1, P]], channel_multiplier=1).then_inc(consts, 1)
            pool.wait_ge(S("rows_found"), 1)
            for h in range(NH):
                if h >= NR:
                    pool.wait_ge(S("row_counted"), h - NR + 1)
                pool.indirect_dma_start(out=rowg[:, h % NR, :], out_offset=None,
                                        in_=dst.rearrange("(r c) -> r c", c=HROW),
                                        in_offset=bass.IndirectOffsetOnAxis(ap=row_i[:, h:h + 1], axis=0)
                                        ).then_inc(S("row_in", h % NR), 16)
            with pool.Fori(0, NH) as h:
                hold(pool, S("index_ready"), h + 1)
                pool.indirect_dma_start(out=g3, out_offset=None, in_=edges,
                                        in_offset=bass.IndirectOffsetOnAxis(ap=next_i[:, 0:1], axis=0)
                                        ).then_inc(S("edges_in"), 16)

        @block.scalar
        def _(act):
            act.sem_inc(S("stored", 1), 16)

            def evacuate(s, block_i, b, j):
                w0, w1 = UNITS[j]
                bk = A_BANK[(b * len(UNITS) + j) % 2]
                hold(act, S("counts_ready"), block_i * UPB + b * len(UNITS) + j + 1)
                d0 = (b * BW + w0) * WN
                act.activation(
                    stage[s][:, :, :, d0:d0 + (w1 - w0) * WN].rearrange("p k i (w d) -> p w (k i) d", d=WN),
                    ps[:, bk:bk + w1 - w0, 0:AC].rearrange("p w (t d) -> p w t d", d=WN),
                    ACT.Copy, saturate=False).then_inc(S("evacuated"), 1)

            def copy_degree(block_i):
                act.wait_ge(S("degree_ready"), block_i + 1)
                act.activation(deg_row[:, bass.ds(block_i * P, P)], bank(MISC)[:, 3 * P:4 * P],
                               ACT.Copy).then_inc(S("degree_copied"), 1)

            def block_of(s, block_i, stored_before):
                if stored_before is not None:
                    act.wait_ge(S("stored", s), stored_before)
                for b in range(NB):
                    for j in range(len(UNITS)):
                        evacuate(s, block_i, b, j)
                    if b == 2 and stored_before is not None:
                        copy_degree(block_i - 1)
            block_of(0, 0, None)
            with act.Fori(0, NH - 1) as k:
                block_of(1, 2 * k + 1, 16 * k + 16)
                block_of(0, 2 * k + 2, 16 * k + 16)
            copy_degree(NT - 1)

            act.wait_ge(S("degree_inverse"), 2)
            act.activation(deg_out[:, :], deg_out[:, :], ACT.Sqrt).then_inc(S("degree_norm"), 1)
            act.activation(z_row, deg_row[:, :], ACT.Sqrt).then_inc(S("degree_norm"), 1)

            def split(p, source):
                if p > 0:
                    wait_sums(act, p - 1, NG - 1)
                for j in range(NG):
                    src = source(j)
                    act.activation(nodes(parts[:, 0], j), src, ACT.Copy).then_inc(S("hi_ready", p), 1)
                    act.wait_ge(S("res_ready", p), j + 1)
                    act.activation(nodes(parts[:, 1], j), res[:, 0:gw(j)], ACT.Copy).then_inc(S("mid_ready", p), 1)

            def of_tmp(p):
                def source(j):
                    act.wait_ge(S("src_ready", p), j + 1)
                    return tmp[:, j % 2, 0:gw(j)]
                return source

            def of_x(layer):
                def source(j):
                    act.wait_ge(S("x_ready", layer), j + 1)
                    return nodes(x_nm, j)
                return source

            def of_psum(p, func):
                def source(j):
                    act.wait_ge(S("src_in_psum", p), j + 1)
                    if j >= 2:
                        act.wait_ge(S("parts_ready", p), j - 1)
                    act.activation(tmp[:, j % 2, 0:gw(j)], bank(SRC[j % 2], gw(j)), func).then_inc(S("src_ready", p), 1)
                    act.wait_ge(S("src_ready", p), j + 1)
                    return tmp[:, j % 2, 0:gw(j)]
                return source

            def copy_aggregates(p):
                def one(g, b, w):
                    wait_sums(act, p, g)
                    if not isinstance(g, int) or g > 0:
                        act.wait_ge(S("proj_done", p), g)
                    act.activation(agg_s[:, 0:w], bank(AGG[b], w), ACT.Copy).then_inc(S("agg_copied", p), 1)
                in_turns(act, one)

            def to_feat(p, to, func, bias):
                def one(g, b, w):
                    act.wait_ge(S("proj_done", p), g + 1)
                    act.activation(to[:, bass.ds(g * (GT * P), w)], bank(PROJ, w), func, bias=bias).then_inc(S("proj_used", p), 1)
                in_turns(act, one)

            def std(kind, n):
                v = bn_a[:, 1:2] if kind == "bn" else mv[:, :, 1]
                act.wait_ge(S(f"{kind}_var_ready", n), 1)
                act.activation(v, v, ACT.Sqrt).then_inc(S(f"{kind}_std_ready", n), 1)

            def bn_relu(n):
                std("bn", n)
                act.wait_ge(S("bn_ready", n), 1)
                for g in range(NG):
                    act.activation(hT[:, cols_of(g)], hT[:, cols_of(g)], ACT.Relu, bias=bn_a[:, 5:6],
                                   scale=bn_a[:, 4:5]).then_inc(S("relu_done", n), 1)

            def copy_xT(layer):
                std("ln", layer)
                for g in range(NG):
                    act.wait_ge(S("xT_in_psum", layer), g + 1)
                    act.activation(xT[:, cols_of(g)], bank(TR[g % 2], gw(g)), ACT.Copy).then_inc(S("xT_ready", layer), 1)

            act.wait_ge(S("cols_in"), 16)
            split(0, of_tmp(0))
            copy_aggregates(0)
            bn_relu(0)
            copy_xT(0)
            for g in range(NG):
                act.wait_ge(S("xT_ready", 0), g + 1)
                act.wait_ge(S("proj_done", 0), NG) if g == 0 else act.wait_ge(S("self_done"), g)
                act.activation(agg_s[:, 0:gw(g)], xT[:, cols_of(g)], ACT.Relu).then_inc(S("self_ready"), 1)
            for t in range(T):
                split(1 + t, of_psum(1 + t, ACT.Relu))
                copy_aggregates(1 + t)
            copy_xT(1)
            split(4, of_x(1))
            to_feat(4, hT, ACT.Identity, cvec[:, COL["b1"]:COL["b1"] + 1])
            bn_relu(1)
            for g in range(NG):
                act.wait_ge(S("lin2_done"), g + 1)
                act.activation(hT[:, cols_of(g)], bank(SRC[g % 2], gw(g)), ACT.Identity,
                               bias=cvec[:, COL["b2"]:COL["b2"] + 1]).then_inc(S("h2_ready"), 1)
            bn_relu(2)
            copy_xT(2)
            split(5, of_x(2))
            to_feat(5, hT, ACT.Relu, cvec[:, COL["f_lb"]:COL["f_lb"] + 1])
            split(6, of_psum(6, ACT.Copy))
            act.wait_ge(S("bias_ready"), 1)
            to_feat(6, z_row, ACT.Relu, bn_a[:, 6:7])
            std("ln", 3)

        @block.vector
        def _(dve):
            ch = Chain(dve, S("vector_steps"))
            link = ch.link

            dve.wait_ge(S("consts"), 8)
            dve.tensor_copy(iota_r, iota_i)
            link(dve.tensor_copy(bnd[:, :], bnd_i[:, :]))
            dve.wait_ge(S("heads_in"), 16)
            dve.tensor_copy(head_f, head_i).then_inc(S("heads_ready"), 1)
            dve.wait_ge(S("heads_spread"), 1)
            for h in range(NH):
                link(dve.tensor_scalar(junk[:, 0:HEADS], bank(MISC, HEADS), bnd[:, h:h + 1], 0.0,
                                       op0=ALU.is_lt, op1=ALU.add, accum_out=cnt[:, h:h + 1]))
            link(dve.tensor_scalar(row_f[:, :], cnt[:, :], -1.0, 0.0, op0=ALU.add, op1=ALU.max))
            dve.tensor_copy(row_i[:, :], row_f[:, :]).then_inc(S("rows_found"), 1)
            for h in range(NH):
                dve.wait_ge(S("row_in", h % NR), 16 * (h // NR + 1))
                dve.tensor_scalar(junk, rowg[:, h % NR, :], bnd[:, h:h + 1], 0.0, op0=ALU.is_lt, op1=ALU.add,
                                  accum_out=cnt2[:, h:h + 1]).then_inc(S("row_counted"), 1)
                dve.wait_ge(S("row_counted"), h + 1)
            link(dve.scalar_tensor_tensor(cnt[:, :], row_f[:, :], float(HROW), cnt2[:, :], op0=ALU.mult, op1=ALU.add))
            dve.memset(start_i[:, NH:NH + 1], 0)
            link(dve.tensor_scalar(start_i[:, 0:NH], cnt[:, :], float(E - WE), None, op0=ALU.min))
            link(dve.memset(deg_acc[:, :], 0.0))
            link(dve.memset(deg_max[:, :], 0.0))
            dve.tensor_copy(next_i[:, :], start_i[:, 0:1]).then_inc(S("index_ready"), 1)

            def window_keys(h, last=False):
                dve.wait_ge(S("edges_in"), 16 * h + 16)
                dve.tensor_scalar(lo_i.bitcast(i32), g3v[:, 0, :], P - 1, None, op0=ALU.bitwise_and)
                dve.tensor_scalar(hi_i.bitcast(i32), g3v[:, 0, :], 7, None, op0=ALU.logical_shift_right)
                link(dve.tensor_scalar(dl, g3v[:, 1, :], bnd[:, bass.ds(h, 1)], None, op0=ALU.subtract))
                dve.tensor_scalar(kw[:, 0, :], lo_i.bitcast(i32), 1.0, None, op0=ALU.add)
                dve.tensor_scalar(ge0, dl, 0.0, None, op0=ALU.is_ge)
                link(dve.scalar_tensor_tensor(key, hi_i.bitcast(i32), float(WN), dl, op0=ALU.mult, op1=ALU.add))
                link(dve.scalar_tensor_tensor(valid, dl, float(WN - 1), ge0, op0=ALU.is_le, op1=ALU.mult,
                                              accum_out=nvalid[:, bass.ds(h, 1)]))
                dve.scalar_tensor_tensor(kw[:, 2, :], key, 1.0, valid, op0=ALU.add, op1=ALU.mult)
                link(dve.scalar_tensor_tensor(dl, g3v[:, 2, :], float(HC), key, op0=ALU.mult, op1=ALU.add))
                dve.scalar_tensor_tensor(kw[:, 1, :], dl, 1.0, valid, op0=ALU.add, op1=ALU.mult).then_inc(S("keys_ready"), 1)

            def next_gather(h):
                dve.wait_ge(S("keys_ready"), h)
                dve.tensor_copy(next_i[:, :], start_i[:, bass.ds(h, 1)]).then_inc(S("index_ready"), 1)

            def take_keys(h):
                dve.wait_ge(S("keys_in_psum"), h + 1)
                dve.tensor_copy(keysT, bank(MISC, 3 * P).rearrange("p (a w) -> p a w", a=3)).then_inc(S("keys_taken"), 1)
                dve.wait_ge(S("keys_taken"), h + 1)

            def onehots(block_i, half, b):
                s = b % 2
                B = NB * block_i + b
                if not (isinstance(B, int) and B < 2):
                    dve.wait_ge(S("onehots_used"), B - 1)
                w = half * SBW + b * BW
                for a, c0, c1 in ((1, 0, OH_T), (2, OH_T, OH_A), (0, OH_A, OH_L)):
                    n = (c1 - c0) // BW
                    ins = dve.tensor_tensor(
                        onehot[:, s, c0:c1].rearrange("p (c w) -> p c w", w=BW),
                        iota_r[:, 0:c1 - c0].rearrange("p (c w) -> p c w", w=BW),
                        keysT[:, a, w:w + BW].unsqueeze(1).to_broadcast([P, n, BW]), ALU.is_equal)
                ins.then_inc(S("onehots_ready"), 1)

            def take_outdegrees(block_i):
                dve.wait_ge(S("onehots_used"), NB * (block_i + 1))
                dve.tensor_tensor(deg_acc[:, :], deg_acc[:, :], bank(DEG_BANK, HC), ALU.add)
                dve.tensor_tensor(deg_max[:, :], deg_max[:, :], bank(DEG_BANK, HC), ALU.max).then_inc(S("outdegrees_taken"), 1)
                dve.wait_ge(S("outdegrees_taken"), block_i + 1)

            window_keys(0)
            next_gather(1)
            take_keys(0)
            for b in range(NB):
                onehots(0, 0, b)
            with dve.Fori(0, NH - 1) as k:
                ch.enter(k, 4)
                for b in range(NB):
                    onehots(2 * k + 1, 1, b)
                    if b == 0:
                        take_outdegrees(2 * k)
                    if b == 2:
                        window_keys(k + 1)
                dve.wait_ge(S("onehots_ready"), NB * (2 * k + 2))
                take_keys(k + 1)
                for b in range(NB):
                    onehots(2 * k + 2, 0, b)
                    if b == 0:
                        take_outdegrees(2 * k + 1)
                    if b == 1:
                        next_gather(k + 2)
                ch.leave(NH - 1)
            take_outdegrees(NT - 1)

            dve.tensor_tensor(deg_out[:, :], deg_acc[:, 0:HC:2], deg_acc[:, 1:HC:2], ALU.add)
            dve.wait_ge(S("degree_copied"), NT)
            link(dve.tensor_scalar(deg_row[:, :], deg_row[:, :], 1.0, None, op0=ALU.max))
            link(dve.tensor_scalar(deg_out[:, :], deg_out[:, :], 1.0, None, op0=ALU.max))
            dve.reciprocal(deg_out[:, :], deg_out[:, :]).then_inc(S("degree_inverse"), 1)
            dve.reciprocal(deg_row[:, :], deg_row[:, :]).then_inc(S("degree_inverse"), 1)
            dve.wait_ge(S("nt_in"), 16)
            dve.wait_ge(S("nttail_in"), 16)
            for t in range(T):
                link(dve.tensor_scalar(nt_m[:, t, :], nt_i[:, :], float(t), None, op0=ALU.is_equal))

            def subtract(p, source):
                for j in range(NG):
                    src = source(j)
                    if j > 0:
                        dve.wait_ge(S("parts_ready", p), j)
                    dve.wait_ge(S("hi_ready", p), j + 1)
                    dve.tensor_tensor(res[:, 0:gw(j)], src, nodes(parts[:, 0], j), ALU.subtract).then_inc(S("res_ready", p), 1)
                    dve.wait_ge(S("res_ready", p), j + 1)
                    dve.wait_ge(S("mid_ready", p), j + 1)
                    dve.tensor_tensor(nodes(parts[:, 2], j), res[:, 0:gw(j)], nodes(parts[:, 1], j),
                                      ALU.subtract).then_inc(S("parts_ready", p), 1)

            def of_tmp(p):
                def source(j):
                    dve.wait_ge(S("src_ready", p), j + 1)
                    return tmp[:, j % 2, 0:gw(j)]
                return source

            def scaled(j):
                if j >= 2:
                    dve.wait_ge(S("parts_ready", 0), j - 1)
                for n, i in enumerate(tiles_of(j)):
                    ins = dve.tensor_scalar(tmp[:, j % 2, n * P:(n + 1) * P], x_nm[:, i, :], deg_out[:, i:i + 1], None, op0=ALU.mult)
                ins.then_inc(S("src_ready", 0), 1)
                dve.wait_ge(S("src_ready", 0), j + 1)
                return tmp[:, j % 2, 0:gw(j)]

            def stats_of(k, g, w):
                n = w if not isinstance(g, int) or g < NG - 1 else N - (NG - 1) * GT * P
                dve.bn_stats(stats[:, bass.ds(g, 1), :].rearrange("p o s -> p (o s)"),
                             hT[:, bass.ds(g * (GT * P), n)]).then_inc(S("stats_done", k), 1)

            def bn_scale(n, gamma, beta):
                dve.wait_ge(S("stats_done", n), NG)
                link(dve.bn_aggr(bn_a[:, 0:2], stats[:, 0:NG, :].rearrange("p g s -> p (g s)")))
                dve.tensor_scalar(bn_a[:, 1:2], bn_a[:, 1:2], BN_EPS, None, op0=ALU.add).then_inc(S("bn_var_ready", n), 1)
                dve.wait_ge(S("bn_std_ready", n), 1)
                link(dve.reciprocal(bn_a[:, 1:2], bn_a[:, 1:2]))
                link(dve.tensor_tensor(bn_a[:, 4:5], bn_a[:, 1:2], cvec[:, COL[gamma]:COL[gamma] + 1], ALU.mult))
                link(dve.tensor_tensor(bn_a[:, 3:4], bn_a[:, 0:1], bn_a[:, 4:5], ALU.mult))
                dve.tensor_tensor(bn_a[:, 5:6], cvec[:, COL[beta]:COL[beta] + 1], bn_a[:, 3:4], ALU.subtract).then_inc(S("bn_ready", n), 1)

            def layer_norm(layer, y):
                for g in range(NG):
                    y(g)
                    for n, i in enumerate(tiles_of(g)):
                        ins = dve.bn_stats(stats[:, n, :], x_nm[:, i, :])
                    link(ins)
                    for n, i in enumerate(tiles_of(g)):
                        ins = dve.bn_aggr(mv[:, i, :], stats[:, n, :])
                    link(ins)
                dve.tensor_scalar(mv[:, :, 1], mv[:, :, 1], LN_EPS, None, op0=ALU.add).then_inc(S("ln_var_ready", layer), 1)
                dve.wait_ge(S("ln_std_ready", layer), 1)
                link(dve.reciprocal(mv[:, :, 1], mv[:, :, 1]))
                for g in range(NG):
                    for i in tiles_of(g):
                        ins = dve.tensor_scalar(x_nm[:, i, :], x_nm[:, i, :], mv[:, i, 0:1], mv[:, i, 1:2],
                                                op0=ALU.subtract, op1=ALU.mult)
                    ins.then_inc(S("x_ready", layer), 1)
                dve.wait_ge(S("x_ready", layer), NG)

            def plus_transposed(layer, times):
                def y(g):
                    dve.wait_ge(S("h_in_psum", layer), g + 1)
                    dve.scalar_tensor_tensor(nodes(x_nm, g), nodes(x_nm, g), times, bank(TR[g % 2], gw(g)),
                                             op0=ALU.mult, op1=ALU.add).then_inc(S("h_taken", layer), 1)
                    dve.wait_ge(S("h_taken", layer), g + 1)
                return y

            dve.wait_ge(S("x_in"), 16)
            dve.wait_ge(S("xtail_in"), 16)
            dve.wait_ge(S("degree_norm"), 2)
            subtract(0, scaled)
            dve.wait_ge(S("cols_in"), 16)

            def layer0_h(g, b, w):
                dve.wait_ge(S("proj_done", 0), g + 1)
                c = bass.ds(g * (GT * P), w)
                dve.tensor_tensor(hT[:, c], bank(PROJ, w), z_row[:, c], ALU.mult).then_inc(S("proj_used", 0), 1)
                dve.wait_ge(S("proj_used", 0), g + 1)
                dve.tensor_scalar(hT[:, c], hT[:, c], cvec[:, 0:1], None, op0=ALU.add).then_inc(S("h_ready", 0), 1)
                dve.wait_ge(S("h_ready", 0), g + 1)
                stats_of(0, g, w)
            in_turns(dve, layer0_h)
            bn_scale(0, "gamma", "beta")
            layer_norm(0, plus_transposed(0, 2.0))

            def update(bank0, g, width, first, done):
                for t in range(T):
                    for n in range(width // P):
                        i = GT * g + n
                        zi = z[:, i, :] if isinstance(i, int) else z[:, bass.ds(i, 1), :].rearrange("p o d -> p (o d)")
                        m = nt_m[:, t, i:i + 1] if isinstance(i, int) else nt_m[:, t, bass.ds(i, 1)]
                        part = ps[:, bank0 + n, t * D:(t + 1) * D]
                        if first and t == 0:
                            ins = dve.tensor_scalar(zi, part, m, None, op0=ALU.mult)
                        else:
                            ins = dve.scalar_tensor_tensor(zi, part, m, zi, op0=ALU.mult, op1=ALU.add)
                    if t < T - 1:
                        link(ins)
                ins.then_inc(done, 1)

            for g in range(NG):
                dve.wait_ge(S("self_done"), g + 1)
                update(PROJ, g, gw(g), True, S("self_taken"))
            for t in range(T):
                subtract(1 + t, of_tmp(1 + t))

                def take(g, b, w):
                    dve.wait_ge(S("proj_done", 1 + t), g + 1)
                    update(PROJ, g, w, False, S("proj_used", 1 + t))
                take(0, 0, GT * P)
                take(1, 1, GT * P)
                with dve.Fori(0, (NG - 3) // 2) as k:
                    ch.enter(k, 2 * (T - 1))
                    take(2 * k + 2, 0, GT * P)
                    take(2 * k + 3, 1, GT * P)
                    ch.leave((NG - 3) // 2)
                take(NG - 1, 0, gw(NG - 1))
                dve.wait_ge(S("proj_used", 1 + t), NG)

            layer_norm(1, lambda g: link(dve.scalar_tensor_tensor(nodes(x_nm, g), nodes(x_nm, g), 2.0, nodes(z, g),
                                                                  op0=ALU.mult, op1=ALU.add)))

            def of_x(j):
                return nodes(x_nm, j)
            dve.wait_ge(S("eps_in"), 16)
            link(dve.tensor_scalar(bn_a[:, 7:8], eps_c[:, :], 1.0, None, op0=ALU.add))
            subtract(4, of_x)

            def plus_self(g, b, w):
                wait_sums(dve, 4, g)
                if not isinstance(g, int) or g > 0:
                    dve.wait_ge(S("proj_done", 4), g)
                dve.scalar_tensor_tensor(agg_s[:, 0:w], xT[:, bass.ds(g * (GT * P), w)], bn_a[:, 7:8], bank(AGG[b], w),
                                         op0=ALU.mult, op1=ALU.add).then_inc(S("agg_copied", 4), 1)

            def layer2(g, b, w):
                plus_self(g, b, w)
                if isinstance(g, int) and g == 0:
                    return
                dve.wait_ge(S("proj_used", 4), g)
                stats_of(1, g - 1, GT * P)
            dve.wait_ge(S("xT_ready", 1), NG)
            in_turns(dve, layer2)
            dve.wait_ge(S("proj_used", 4), NG)
            stats_of(1, NG - 1, gw(NG - 1))
            bn_scale(1, "g1", "beta1")
            for g in range(NG):
                dve.wait_ge(S("h2_ready"), g + 1)
                stats_of(2, g, gw(g))
            bn_scale(2, "g2", "beta2")
            layer_norm(2, plus_transposed(2, 1.0))

            dve.tensor_tensor(bn_a[:, 6:7], cvec[:, COL["n_lb"]:COL["n_lb"] + 1], cvec[:, COL["fc_b"]:COL["fc_b"] + 1], ALU.add).then_inc(S("bias_ready"), 1)
            for p in (5, 6):
                subtract(p, of_x if p == 5 else of_tmp(p))

                def mean(g, b, w):
                    wait_sums(dve, p, g)
                    if not isinstance(g, int) or g > 0:
                        dve.wait_ge(S("proj_done", p), g)
                    dve.tensor_tensor(agg_s[:, 0:w], bank(AGG[b], w), deg_row[:, bass.ds(g * (GT * P), w)],
                                      ALU.mult).then_inc(S("agg_copied", p), 1)
                in_turns(dve, mean)
            layer_norm(3, plus_transposed(3, 1.0))

        @block.tensor
        def _(pe):
            def mat(name):
                return wts[:, MAT[name], :]

            pe.wait_ge(S("consts"), 8)
            pe.wait_ge(S("heads_ready"), 1)
            pe.matmul(bank(MISC, HEADS), ones[0:1, :], head_f, start=True, stop=True).then_inc(S("heads_spread"), 1)

            def turn_keys(h):
                pe.wait_ge(S("keys_ready"), h + 1)
                for a in range(3):
                    ins = pe.transpose(bank(MISC)[:, a * P:(a + 1) * P], kw[:, a, :], ident[:, :])
                ins.then_inc(S("keys_in_psum"), 1)

            def count(block_i, b):
                s = b % 2
                pe.wait_ge(S("onehots_ready"), NB * block_i + b + 1)
                place = onehot[:, s, 0:OH_A].rearrange("p (c w) -> p c w", w=BW)
                source = onehot[:, s, OH_A:OH_L].rearrange("p (c w) -> p c w", w=BW)
                for j, (w0, w1) in enumerate(UNITS):
                    u = b * len(UNITS) + j
                    if not (isinstance(block_i, int) and u < 2):
                        pe.wait_ge(S("evacuated"), block_i * UPB + u - 1)
                    for w in range(w0, w1):
                        ins = pe.matmul(ps[:, A_BANK[u % 2] + w - w0, 0:AC], source[:, :, w], place[:, :, w], start=True, stop=True)
                    ins.then_inc(S("counts_ready"), 1)
                    if b == 0 and j == 0 and not isinstance(block_i, int):
                        pe.wait_ge(S("outdegrees_taken"), block_i)
                    for w in range(w0, w1):
                        last = pe.matmul(bank(DEG_BANK, HC), source[:, :, w], place[:, T * HC:, w],
                                         start=(b == 0 and w == 0), stop=(b == NB - 1 and w == BW - 1))
                last.then_inc(S("onehots_used"), 1)

            def indegree(s, block_i):
                hold(pe, S("evacuated"), (block_i + 1) * UPB)
                for i in range(NT):
                    ins = pe.matmul(bank(MISC)[:, 3 * P:4 * P], ones_b[:, :], stage[s][:, ALL, i, :], start=(i == 0), stop=(i == NT - 1))
                ins.then_inc(S("degree_ready"), 1)

            turn_keys(0)
            for b in range(NB):
                count(0, b)
            with pe.Fori(0, NH - 1) as k:
                for b in range(NB):
                    count(2 * k + 1, b)
                    if b == 1:
                        indegree(0, 2 * k)
                    if b == 4:
                        pe.wait_ge(S("degree_copied"), 2 * k + 1)
                        turn_keys(k + 1)
                for b in range(NB):
                    count(2 * k + 2, b)
                    if b == 1:
                        indegree(1, 2 * k + 1)
            pe.wait_ge(S("degree_copied"), NT - 1)
            indegree(0, NT - 1)

            def aggregate(p, g, b, w):
                gq = NG * p + g
                for c in range(NC):
                    hold(pe, S("chunk_in", c), 16 * gq + 16)
                    if isinstance(g, int) and g == 0:
                        pe.wait_ge(S("parts_ready", p), min(NG, (c * CI + CI - 1) // GT + 1))
                    for i in range(CI):
                        moving = ring[:, c, 0:w // P, i * P:(i + 1) * P].bitcast(fp8)
                        for s in range(PARTS):
                            t = c * CI + i
                            ins = pe.matmul(bank(AGG[b], w), parts[:, s, t, :], moving,
                                            start=(t == 0 and s == 0), stop=(t == NT - 1 and s == PARTS - 1))
                    ins.then_inc(S("chunk_used"), 1)

            def run_pass(p, project):
                def one(g, b, w):
                    aggregate(p, g, b, w)
                in_lag = GT * P
                aggregate(p, 0, 0, in_lag)
                aggregate(p, 1, 1, in_lag)
                lagged(p, 0, in_lag, project)
                with pe.Fori(0, (NG - 3) // 2) as k:
                    aggregate(p, 2 * k + 2, 0, in_lag)
                    lagged(p, 2 * k + 1, in_lag, project)
                    aggregate(p, 2 * k + 3, 1, in_lag)
                    lagged(p, 2 * k + 2, in_lag, project)
                aggregate(p, NG - 1, 0, gw(NG - 1))
                lagged(p, NG - 2, in_lag, project)
                lagged(p, NG - 1, gw(NG - 1), project)

            def lagged(p, g, w, project):
                pe.wait_ge(S("agg_copied", p), g + 1)
                if not isinstance(g, int) or g > 0:
                    pe.wait_ge(S("proj_used", p), g)
                project(g, w).then_inc(S("proj_done", p), 1)

            def transposes(buf, g, to):
                for n, i in enumerate(tiles_of(g)):
                    ins = pe.transpose(to[:, n * P:(n + 1) * P], buf(i), ident[:, :])
                return ins

            def to_nodes(layer, buf, before):
                for g in range(NG):
                    before(g)
                    if g >= 2:
                        pe.wait_ge(S("h_taken", layer), g - 1)
                    transposes(lambda i: buf[:, i * P:(i + 1) * P], g, bank(TR[g % 2])).then_inc(S("h_in_psum", layer), 1)

            def to_features(layer):
                for g in range(NG):
                    pe.wait_ge(S("x_ready", layer), g + 1)
                    if g >= 2:
                        pe.wait_ge(S("xT_ready", layer), g - 1)
                    transposes(lambda i: x_nm[:, i, :], g, bank(TR[g % 2])).then_inc(S("xT_in_psum", layer), 1)

            pe.wait_ge(S("mats_in"), 16)
            pe.wait_ge(S("rows_in"), 16)
            run_pass(0, lambda g, w: pe.matmul(bank(PROJ, w), mat("W"), agg_s[:, 0:w], start=True, stop=True))
            to_nodes(0, hT, lambda g: pe.wait_ge(S("relu_done", 0), g + 1))
            to_features(0)

            def node_update(block_k, w, bias=False):
                for n in range(w // P):
                    o = ps[:, PROJ + n, 0:T * D]
                    m = MAT[f"Wn{block_k}0"]
                    ins = pe.matmul(o, agg_s[:, n * P:(n + 1) * P], wts[:, m:m + T, :].rearrange("p m d -> p (m d)"),
                                    start=True, stop=not bias)
                    if bias:
                        ins = pe.matmul(o, ones[0:1, :], rvec[:, 1, :], start=False, stop=True)
                return ins
            for g in range(NG):
                pe.wait_ge(S("self_ready"), g + 1)
                if g > 0:
                    pe.wait_ge(S("self_taken"), g)
                node_update(0, gw(g), bias=True).then_inc(S("self_done"), 1)
            pe.wait_ge(S("self_taken"), NG)
            for t in range(T):
                if t > 0:
                    pe.wait_ge(S("proj_used", t), NG)
                for g in range(NG):
                    if g >= 2:
                        pe.wait_ge(S("src_ready", 1 + t), g - 1)
                    for n, i in enumerate(tiles_of(g)):
                        o = bank(SRC[g % 2])[:, n * P:(n + 1) * P]
                        pe.matmul(o, xT[:, i * P:(i + 1) * P], mat(f"We{t}"), start=True, stop=False)
                        ins = pe.matmul(o, ones[0:1, :], rvec[:, 0, t * D:(t + 1) * D], start=False, stop=True)
                    ins.then_inc(S("src_in_psum", 1 + t), 1)
                run_pass(1 + t, lambda g, w: node_update(1 + t, w))
            to_features(1)

            pe.wait_ge(S("late_mats_in"), 16)
            run_pass(4, lambda g, w: pe.matmul(bank(PROJ, w), mat("W1"), agg_s[:, 0:w], start=True, stop=True))
            for g in range(NG):
                pe.wait_ge(S("relu_done", 1), g + 1)
                if g >= 2:
                    pe.wait_ge(S("h2_ready"), g - 1)
                pe.matmul(bank(SRC[g % 2], gw(g)), mat("W2"), hT[:, cols_of(g)], start=True, stop=True).then_inc(S("lin2_done"), 1)
            to_nodes(2, hT, lambda g: pe.wait_ge(S("relu_done", 2), g + 1))
            to_features(2)

            def sage(p, terms):
                def project(g, w):
                    o = bank(PROJ, w)
                    c = bass.ds(g * (GT * P), w)
                    pe.matmul(o, mat(terms[0]), agg_s[:, 0:w], start=True, stop=False)
                    for n, (m, buf) in enumerate(terms[1:]):
                        ins = pe.matmul(o, mat(m), buf[:, c], start=False, stop=(n == len(terms) - 2))
                    return ins
                run_pass(p, project)
            pe.wait_ge(S("xT_ready", 2), NG)
            sage(5, ["f_lw", ("f_rw", xT)])
            pe.wait_ge(S("proj_used", 5), NG)
            for g in range(NG):
                if g >= 2:
                    pe.wait_ge(S("src_ready", 6), g - 1)
                transposes(lambda i: hT[:, i * P:(i + 1) * P], g, bank(SRC[g % 2])).then_inc(S("src_in_psum", 6), 1)
            sage(6, ["n_lw", ("n_rw", hT), ("fc", xT)])
            to_nodes(3, z_row, lambda g: pe.wait_ge(S("proj_used", 6), NG) if g == 0 else None)


def kernel(**inputs):
    import numpy as np
    import concourse.bacc as bacc
    from concourse.bass_utils import run_bass_kernel_spmd

    a = {k: np.asarray(v) for k, v in inputs.items()}
    t = lambda w: np.ascontiguousarray(w.T)
    we, wn = a["L1_gnn_W_e"], a["L1_gnn_W_n"]
    D = a["x"].shape[1]
    mats = [a["L0_gnn_W"]] + [we[i].T for i in range(3)]
    mats += [wn[i][:, k * D:(k + 1) * D].T for k in range(4) for i in range(3)]
    mats += [a[f"L2_gnn_{n}"].T for n in ("W1", "W2")]
    mats += [a[f"L3_gnn_{n}"].T for n in ("fc_w", "f_lw", "f_rw", "n_lw", "n_rw")]
    cols = [a[n] for n in ("L0_gnn_b", "L0_gnn_gamma", "L0_gnn_beta", "L2_gnn_b1", "L2_gnn_g1", "L2_gnn_beta1",
                           "L2_gnn_b2", "L2_gnn_g2", "L2_gnn_beta2", "L3_gnn_f_lb", "L3_gnn_n_lb", "L3_gnn_fc_b")]
    rows = [a["L1_gnn_b_e"].reshape(-1), a["L1_gnn_b_n"].reshape(-1)]
    arrays = {
        "x": a["x"],
        "edges": np.ascontiguousarray(np.stack([a["src"], a["dst"], a["edge_type_3"]], axis=1)),
        "dst": a["dst"],
        "node_type": a["node_type_3"],
        "mats": np.ascontiguousarray(np.concatenate(mats, axis=1)),
        "cols": np.ascontiguousarray(np.stack(cols, axis=1)),
        "rows": np.ascontiguousarray(np.stack(rows, axis=0)),
        "eps2": a["L2_gnn_eps"],
    }
    nc = bacc.Bacc("TRN2", target_bir_lowering=False, num_devices=1)
    args = [nc.dram_tensor(n, v.shape, mybir.dt.from_np(v.dtype), kind="ExternalInput").ap() for n, v in arrays.items()]
    out = nc.dram_tensor("out", a["x"].shape, mybir.dt.float32, kind="ExternalOutput").ap()
    gnn_resnorm_kernel(nc, *args, out)
    r = run_bass_kernel_spmd(nc, [arrays], core_ids=[0])
    return r.results[0]["out"]
```

```python
import concourse.bass as bass
from concourse import mybir
from contextlib import ExitStack


class Chain:

    def __init__(self, eng, sem):
        self.eng, self.sem, self.done, self.turn = eng, sem, 0, 0

    def link(self, ins):
        ins.then_inc(self.sem, 1)
        self.done += 1
        self.eng.wait_ge(self.sem, self.turn + self.done)

    def enter(self, i, per_turn):
        self.before, self.per, self.turn = self.done, per_turn, i * per_turn

    def leave(self, turns):
        assert self.done - self.before == self.per, (self.done - self.before, self.per)
        self.done, self.turn = self.before + turns * self.per, 0


def gnn_resnorm_kernel(nc, x, edges, dst, node_type, mats, cols, rows, eps2, out):
    fp32, bf16, fp16 = mybir.dt.float32, mybir.dt.bfloat16, mybir.dt.float16
    fp8, u8, i16, i32 = mybir.dt.float8e4, mybir.dt.uint8, mybir.dt.int16, mybir.dt.int32
    ALU, ACT, AX = mybir.AluOpType, mybir.ActivationFunctionType, mybir.AxisListType

    N, D = x.shape
    E = edges.shape[0]
    T = 3
    P = 128
    NT = -(-N // P)
    NP = NT * P
    LASTN = N - (NT - 1) * P
    GT = 4
    NG = -(-NT // GT)
    WN = 2
    WE = 128
    SBW = P // WN
    NH = -(-NT // 2)
    KINDS = T + 1
    AC = KINDS * NT
    BW = 16
    NB = SBW // BW
    UW = 4
    UPB = SBW // UW
    FIELD = 256.0
    BYTE = 2.0 ** -9
    HEADS = 375
    HROW = E // HEADS
    assert HEADS * HROW == E and NT % 2 == 1
    CI = 7
    NC = NT // CI
    PARTS = 2
    BN_EPS = LN_EPS = 1e-5
    XMAX = 11.5
    X_SCALE = 2.0 ** 11
    MAXCOUNT = 16.0

    EARLY = ["W"] + [f"We{t}" for t in range(T)] + [f"Wn{k}{t}" for k in range(T + 1) for t in range(T)]
    LATE = ["W1", "W2", "fc", "f_lw", "f_rw", "n_lw", "n_rw"]
    MAT = {n: i for i, n in enumerate(EARLY)} | {n: i for i, n in enumerate(LATE)}
    COL = {n: i for i, n in enumerate(
        ["b", "gamma", "beta", "b1", "g1", "beta1", "b2", "g2", "beta2", "f_lb", "n_lb", "fc_b"])}
    ALL = T
    PASSES = [ALL, 0, 1, 2, ALL, ALL, ALL]
    NPASS = len(PASSES)

    CH = 125
    NCH = E // CH
    assert NCH * CH == E
    table = nc.dram_tensor("table", (NP, PARTS, D), fp16, kind="Internal").ap()
    sums = nc.dram_tensor("sums", (NP, D), fp32, kind="Internal").ap()
    adj = nc.dram_tensor("adjacency", (KINDS, NT, P, NT * P), u8, kind="Internal").ap()

    ctx = ExitStack()
    with ctx:
        def sb(name, shape, dt):
            return ctx.enter_context(nc.sbuf_tensor(name, shape, dt))

        def sem(name):
            return ctx.enter_context(nc.semaphore(name))

        x_nm = sb("x_nm", [P, NT, D], fp32)
        feat = sb("feat", [P, 2, NP], fp32)
        xT, hT = feat[:, 0, :], feat[:, 1, :]
        stage = [feat[:, s, :].bitcast(fp8).rearrange("p (k i d) -> p k i d", k=KINDS, d=P) for s in range(2)]
        deg_row = sb("deg_row", [P, NP], fp32)
        z = sb("z", [P, NT, D], fp32)
        z_row = z[:, :, :].rearrange("p i d -> p (i d)")
        work = sb("work", [P, 10000], fp32)
        parts = work[:, 0:PARTS * NT * D // 2].bitcast(fp16).rearrange("p (s i d) -> p s i d", s=PARTS, d=D)
        scale = sb("scale", [P, T + 2, 2], fp32)
        bound = sb("bound", [P, 8], fp32)
        ring = sb("ring", [P, NC, GT, CI * P], u8)
        wts = sb("wts", [P, len(EARLY), D], fp32)
        cvec = sb("cvec", [P, len(COL)], fp32)
        rvec = sb("rvec", [1, 2, T * D], fp32)
        eps_c = sb("eps_c", [P, 1], fp32)
        ident = sb("ident", [P, P], fp32)
        ones = sb("ones", [P, P], fp32)
        ones_h = sb("ones_h", [P, P], fp16)
        probe = sb("probe", [P, int(MAXCOUNT)], u8)
        probe_i = sb("probe_i", [P, 1, int(MAXCOUNT)], i32)
        probe_f = sb("probe_f", [P, int(MAXCOUNT)], fp32)
        agg_s = sb("agg_s", [P, GT * P], fp32)
        square_l = agg_s[:, 0:2 * D + 1]
        tmp = sb("tmp", [P, 2, GT * P], fp32)
        nt_i = sb("nt_i", [P, NT], i32)
        nt_m = sb("nt_m", [P, T, NT], fp32)
        deg_out = sb("deg_out", [P, NT], fp32)
        stats = sb("stats", [P, max(NG, GT), 6], fp32)
        mv = sb("mv", [P, NT, 2], fp32)
        mv_g = sb("mv_g", [P, GT, 2], fp32)
        bn_a = sb("bn_a", [P, 8], fp32)
        start_i = sb("start_i", [P, NH + 1], i32)
        next_i = sb("next_i", [P, 1], i32)

        flag = sb("flag", [1, 1], i32)
        ring_f = ring[:, :, :, :].rearrange("p c b n -> p (c b n)").bitcast(fp32)
        o = [0]

        def of_ring(words):
            o[0] += words
            assert o[0] <= ring_f.shape[1]
            return ring_f[:, o[0] - words:o[0]]
        c_edges = of_ring(3)[0:CH].bitcast(i32)
        c_rows = of_ring(PARTS * D // 2)[0:CH].bitcast(fp16)
        c_old, c_new = of_ring(D)[0:CH], of_ring(D)[0:CH]
        c_diag = of_ring(P)[0:CH, 0:CH]
        c_same = of_ring(P)[0:CH, 0:CH]
        c_sel = of_ring(P)[0:CH].bitcast(fp16)[:, 0:CH]
        c_tri = of_ring(P)[0:CH, 0:CH]
        c_idx = of_ring(1)[0:CH].bitcast(i32)
        c_dst, c_typ, c_dup, c_idf = (of_ring(1)[0:CH] for _ in range(4))
        zeros = of_ring(GT * P)
        sums_n = of_ring(GT * P).rearrange("p (i d) -> p i d", d=D)

        at = [0]

        def scratch(words):
            at[0] += words
            assert at[0] <= work.shape[1]
            return work[:, at[0] - words:at[0]]
        onehot = scratch(BW * (AC + P)).bitcast(fp16).rearrange("p (s n) -> p s n", s=2)
        OH_T, OH_A, OH_L = T * NT * BW, AC * BW, (AC + P) * BW
        keysT = scratch(4 * P // 2).bitcast(fp16).rearrange("p (a w) -> p a w", a=4)
        key_d = scratch(P)
        g3 = scratch(3 * WE).bitcast(i32)
        deg_acc, deg_max, deg_hi, deg_b = (scratch(NT) for _ in range(4))
        deg_i = scratch(NT).bitcast(i32)
        bnd = scratch(NH)
        cnt, cnt2, row_f = (scratch(NH) for _ in range(3))
        bnd_i, row_i = scratch(NH).bitcast(i32), scratch(NH).bitcast(i32)
        g3v = g3.rearrange("p (e a) -> p a e", a=3)
        lo_i, hi_i, dl, ge0, valid, key = (scratch(WE) for _ in range(6))
        kw = scratch(3 * WE).rearrange("p (a e) -> p a e", a=3)
        iota_r = scratch(AC * BW // 2).bitcast(fp16)
        bias_b = work[:, PARTS * NT * D // 2:PARTS * NT * D // 2 + 2 * T * D].rearrange("p (a d) -> p a d", a=2)
        f_flat = feat[:, :, :].rearrange("p a n -> p (a n)")
        iota_i = f_flat[:, 0:AC * BW].bitcast(i32)
        NR = 5
        o = AC * BW
        rowg = f_flat[:, o:o + NR * HROW].bitcast(i32).rearrange("p (s n) -> p s n", s=NR)
        o += NR * HROW
        junk = f_flat[:, o:o + HROW]
        o += HROW
        square = f_flat[:, o:o + T * D]
        o += T * D
        head_i = f_flat[0:1, o:o + HEADS].bitcast(i32)
        head_f = f_flat[0:1, o + HEADS:o + 2 * HEADS]

        ps = ctx.enter_context(nc.psum_tensor("ps", [P, 8, 512], fp32))
        A_BANK, DEG_BANK, MISC = (0, 2, 4), 6, 7
        AGG, PROJ, SRC, TR = (0, 1), 2, (2, 3), (6, 7)

        made = {}

        def S(signal, phase=""):
            name = f"{signal}{phase}"
            if name not in made:
                made[name] = ctx.enter_context(nc.semaphore(name))
            return made[name]

        block = ctx.enter_context(nc.Block())

        def gw(g):
            return min(GT * P, NP - g * GT * P)

        def cols_of(g):
            return slice(g * GT * P, g * GT * P + gw(g))

        def tiles_of(g):
            return range(GT * g, min(GT * (g + 1), NT))

        def banks_of(u):
            return A_BANK[u % 3 if u < UPB - 1 else 1]

        def bank(i, w=512):
            return ps[:, i, 0:w]

        def nodes(buf, g):
            return buf[:, GT * g:min(GT * (g + 1), NT), :].rearrange("p i d -> p (i d)")

        def in_turns(eng, one):
            one(0, 0, GT * P)
            one(1, 1, GT * P)
            with eng.Fori(0, (NG - 3) // 2) as k:
                one(2 * k + 2, 0, GT * P)
                one(2 * k + 3, 1, GT * P)
            one(NG - 1, 0, gw(NG - 1))

        def hold(eng, signal, value):
            eng.wait_ge(signal, value)
            if not isinstance(value, int):
                eng.sem_inc(S("holds"), 1)

        def scale_of(p):
            k = {0: 0, 1: 1, 2: 2, 3: 3, 6: T + 1}.get(p)
            return (X_SCALE, 1.0 / (X_SCALE * BYTE)) if k is None else (scale[:, k, 0:1], scale[:, k, 1:2])

        def table_init(sp, n, ready, count):
            sp.wait_ge(ready, count)
            sp.wait_ge(S("zeros_ready"), 1)
            for k in range(PARTS):
                sp.dma_start(table[:, k, :].rearrange("(i p) d -> p i d", p=P), parts[:, k]).then_inc(S("init_done"), 16)
            for g in range(NG):
                sp.dma_start(sums[g * GT * P:g * GT * P + gw(g), :].rearrange("(i p) d -> p i d", p=P),
                             zeros[:, 0:gw(g)].rearrange("p (i d) -> p i d", d=D)).then_inc(S("init_done"), 16)
            sp.wait_ge(S("init_done"), 16 * (PARTS + NG) * (n + 1))

        def any_edges_sync(sp, n):
            sp.dma_start(c_edges, edges[0:CH, :]).then_inc(S("chunk_edges_in", n // 2), 16)
            with sp.Fori(1, NCH) as i:
                hold(sp, S("sums_put", n // 2), 16 * i + 16 * (n % 2 * NCH))
                sp.dma_start(c_edges, edges[bass.ds(i * CH, CH), :]).then_inc(S("chunk_edges_in", n // 2), 16)
            sp.wait_ge(S("sums_put", n // 2), 16 * (n % 2 + 1) * NCH)

        def any_edges_pool(pool, n, src, dst_col):
            with pool.Fori(0, NCH) as i:
                hold(pool, S("chunk_edges_in", n // 2), 16 * i + 16 * (n % 2 * NCH + 1))
                pool.indirect_dma_start(out=c_rows, out_offset=None, in_=table.rearrange("n s d -> n (s d)"),
                                        in_offset=bass.IndirectOffsetOnAxis(ap=c_edges[:, src:src + 1], axis=0)
                                        ).then_inc(S("chunk_rows_in", n // 2), 16)
                pool.indirect_dma_start(out=c_old, out_offset=None, in_=sums,
                                        in_offset=bass.IndirectOffsetOnAxis(ap=c_edges[:, dst_col:dst_col + 1], axis=0)
                                        ).then_inc(S("chunk_old_in", n // 2), 16)
                hold(pool, S("chunk_new"), i + (n * NCH + 1))
                pool.indirect_dma_start(out=sums, out_offset=bass.IndirectOffsetOnAxis(ap=c_idx[:, 0:1], axis=0),
                                        in_=c_new, in_offset=None, bounds_check=NP - 1, oob_is_err=False
                                        ).then_inc(S("sums_put", n // 2), 16)

        def any_edges_vector(dve, ch, n, kind, dst_col):
            with dve.Fori(0, NCH) as i:
                ch.enter(i, 7)
                dve.wait_ge(S("chunk_edges_in", n // 2), 16 * i + 16 * (n % 2 * NCH + 1))
                ch.link(dve.tensor_copy(c_dst, c_edges[:, dst_col:dst_col + 1]))
                dve.tensor_scalar(c_diag, ident[0:CH, 0:CH], c_dst, None, op0=ALU.mult).then_inc(S("chunk_diag"), 1)
                if kind == ALL:
                    ch.link(dve.memset(c_typ, BYTE))
                else:
                    ch.link(dve.tensor_scalar(c_typ, c_edges[:, 2:3], float(kind), BYTE, op0=ALU.is_equal, op1=ALU.mult))
                dve.wait_ge(S("chunk_spread"), i + (n * NCH + 1))
                ch.link(dve.tensor_scalar(c_same, bank(PROJ, CH)[0:CH], c_dst, None, op0=ALU.is_equal))
                dve.tensor_scalar(c_sel, c_same, c_typ, None, op0=ALU.mult).then_inc(S("chunk_sel"), 1)
                ch.link(dve.tensor_tensor(c_diag, c_same, c_tri, ALU.mult))
                ch.link(dve.tensor_reduce(c_dup, c_diag, axis=AX.X, op=ALU.add))
                ch.link(dve.scalar_tensor_tensor(c_idf, c_dup, float(NP), c_dst, op0=ALU.mult, op1=ALU.add))
                dve.tensor_copy(c_idx, c_idf)
                dve.wait_ge(S("chunk_old_in", n // 2), 16 * i + 16 * (n % 2 * NCH + 1))
                dve.wait_ge(S("chunk_sum"), i + (n * NCH + 1))
                ch.link(dve.tensor_tensor(c_new, c_old, bank(PROJ + 1)[0:CH, 0:D], ALU.add))
                dve.tensor_tensor(c_new, c_new, bank(PROJ + 1)[0:CH, D:2 * D], ALU.add).then_inc(S("chunk_new"), 1)
                dve.wait_ge(S("chunk_new"), i + (n * NCH + 1))
                ch.leave(NCH)

        def any_edges_tensor(pe, n):
            with pe.Fori(0, NCH) as i:
                pe.wait_ge(S("chunk_diag"), i + (n * NCH + 1))
                pe.matmul(bank(PROJ, CH)[0:CH], ones[0:CH, 0:CH], c_diag, start=True, stop=True).then_inc(S("chunk_spread"), 1)
                pe.wait_ge(S("chunk_sel"), i + (n * NCH + 1))
                pe.wait_ge(S("chunk_rows_in", n // 2), 16 * i + 16 * (n % 2 * NCH + 1))
                pe.matmul(bank(PROJ + 1)[0:CH, 0:PARTS * D], c_sel, c_rows, start=True, stop=True).then_inc(S("chunk_sum"), 1)

        def read_flag(eng):
            eng.wait_ge(S("flag_ready"), 1)
            return eng.value_load(flag[0:1, 0:1], min_val=0, max_val=1)

        def wait_sums(eng, p, g):
            eng.wait_ge(S("chunk_used"), NC * (NG * p + g + 1))

        @block.sync
        def _(sp):
            with nc.allow_non_contiguous_dma(reason="single integers"):
                sp.dma_start(head_i, dst.rearrange("(r c) -> c r", c=HROW)[0:1, :]).then_inc(S("heads_in"), 16)
            sp.dma_start(x_nm[:, 0:NT - 1, :], x[0:(NT - 1) * P, :].rearrange("(i p) d -> p i d", p=P)).then_inc(S("x_in"), 16)
            sp.wait_ge(S("consts"), 2)
            sp.dma_start(x_nm[0:LASTN, NT - 1, :], x[(NT - 1) * P:N, :]).then_inc(S("xtail_in"), 16)
            sp.dma_start(wts[:, :, :], mats[:, 0:len(EARLY) * D].rearrange("p (m d) -> p m d", d=D)).then_inc(S("mats_in"), 16)
            sp.dma_start(cvec[:, :], cols).then_inc(S("cols_in"), 16)
            sp.dma_start(rvec[:, :, :], rows.unsqueeze(0)).then_inc(S("rows_in"), 16)
            sp.dma_start(eps_c[:, :], eps2.unsqueeze(0).to_broadcast([P, 1])).then_inc(S("eps_in"), 16)
            with nc.allow_non_contiguous_dma(reason="single integers"):
                sp.dma_start(nt_i[:, 0:NT - 1], node_type[0:(NT - 1) * P].rearrange("(i p) -> p i", p=P)).then_inc(S("nt_in"), 16)
                sp.dma_start(nt_i[0:LASTN, NT - 1:NT], node_type[(NT - 1) * P:N].unsqueeze(1)).then_inc(S("nttail_in"), 16)

            def store(s, block_i):
                hold(sp, S("evacuated"), (block_i + 1) * UPB)
                sp.dma_start(adj[:, bass.ds(block_i, 1), :, :].rearrange("k o p n -> p (k o) n"),
                             stage[s].rearrange("p k i d -> p k (i d)").bitcast(u8)).then_inc(S("stored", s), 16)
            store(0, 0)
            with sp.Fori(0, NH - 1) as k:
                store(1, 2 * k + 1)
                store(0, 2 * k + 2)
            sp.wait_ge(S("stored", 0), 16 * NH)
            sp.wait_ge(S("stored", 1), 16 * NH)

            any_edges = read_flag(sp)
            with sp.If(any_edges > 0):
                table_init(sp, 0, S("ones_ready"), 1)
                any_edges_sync(sp, 0)
                for g in range(NG):
                    if g > 0:
                        sp.wait_ge(S("any_degree_taken"), g)
                    sp.dma_start(sums_n[:, 0:gw(g) // P, :], sums[g * GT * P:g * GT * P + gw(g), :]
                                 .rearrange("(i p) d -> p i d", p=P)).then_inc(S("any_degree_in"), 16)
                sp.wait_ge(S("any_degree_taken"), NG)
                table_init(sp, 1, S("ones_ready"), 1)
                any_edges_sync(sp, 1)
                with nc.allow_non_contiguous_dma(reason="one number per node"):
                    sp.dma_start(deg_out[:, :], sums[:, 0:1].rearrange("(i p) d -> p (i d)", p=P)).then_inc(S("any_outdegree_in"), 16)
                sp.wait_ge(S("any_outdegree_in"), 16)
            sp.nop()

            def load_sums(p, g, width, first):
                if not first:
                    hold(sp, S("chunk_used"), NC * (NG * p + g))
                sp.dma_start(sums_n[:, 0:width, :], sums[bass.ds(g * (GT * P), width * P), :]
                             .rearrange("(i p) d -> p i d", p=P)).then_inc(S("sums_in"), 16)

            def load(p, g, width, first=False):
                if isinstance(g, int) and g == 0:
                    with sp.If(any_edges > 0):
                        table_init(sp, 2 + p, S("parts_ready"), NG * (p + 1))
                        any_edges_sync(sp, 2 + p)
                    sp.nop()
                with sp.If(any_edges > 0):
                    load_sums(p, g, width, first)
                with sp.Else():
                    load_chunks(p, g, width, first)
                sp.nop()

            def load_chunks(p, g, width, first):
                for c in range(NC):
                    if not first:
                        hold(sp, S("chunk_used"), NC * (NG * p + g - 1) + c + 1)
                    sp.dma_start(ring[:, c, 0:width, :],
                                 adj[PASSES[p], bass.ds(GT * g, width), :, c * CI * P:(c + 1) * CI * P]
                                 .rearrange("b p n -> p b n")).then_inc(S("chunk_in", c), 16)
            for p in range(NPASS):
                if p == T + 1:
                    sp.wait_ge(S("proj_used"), NG * (T + 1))
                    sp.dma_start(wts[:, 0:len(LATE), :], mats[:, len(EARLY) * D:].rearrange("p (m d) -> p m d", d=D)
                                 ).then_inc(S("late_mats_in"), 16)
                load(p, 0, GT, first=(p == 0))
                with sp.Fori(1, NG - 1) as g:
                    load(p, g, GT)
                load(p, NG - 1, NT - GT * (NG - 1))

            for g in range(NG):
                sp.wait_ge(S("x_ready", 3), g + 1)
                if g < NG - 1:
                    sp.dma_start(out[g * GT * P:(g + 1) * GT * P, :].rearrange("(i p) d -> p i d", p=P),
                                 x_nm[:, GT * g:GT * (g + 1), :]).then_inc(S("out_stored"), 16)
                else:
                    sp.dma_start(out[(NT - 1) * P:N, :], x_nm[0:LASTN, NT - 1, :]).then_inc(S("out_stored"), 16)
            sp.wait_ge(S("out_stored"), 16 * NG)

        @block.gpsimd
        def _(pool):
            consts = S("consts")
            pool.memset(x_nm[:, NT - 1, :], 0.0).then_inc(consts, 1)
            pool.memset(nt_i[:, NT - 1:NT], 0).then_inc(consts, 1)
            pool.iota(bnd_i[:, :], pattern=[[P * WN, NH]], base=0, channel_multiplier=WN).then_inc(consts, 1)
            pool.memset(ones[:, :], 1.0).then_inc(consts, 1)
            pool.iota(iota_i, pattern=[[1, AC], [0, BW]], base=1, channel_multiplier=0).then_inc(consts, 1)
            pool.iota(probe_i[:, 0, :], pattern=[[1, int(MAXCOUNT)]], base=1, channel_multiplier=0).then_inc(consts, 1)
            pool.memset(ones_h[:, :], 1.0).then_inc(consts, 1)
            pool.memset(ident[:, :], 0.0).then_inc(consts, 1)
            pool.wait_ge(consts, 8)
            pool.affine_select(out=ident[:, :], in_=ident[:, :], compare_op=ALU.not_equal, fill=1.0,
                               base=0, pattern=[[-1, P]], channel_multiplier=1).then_inc(consts, 1)
            pool.wait_ge(S("rows_found"), 1)
            for h in range(NH):
                if h >= NR:
                    pool.wait_ge(S("row_counted"), h - NR + 1)
                pool.indirect_dma_start(out=rowg[:, h % NR, :], out_offset=None,
                                        in_=dst.rearrange("(r c) -> r c", c=HROW),
                                        in_offset=bass.IndirectOffsetOnAxis(ap=row_i[:, h:h + 1], axis=0)
                                        ).then_inc(S("row_in", h % NR), 16)
            with pool.Fori(0, NH) as h:
                hold(pool, S("index_ready"), h + 1)
                pool.indirect_dma_start(out=g3, out_offset=None, in_=edges,
                                        in_offset=bass.IndirectOffsetOnAxis(ap=next_i[:, 0:1], axis=0)
                                        ).then_inc(S("edges_in"), 16)
            any_edges = read_flag(pool)
            with pool.If(any_edges > 0):
                pool.memset(zeros, 0.0).then_inc(S("zeros_ready"), 1)
                pool.memset(c_tri, 1.0).then_inc(S("tri_ready"), 1)
                pool.wait_ge(S("tri_ready"), 1)
                pool.affine_select(out=c_tri, in_=c_tri, compare_op=ALU.is_gt, fill=0.0, base=0,
                                   pattern=[[-1, CH]], channel_multiplier=1).then_inc(S("tri_ready"), 1)
                any_edges_pool(pool, 0, 0, 1)
                any_edges_pool(pool, 1, 1, 0)
                for p in range(NPASS):
                    any_edges_pool(pool, 2 + p, 0, 1)
            pool.nop()

        @block.scalar
        def _(act):
            act.sem_inc(S("stored", 1), 16)
            act.wait_ge(S("norms_ready"), 1)
            act.activation(bound[:, 1:1 + T], bound[:, 1:1 + T], ACT.Sqrt).then_inc(S("norms_rooted"), 1)

            def evacuate(s, block_i, u):
                hold(act, S("counts_ready"), block_i * UPB + u + 1)
                act.activation(
                    stage[s].rearrange("p k i d -> p (k i) d").bitcast(i16)[:, :, u * UW:(u + 1) * UW].rearrange("p c (b w) -> p b w c", w=2),
                    ps[:, banks_of(u):banks_of(u) + UW // 2, 0:2 * AC].rearrange("p b (w c) -> p b w c", w=2),
                    ACT.Copy).then_inc(S("evacuated"), 1)

            def copy_degree(block_i):
                act.wait_ge(S("degree_ready"), block_i + 1)
                act.activation(deg_row[:, bass.ds(block_i * P, P)], bank(MISC)[:, 3 * P:4 * P],
                               ACT.Copy, scale=1.0 / BYTE).then_inc(S("degree_copied"), 1)

            def block_of(s, block_i, stored_before):
                if stored_before is not None:
                    act.wait_ge(S("stored", s), stored_before)
                for u in range(UPB):
                    evacuate(s, block_i, u)
                    if u == 5 and stored_before is not None:
                        copy_degree(block_i - 1)
            block_of(0, 0, None)
            with act.Fori(0, NH - 1) as k:
                block_of(1, 2 * k + 1, 16 * k + 16)
                block_of(0, 2 * k + 2, 16 * k + 16)
            copy_degree(NT - 1)

            act.wait_ge(S("degree_inverse"), 1)
            act.activation(deg_out[:, :], deg_out[:, :], ACT.Sqrt).then_inc(S("degree_norm"), 1)

            def split(p, source):
                if p > 0:
                    wait_sums(act, p - 1, NG - 1)
                for j in range(NG):
                    src = source(j)
                    act.activation(nodes(parts[:, 0], j), src, ACT.Copy, scale=scale_of(p)[0]).then_inc(S("hi_ready"), 1)

            def of_tmp(p):
                def source(j):
                    act.wait_ge(S("src_ready", p), j + 1)
                    return tmp[:, j % 2, 0:gw(j)]
                return source

            def of_x(layer):
                def source(j):
                    act.wait_ge(S("x_ready", layer), j + 1)
                    return nodes(x_nm, j)
                return source

            def of_message(p):
                def source(j):
                    m = tmp[:, j % 2, 0:gw(j)]
                    act.wait_ge(S("bias_added", p), j + 1)
                    act.activation(m, m, ACT.Relu).then_inc(S("src_ready", p), 1)
                    act.wait_ge(S("src_ready", p), j + 1)
                    return m
                return source

            def relu_x(g, b, w):
                act.activation(tmp[:, b, 0:w], xT[:, bass.ds(g * (GT * P), w)], ACT.Relu).then_inc(S("self_ready"), 1)

            def of_psum(p, func):
                def source(j):
                    act.wait_ge(S("src_in_psum", p), j + 1)
                    if j >= 2:
                        act.wait_ge(S("parts_ready"), j - 1 + NG * p)
                    act.activation(tmp[:, j % 2, 0:gw(j)], bank(SRC[j % 2], gw(j)), func).then_inc(S("src_ready", p), 1)
                    act.wait_ge(S("src_ready", p), j + 1)
                    return tmp[:, j % 2, 0:gw(j)]
                return source

            def copy_aggregates(p, first=None):
                def one(g, b, w):
                    if not isinstance(g, int) or g > 0:
                        act.wait_ge(S("proj_done"), g + NG * p)
                    if first:
                        first(g, b, w)
                    wait_sums(act, p, g)
                    act.activation(agg_s[:, 0:w], bank(AGG[b], w), ACT.Copy, scale=scale_of(p)[1]).then_inc(S("agg_copied"), 1)
                in_turns(act, one)

            def to_feat(p, to, func, bias, unscale=1.0):
                def one(g, b, w):
                    act.wait_ge(S("proj_done"), g + 1 + NG * p)
                    act.activation(to[:, bass.ds(g * (GT * P), w)], bank(PROJ, w), func, bias=bias,
                                   scale=unscale).then_inc(S("proj_used"), 1)
                in_turns(act, one)

            def std(kind, n):
                v = bn_a[:, 1:2] if kind == "bn" else mv[:, :, 1]
                act.wait_ge(S(f"{kind}_var_ready"), n + 1)
                act.activation(v, v, ACT.Sqrt).then_inc(S(f"{kind}_std_ready"), 1)

            def bn_relu(n):
                std("bn", n)
                act.wait_ge(S("bn_ready"), n + 1)
                for g in range(NG):
                    act.activation(hT[:, cols_of(g)], hT[:, cols_of(g)], ACT.Relu, bias=bn_a[:, 5:6],
                                   scale=bn_a[:, 4:5]).then_inc(S("relu_done", n), 1)

            def copy_xT(layer):
                std("ln", layer)
                for g in range(NG):
                    act.wait_ge(S("xT_in_psum", layer), g + 1)
                    act.activation(xT[:, cols_of(g)], bank(TR[g % 2], gw(g)), ACT.Copy).then_inc(S("xT_ready", layer), 1)

            act.wait_ge(S("cols_in"), 16)
            split(0, of_tmp(0))
            act.wait_ge(S("degree_inverse"), 2)
            act.activation(z_row, deg_row[:, :], ACT.Sqrt).then_inc(S("degree_norm"), 1)
            copy_aggregates(0)
            bn_relu(0)
            copy_xT(0)
            for t in range(T):
                split(1 + t, of_message(1 + t))
                if t == 0:
                    act.wait_ge(S("xT_ready", 0), NG)
                    act.wait_ge(S("parts_ready"), NG * 2)
                copy_aggregates(1 + t, relu_x if t == 0 else None)
            copy_xT(1)
            split(4, of_x(1))
            to_feat(4, hT, ACT.Identity, cvec[:, COL["b1"]:COL["b1"] + 1], unscale=scale_of(4)[1])
            bn_relu(1)
            for g in range(NG):
                act.wait_ge(S("lin2_done"), g + 1)
                act.activation(hT[:, cols_of(g)], bank(SRC[g % 2], gw(g)), ACT.Identity,
                               bias=cvec[:, COL["b2"]:COL["b2"] + 1]).then_inc(S("h2_ready"), 1)
            bn_relu(2)
            copy_xT(2)
            act.wait_ge(S("norms_ready"), 2)
            act.activation(bound[:, 1:3], bound[:, 1:3], ACT.Sqrt).then_inc(S("norms_rooted"), 1)
            split(5, of_x(2))
            to_feat(5, hT, ACT.Relu, cvec[:, COL["f_lb"]:COL["f_lb"] + 1])
            split(6, of_psum(6, ACT.Copy))
            act.wait_ge(S("bias_ready"), 1)
            to_feat(6, z_row, ACT.Relu, bn_a[:, 6:7])
            std("ln", 3)

        @block.vector
        def _(dve):
            ch = Chain(dve, S("vector_steps"))
            link = ch.link

            dve.wait_ge(S("consts"), 9)
            dve.tensor_copy(iota_r, iota_i)
            dve.tensor_copy(probe[:, :], probe_i[:, 0, :]).then_inc(S("probe_ready"), 1)
            link(dve.tensor_copy(bnd[:, :], bnd_i[:, :]))
            def power_of_two(k):
                b, sc, inv = bound[:, 0:1], scale[:, k, 0:1], scale[:, k, 1:2]
                link(dve.tensor_scalar(b, b, 2.0 ** -80, None, op0=ALU.max))
                link(dve.tensor_scalar(inv.bitcast(i32), b.bitcast(i32), 0x7F800000, None, op0=ALU.bitwise_and))
                link(dve.tensor_scalar(sc.bitcast(i32), inv.bitcast(i32), -1.0, float(254 << 23), op0=ALU.mult, op1=ALU.add))
                link(dve.tensor_scalar(sc, sc, 2.0 ** 14, None, op0=ALU.mult))
                link(dve.tensor_scalar(inv, inv, 2.0 ** -14 / BYTE, None, op0=ALU.mult))

            dve.wait_ge(S("x_in"), 16)
            dve.wait_ge(S("xtail_in"), 16)
            dve.tensor_reduce(bound[:, 1:2], x_nm[:, :, :].rearrange("p i d -> p (i d)"), axis=AX.X, op=ALU.max,
                              apply_absolute_value=True).then_inc(S("xmax_ready"), 1)
            dve.wait_ge(S("xmax_turned"), 1)
            dve.tensor_reduce(bound[0:1, 2:3], bank(MISC, P)[0:1, :], axis=AX.X, op=ALU.max).then_inc(S("xmax_ready"), 1)
            dve.wait_ge(S("xmax_spread"), 1)
            link(dve.tensor_copy(bound[:, 0:1], bank(MISC, 1)))
            power_of_two(0)
            dve.wait_ge(S("mats_in"), 16)
            dve.wait_ge(S("rows_in"), 16)
            we = wts[:, MAT["We0"]:MAT["We0"] + T, :].rearrange("p m d -> p (m d)")
            dve.tensor_tensor(square[:, 0:T * D], we, we, ALU.mult).then_inc(S("squares_ready"), 1)
            dve.wait_ge(S("squares_summed"), 1)
            link(dve.tensor_reduce(bound[:, 1:1 + T], bank(MISC, T * D).rearrange("p (t d) -> p t d", t=T), axis=AX.X, op=ALU.max))
            link(dve.tensor_reduce(bound[:, 4:4 + T], bank(DEG_BANK, T * D).rearrange("p (t d) -> p t d", t=T), axis=AX.X,
                                   op=ALU.max, apply_absolute_value=True))
            dve.sem_inc(S("norms_ready"), 1)
            dve.wait_ge(S("norms_rooted"), 1)
            for t in range(T):
                link(dve.scalar_tensor_tensor(bound[:, 0:1], bound[:, 1 + t:2 + t], XMAX, bound[:, 4 + t:5 + t],
                                              op0=ALU.mult, op1=ALU.add))
                power_of_two(1 + t)

            dve.wait_ge(S("heads_in"), 16)
            dve.tensor_copy(head_f, head_i).then_inc(S("heads_ready"), 1)
            dve.wait_ge(S("heads_spread"), 1)
            for h in range(NH):
                link(dve.tensor_scalar(junk[:, 0:HEADS], bank(MISC, HEADS), bnd[:, h:h + 1], 0.0,
                                       op0=ALU.is_lt, op1=ALU.add, accum_out=cnt[:, h:h + 1]))
            link(dve.tensor_scalar(row_f[:, :], cnt[:, :], -1.0, 0.0, op0=ALU.add, op1=ALU.max))
            dve.tensor_copy(row_i[:, :], row_f[:, :]).then_inc(S("rows_found"), 1)
            for h in range(NH):
                dve.wait_ge(S("row_in", h % NR), 16 * (h // NR + 1))
                dve.tensor_scalar(junk, rowg[:, h % NR, :], bnd[:, h:h + 1], 0.0, op0=ALU.is_lt, op1=ALU.add,
                                  accum_out=cnt2[:, h:h + 1]).then_inc(S("row_counted"), 1)
                dve.wait_ge(S("row_counted"), h + 1)
            link(dve.scalar_tensor_tensor(cnt[:, :], row_f[:, :], float(HROW), cnt2[:, :], op0=ALU.mult, op1=ALU.add))
            dve.memset(start_i[:, NH:NH + 1], 0)
            link(dve.tensor_scalar(start_i[:, 0:NH], cnt[:, :], float(E - WE), None, op0=ALU.min))
            dve.wait_ge(S("probe_done"), 1)
            link(dve.scalar_tensor_tensor(probe_f[:, :], probe_i[:, 0, :], float(P * BYTE), bank(DEG_BANK, int(MAXCOUNT)),
                                          op0=ALU.mult, op1=ALU.not_equal))
            dve.tensor_reduce(bound[:, 7:8], probe_f[:, :], axis=AX.X, op=ALU.max).then_inc(S("probe_done"), 1)
            link(dve.memset(deg_acc[:, :], 0.0))
            link(dve.memset(deg_max[:, :], 0.0))
            dve.tensor_copy(next_i[:, :], start_i[:, 0:1]).then_inc(S("index_ready"), 1)

            def window_keys(h, last=False):
                dve.wait_ge(S("edges_in"), 16 * h + 16)
                dve.tensor_scalar(lo_i.bitcast(i32), g3v[:, 0, :], P - 1, None, op0=ALU.bitwise_and)
                dve.tensor_scalar(hi_i.bitcast(i32), g3v[:, 0, :], 7, None, op0=ALU.logical_shift_right)
                link(dve.tensor_scalar(dl, g3v[:, 1, :], bnd[:, bass.ds(h, 1)], None, op0=ALU.subtract))
                dve.tensor_scalar(kw[:, 0, :], lo_i.bitcast(i32), 1.0, None, op0=ALU.add)
                dve.tensor_scalar(ge0, dl, 0.0, None, op0=ALU.is_ge)
                link(dve.scalar_tensor_tensor(key, g3v[:, 2, :], float(NT), hi_i.bitcast(i32), op0=ALU.mult, op1=ALU.add))
                link(dve.scalar_tensor_tensor(valid, dl, float(WN - 1), ge0, op0=ALU.is_le, op1=ALU.mult))
                link(dve.tensor_tensor(dl, dl, valid, ALU.mult))
                dve.scalar_tensor_tensor(kw[:, 0, :], dl, 2.0 * P, kw[:, 0, :], op0=ALU.mult, op1=ALU.add)
                dve.scalar_tensor_tensor(kw[:, 2, :], hi_i.bitcast(i32), 1.0, valid, op0=ALU.add, op1=ALU.mult)
                dve.scalar_tensor_tensor(kw[:, 1, :], key, 1.0, valid, op0=ALU.add, op1=ALU.mult).then_inc(S("keys_ready"), 1)

            def next_gather(h):
                dve.wait_ge(S("keys_ready"), h)
                dve.tensor_copy(next_i[:, :], start_i[:, bass.ds(h, 1)]).then_inc(S("index_ready"), 1)

            def take_keys(h):
                dve.wait_ge(S("keys_in_psum"), h + 1)
                link(dve.tensor_scalar(key_d, bank(MISC, P), 2.0 * P, None, op0=ALU.is_ge))
                dve.tensor_scalar(keysT[:, 3, :], key_d, FIELD - 1.0, 1.0, op0=ALU.mult, op1=ALU.add)
                dve.scalar_tensor_tensor(keysT[:, 2, :], key_d, -2.0 * P, bank(MISC, P), op0=ALU.mult, op1=ALU.add)
                dve.tensor_copy(keysT[:, 0:2, :], bank(MISC)[:, P:3 * P].rearrange("p (a w) -> p a w", a=2)).then_inc(S("keys_taken"), 1)
                dve.wait_ge(S("keys_taken"), h + 1)

            def onehots(block_i, half, b):
                s = b % 2
                B = NB * block_i + b
                if not (isinstance(B, int) and B < 2):
                    dve.wait_ge(S("onehots_used"), B - 1)
                w = half * SBW + b * BW
                def columns(c0, c1):
                    return onehot[:, s, c0:c1].rearrange("p (c w) -> p c w", w=BW)

                def key(a, c0, c1):
                    return keysT[:, a, w:w + BW].unsqueeze(1).to_broadcast([P, (c1 - c0) // BW, BW])
                for a, c0, c1 in ((2, OH_A, OH_L), (0, 0, OH_T), (1, OH_T, OH_A)):
                    dve.tensor_tensor(columns(c0, c1), iota_r[:, 0:c1 - c0].rearrange("p (c w) -> p c w", w=BW),
                                      key(a, c0, c1), ALU.is_equal).then_inc(S("onehot_steps"), 1)
                dve.wait_ge(S("onehot_steps"), 3 * B + 1)
                ins = dve.tensor_tensor(columns(OH_A, OH_L), columns(OH_A, OH_L), key(3, OH_A, OH_L), ALU.mult)
                ins.then_inc(S("onehots_ready"), 1)

            def take_outdegrees(block_i, step):
                dve.wait_ge(S("onehots_used"), NB * (block_i + 1))
                step(dve.tensor_copy(deg_i, bank(DEG_BANK, NT)))
                step(dve.tensor_scalar(deg_i, deg_i, 8, None, op0=ALU.logical_shift_right))
                step(dve.scalar_tensor_tensor(deg_b, deg_i, 1.0 - FIELD, bank(DEG_BANK, NT), op0=ALU.mult, op1=ALU.add))
                dve.tensor_tensor(deg_acc[:, :], deg_acc[:, :], deg_b, ALU.add)
                dve.tensor_tensor(deg_max[:, :], deg_max[:, :], deg_b, ALU.max).then_inc(S("outdegrees_taken"), 1)
                dve.wait_ge(S("outdegrees_taken"), block_i + 1)

            window_keys(0)
            next_gather(1)
            take_keys(0)
            for b in range(NB):
                onehots(0, 0, b)
            with dve.Fori(0, NH - 1) as k:
                ch.enter(k, 11)
                for b in range(NB):
                    onehots(2 * k + 1, 1, b)
                    if b == 0:
                        take_outdegrees(2 * k, link)
                    if b == 1:
                        window_keys(k + 1)
                dve.wait_ge(S("onehots_ready"), NB * (2 * k + 2))
                take_keys(k + 1)
                for b in range(NB):
                    onehots(2 * k + 2, 0, b)
                    if b == 0:
                        take_outdegrees(2 * k + 1, link)
                    if b == 1:
                        next_gather(k + 2)
                ch.leave(NH - 1)
            take_outdegrees(NT - 1, link)

            dve.tensor_copy(deg_out[:, :], deg_acc[:, :])
            dve.tensor_reduce(bound[:, 1:2], deg_acc, axis=AX.X, op=ALU.add)
            link(dve.tensor_reduce(bound[:, 2:3], deg_max, axis=AX.X, op=ALU.max))
            link(dve.tensor_scalar(bound[:, 2:3], bound[:, 2:3], MAXCOUNT, None, op0=ALU.is_gt))
            dve.tensor_tensor(bound[:, 2:3], bound[:, 2:3], bound[:, 7:8], ALU.add).then_inc(S("holds_counted"), 1)
            dve.wait_ge(S("holds_summed"), 1)
            link(dve.tensor_copy(bound[0:1, 4:6], bank(PROJ, 2)[0:1, :]))
            link(dve.tensor_scalar(bound[0:1, 4:5], bound[0:1, 4:5], float(E), None, op0=ALU.not_equal))
            link(dve.tensor_tensor(bound[0:1, 4:5], bound[0:1, 4:5], bound[0:1, 5:6], ALU.add))
            dve.tensor_scalar(flag[0:1, 0:1], bound[0:1, 4:5], 1.0, None, op0=ALU.min).then_inc(S("flag_ready"), 1)
            dve.wait_ge(S("degree_copied"), NT)
            any_edges = read_flag(dve)
            ach = Chain(dve, S("any_steps"))
            with dve.If(any_edges > 0):
                dve.memset(parts[:, 0], 1.0)
                dve.memset(parts[:, 1], 0.0).then_inc(S("ones_ready"), 1)
                dve.wait_ge(S("tri_ready"), 2)
                any_edges_vector(dve, ach, 0, ALL, 1)
                for g in range(NG):
                    dve.wait_ge(S("any_degree_turned"), g + 1)
                    dve.tensor_scalar(deg_row[:, cols_of(g)], bank(AGG[0], gw(g)), 1.0 / BYTE, None, op0=ALU.mult).then_inc(S("any_degree_taken"), 1)
                any_edges_vector(dve, ach, 1, ALL, 0)
                dve.wait_ge(S("any_outdegree_in"), 16)
                ach.link(dve.tensor_scalar(deg_out[:, :], deg_out[:, :], 1.0 / BYTE, None, op0=ALU.mult))
                dve.wait_ge(S("any_degree_taken"), NG)
            dve.nop()
            link(dve.tensor_scalar(deg_out[:, :], deg_out[:, :], 1.0, None, op0=ALU.max))
            dve.reciprocal(deg_out[:, :], deg_out[:, :]).then_inc(S("degree_inverse"), 1)
            dve.wait_ge(S("nt_in"), 16)
            dve.wait_ge(S("nttail_in"), 16)
            for t in range(T):
                link(dve.tensor_scalar(nt_m[:, t, :], nt_i[:, :], float(t), None, op0=ALU.is_equal))

            def subtract(p, source):
                for j in range(NG):
                    src = source(j)
                    dve.wait_ge(S("hi_ready"), j + 1 + NG * p)
                    dve.scalar_tensor_tensor(nodes(parts[:, 1], j), src, scale_of(p)[0], nodes(parts[:, 0], j),
                                             op0=ALU.mult, op1=ALU.subtract).then_inc(S("parts_ready"), 1)
                any_sums(p)

            def of_tmp(p):
                def source(j):
                    dve.wait_ge(S("src_ready", p), j + 1)
                    return tmp[:, j % 2, 0:gw(j)]
                return source

            def scaled(j):
                if j >= 2:
                    dve.wait_ge(S("parts_ready"), j - 1)
                for n, i in enumerate(tiles_of(j)):
                    ins = dve.tensor_scalar(tmp[:, j % 2, n * P:(n + 1) * P], x_nm[:, i, :], deg_out[:, i:i + 1], None, op0=ALU.mult)
                ins.then_inc(S("src_ready", 0), 1)
                dve.wait_ge(S("src_ready", 0), j + 1)
                return tmp[:, j % 2, 0:gw(j)]

            def stats_of(k, g, w):
                n = w if not isinstance(g, int) or g < NG - 1 else N - (NG - 1) * GT * P
                dve.bn_stats(stats[:, bass.ds(g, 1), :].rearrange("p o s -> p (o s)"),
                             hT[:, bass.ds(g * (GT * P), n)]).then_inc(S("stats_done", k), 1)

            def bn_scale(n, gamma, beta):
                dve.wait_ge(S("stats_done", n), NG)
                link(dve.bn_aggr(bn_a[:, 0:2], stats[:, 0:NG, :].rearrange("p g s -> p (g s)")))
                dve.tensor_scalar(bn_a[:, 1:2], bn_a[:, 1:2], BN_EPS, None, op0=ALU.add).then_inc(S("bn_var_ready"), 1)
                dve.wait_ge(S("bn_std_ready"), n + 1)
                link(dve.reciprocal(bn_a[:, 1:2], bn_a[:, 1:2]))
                link(dve.tensor_tensor(bn_a[:, 4:5], bn_a[:, 1:2], cvec[:, COL[gamma]:COL[gamma] + 1], ALU.mult))
                link(dve.tensor_tensor(bn_a[:, 3:4], bn_a[:, 0:1], bn_a[:, 4:5], ALU.mult))
                dve.tensor_tensor(bn_a[:, 5:6], cvec[:, COL[beta]:COL[beta] + 1], bn_a[:, 3:4], ALU.subtract).then_inc(S("bn_ready"), 1)

            def apart():
                dve.sem_inc(S("vector_holds"), 1)

            def tile(buf, i):
                return buf[:, i, :] if isinstance(i, int) else buf[:, bass.ds(i, 1), :].rearrange("p o d -> p (o d)")

            def node_stats(y, to, width):
                for n in range(width // P):
                    ins = dve.bn_stats(stats[:, n, :], y(n))
                link(ins)
                apart()
                for n in range(width // P):
                    ins = dve.bn_aggr(to(n), stats[:, n, :])
                link(ins)

            def layer_norm(layer, y=None):
                if y:
                    for g in range(NG):
                        y(g)
                        node_stats(lambda n: x_nm[:, GT * g + n, :], lambda n: mv[:, GT * g + n, :], gw(g))
                dve.tensor_scalar(mv[:, :, 1], mv[:, :, 1], LN_EPS, None, op0=ALU.add).then_inc(S("ln_var_ready"), 1)
                dve.wait_ge(S("ln_std_ready"), layer + 1)
                link(dve.reciprocal(mv[:, :, 1], mv[:, :, 1]))
                for g in range(NG):
                    for i in tiles_of(g):
                        ins = dve.tensor_scalar(x_nm[:, i, :], x_nm[:, i, :], mv[:, i, 0:1], mv[:, i, 1:2],
                                                op0=ALU.subtract, op1=ALU.mult)
                    ins.then_inc(S("x_ready", layer), 1)
                dve.wait_ge(S("x_ready", layer), NG)

            def plus_transposed(layer, times):
                def y(g):
                    dve.wait_ge(S("h_in_psum", layer), g + 1)
                    dve.scalar_tensor_tensor(nodes(x_nm, g), nodes(x_nm, g), times, bank(TR[g % 2], gw(g)),
                                             op0=ALU.mult, op1=ALU.add).then_inc(S("h_taken", layer), 1)
                    dve.wait_ge(S("h_taken", layer), g + 1)
                return y

            def any_sums(p):
                with dve.If(any_edges > 0):
                    any_edges_vector(dve, ach, 2 + p, PASSES[p], 1)
                dve.nop()

            dve.wait_ge(S("biases_spread"), 1)
            for n in range(2):
                ins = dve.tensor_copy(bias_b[:, n, :], bank(SRC[n], T * D))
            ins.then_inc(S("biases_taken"), 1)
            dve.wait_ge(S("degree_norm"), 1)
            subtract(0, scaled)
            link(dve.tensor_scalar(deg_row[:, :], deg_row[:, :], 1.0, None, op0=ALU.max))
            dve.reciprocal(deg_row[:, :], deg_row[:, :]).then_inc(S("degree_inverse"), 1)
            dve.wait_ge(S("degree_norm"), 2)
            dve.wait_ge(S("cols_in"), 16)

            def layer0_h(g, b, w):
                dve.wait_ge(S("proj_done"), g + 1)
                c = bass.ds(g * (GT * P), w)
                dve.tensor_tensor(hT[:, c], bank(PROJ, w), z_row[:, c], ALU.mult).then_inc(S("proj_used"), 1)
                dve.wait_ge(S("proj_used"), g + 1)
                dve.tensor_scalar(hT[:, c], hT[:, c], cvec[:, 0:1], None, op0=ALU.add).then_inc(S("h_ready", 0), 1)
                dve.wait_ge(S("h_ready", 0), g + 1)
                stats_of(0, g, w)
            in_turns(dve, layer0_h)
            bn_scale(0, "gamma", "beta")
            layer_norm(0, plus_transposed(0, 2.0))

            def update(g, width, first):
                terms = [(t, b) for b in ([True] if first else []) + [False] for t in range(T)]
                for k, (t, is_bias) in enumerate(terms):
                    for n in range(width // P):
                        i = GT * g + n if isinstance(g, int) else g * GT + n
                        m = nt_m[:, t, i:i + 1] if isinstance(i, int) else nt_m[:, t, bass.ds(i, 1)]
                        part = bias_b[:, 1, t * D:(t + 1) * D] if is_bias else ps[:, PROJ + n, t * D:(t + 1) * D]
                        if first and k == 0:
                            ins = dve.tensor_scalar(tile(z, i), part, m, None, op0=ALU.mult)
                        else:
                            ins = dve.scalar_tensor_tensor(tile(z, i), part, m, tile(z, i), op0=ALU.mult, op1=ALU.add)
                    if k < len(terms) - 1:
                        link(ins)
                ins.then_inc(S("proj_used"), 1)

            def message(t):
                def add_bias(j):
                    n = gw(j) // P
                    dve.wait_ge(S("src_in_psum", 1 + t), j + 1)
                    dve.tensor_tensor(tmp[:, j % 2, 0:gw(j)].rearrange("p (n d) -> p n d", d=D),
                                      bank(SRC[j % 2], gw(j)).rearrange("p (n d) -> p n d", d=D),
                                      bias_b[:, 0, t * D:(t + 1) * D].unsqueeze(1).to_broadcast([P, n, D]),
                                      ALU.add).then_inc(S("bias_added", 1 + t), 1)

                def source(j):
                    if j == 0:
                        add_bias(0)
                    if j + 1 < NG:
                        if j > 0:
                            dve.wait_ge(S("parts_ready"), NG * (1 + t) + j)
                        add_bias(j + 1)
                    dve.wait_ge(S("src_ready", 1 + t), j + 1)
                    return tmp[:, j % 2, 0:gw(j)]
                return source

            for t in range(T):
                subtract(1 + t, message(t))

                def take(g, b, w):
                    dve.wait_ge(S("proj_done"), g + 1 + NG * (1 + t))
                    update(g, w, t == 0)
                    if t == T - 1:
                        c = slice(GT * g, GT * g + w // P) if isinstance(g, int) else bass.ds(g * GT, w // P)
                        dve.wait_ge(S("proj_used"), g + 1 + NG * (1 + t))
                        x_g, z_g = (v[:, c, :].rearrange("p i d -> p (i d)") for v in (x_nm, z))
                        y = tmp[:, b, 0:w]
                        link(dve.scalar_tensor_tensor(y, x_g, 2.0, z_g, op0=ALU.mult, op1=ALU.add))
                        apart()
                        dve.tensor_copy(x_g, y)
                        node_stats(lambda n: tmp[:, b, n * P:(n + 1) * P], lambda n: mv_g[:, n, :], w)
                        link(dve.tensor_copy(mv[:, c, :], mv_g[:, 0:w // P, :]))
                take(0, 0, GT * P)
                take(1, 1, GT * P)
                with dve.Fori(0, (NG - 3) // 2) as k:
                    ch.enter(k, 2 * {0: 2 * T - 1, T - 1: T - 1 + 4}.get(t, T - 1))
                    take(2 * k + 2, 0, GT * P)
                    take(2 * k + 3, 1, GT * P)
                    ch.leave((NG - 3) // 2)
                take(NG - 1, 0, gw(NG - 1))
                dve.wait_ge(S("proj_used"), NG * (t + 2))

            layer_norm(1)

            def of_x(j):
                return nodes(x_nm, j)
            dve.wait_ge(S("eps_in"), 16)
            link(dve.tensor_scalar(bn_a[:, 7:8], eps_c[:, :], 1.0, X_SCALE * BYTE, op0=ALU.add, op1=ALU.mult))
            subtract(4, of_x)

            def plus_self(g, b, w):
                wait_sums(dve, 4, g)
                if not isinstance(g, int) or g > 0:
                    dve.wait_ge(S("proj_done"), g + NG * 4)
                dve.scalar_tensor_tensor(agg_s[:, 0:w], xT[:, bass.ds(g * (GT * P), w)], bn_a[:, 7:8], bank(AGG[b], w),
                                         op0=ALU.mult, op1=ALU.add).then_inc(S("agg_copied"), 1)

            def layer2(g, b, w):
                plus_self(g, b, w)
                if isinstance(g, int) and g == 0:
                    return
                dve.wait_ge(S("proj_used"), g + NG * 4)
                stats_of(1, g - 1, GT * P)
            dve.wait_ge(S("xT_ready", 1), NG)
            in_turns(dve, layer2)
            dve.wait_ge(S("proj_used"), NG * 5)
            stats_of(1, NG - 1, gw(NG - 1))
            bn_scale(1, "g1", "beta1")
            for g in range(NG):
                dve.wait_ge(S("h2_ready"), g + 1)
                stats_of(2, g, gw(g))
            bn_scale(2, "g2", "beta2")
            layer_norm(2, plus_transposed(2, 1.0))

            fl, fr = wts[:, MAT["f_lw"], :], wts[:, MAT["f_rw"], :]
            dve.wait_ge(S("late_mats_in"), 16)
            dve.tensor_tensor(square_l[:, 0:D], fl, fl, ALU.mult)
            lb = cvec[:, COL["f_lb"]:COL["f_lb"] + 1]
            dve.scalar_tensor_tensor(square_l[:, 2 * D:2 * D + 1], lb, -1.0, lb, op0=ALU.mult, op1=ALU.max)
            dve.tensor_tensor(square_l[:, D:2 * D], fr, fr, ALU.mult).then_inc(S("squares_ready"), 1)
            dve.wait_ge(S("squares_summed"), 2)
            link(dve.tensor_reduce(bound[:, 1:3], bank(PROJ, 2 * D).rearrange("p (t d) -> p t d", t=2), axis=AX.X, op=ALU.max))
            link(dve.tensor_copy(bound[:, 4:5], bank(PROJ)[:, 2 * D:2 * D + 1]))
            dve.sem_inc(S("norms_ready"), 1)
            dve.wait_ge(S("norms_rooted"), 2)
            for n in range(2):
                link(dve.scalar_tensor_tensor(bound[:, 4:5], bound[:, 1 + n:2 + n], XMAX, bound[:, 4:5], op0=ALU.mult, op1=ALU.add))
            link(dve.tensor_copy(bound[:, 0:1], bound[:, 4:5]))
            power_of_two(T + 1)
            dve.tensor_tensor(bn_a[:, 6:7], cvec[:, COL["n_lb"]:COL["n_lb"] + 1], cvec[:, COL["fc_b"]:COL["fc_b"] + 1], ALU.add).then_inc(S("bias_ready"), 1)
            for p in (5, 6):
                subtract(p, of_x if p == 5 else of_tmp(p))

                def mean(g, b, w):
                    wait_sums(dve, p, g)
                    if not isinstance(g, int) or g > 0:
                        dve.wait_ge(S("proj_done"), g + NG * p)
                    dve.scalar_tensor_tensor(agg_s[:, 0:w], bank(AGG[b], w), scale_of(p)[1],
                                             deg_row[:, bass.ds(g * (GT * P), w)],
                                             op0=ALU.mult, op1=ALU.mult).then_inc(S("agg_copied"), 1)
                in_turns(dve, mean)
            layer_norm(3, plus_transposed(3, 1.0))

        @block.tensor
        def _(pe):
            def mat(name):
                return wts[:, MAT[name], :]

            pe.wait_ge(S("consts"), 9)

            def transposes(buf, g, to):
                for n, i in enumerate(tiles_of(g)):
                    ins = pe.transpose(to[:, n * P:(n + 1) * P], buf(i), ident[:, :])
                return ins

            pe.wait_ge(S("xmax_ready"), 1)
            pe.transpose(bank(MISC)[0:1, 0:P], bound[:, 1:2], ident[:, :]).then_inc(S("xmax_turned"), 1)
            pe.wait_ge(S("xmax_ready"), 2)
            pe.matmul(bank(MISC, 1), ones[0:1, :], bound[0:1, 2:3], start=True, stop=True).then_inc(S("xmax_spread"), 1)
            pe.wait_ge(S("squares_ready"), 1)
            pe.matmul(bank(MISC, T * D), ones[:, :], square[:, :], start=True, stop=True)
            pe.matmul(bank(DEG_BANK, T * D), ones[0:1, :], rvec[:, 0, :], start=True, stop=True).then_inc(S("squares_summed"), 1)
            pe.wait_ge(S("norms_rooted"), 1)
            pe.wait_ge(S("heads_ready"), 1)
            pe.matmul(bank(MISC, HEADS), ones[0:1, :], head_f, start=True, stop=True).then_inc(S("heads_spread"), 1)

            def turn_keys(h):
                pe.wait_ge(S("keys_ready"), h + 1)
                for a in range(3):
                    ins = pe.transpose(bank(MISC)[:, a * P:(a + 1) * P], kw[:, a, :], ident[:, :])
                ins.then_inc(S("keys_in_psum"), 1)

            def count(block_i, b):
                s = b % 2
                pe.wait_ge(S("onehots_ready"), NB * block_i + b + 1)
                place = onehot[:, s, 0:OH_A].rearrange("p (c w) -> p c w", w=BW)
                source = onehot[:, s, OH_A:OH_L].rearrange("p (c w) -> p c w", w=BW)
                for j in range(BW // UW):
                    u = b * (BW // UW) + j
                    if not (isinstance(block_i, int) and u < 3):
                        pe.wait_ge(S("evacuated"), block_i * UPB + {0: -3, 1: 0, 2: -1, UPB - 1: UPB - 2}.get(u, u - 2))
                    for w in range(UW):
                        o = ps[:, banks_of(u) + w // 2, w % 2 * AC:(w % 2 + 1) * AC]
                        ins = pe.matmul(o, source[:, :, j * UW + w], place[:, :, j * UW + w], start=True, stop=True)
                    ins.then_inc(S("counts_ready"), 1)
                    if b == 0 and j == 0 and not isinstance(block_i, int):
                        pe.wait_ge(S("outdegrees_taken"), block_i)
                    for w in range(j * UW, (j + 1) * UW):
                        last = pe.matmul(bank(DEG_BANK, NT), source[:, :, w], place[:, T * NT:, w],
                                         start=(b == 0 and w == 0), stop=(b == NB - 1 and w == BW - 1))
                last.then_inc(S("onehots_used"), 1)

            def indegree(s, block_i):
                hold(pe, S("evacuated"), (block_i + 1) * UPB)
                for i in range(NT):
                    ins = pe.matmul(bank(MISC)[:, 3 * P:4 * P], ones_h[:, :], stage[s][:, ALL, i, :], start=(i == 0), stop=(i == NT - 1))
                ins.then_inc(S("degree_ready"), 1)

            pe.wait_ge(S("probe_ready"), 1)
            pe.matmul(bank(DEG_BANK, int(MAXCOUNT)), ones_h[:, :], probe[:, :].bitcast(fp8), start=True, stop=True).then_inc(S("probe_done"), 1)

            turn_keys(0)
            pe.wait_ge(S("probe_done"), 2)
            for b in range(NB):
                count(0, b)
            with pe.Fori(0, NH - 1) as k:
                for b in range(NB):
                    count(2 * k + 1, b)
                    if b == 1:
                        indegree(0, 2 * k)
                    if b == 2:
                        pe.wait_ge(S("degree_copied"), 2 * k + 1)
                        turn_keys(k + 1)
                for b in range(NB):
                    count(2 * k + 2, b)
                    if b == 1:
                        indegree(1, 2 * k + 1)
            pe.wait_ge(S("degree_copied"), NT - 1)
            indegree(0, NT - 1)

            pe.wait_ge(S("holds_counted"), 1)
            pe.matmul(bank(PROJ, 2), ones[:, :], bound[:, 1:3], start=True, stop=True).then_inc(S("holds_summed"), 1)
            any_edges = read_flag(pe)
            with pe.If(any_edges > 0):
                any_edges_tensor(pe, 0)
                for g in range(NG):
                    pe.wait_ge(S("any_degree_in"), 16 * g + 16)
                    if g > 0:
                        pe.wait_ge(S("any_degree_taken"), g)
                    transposes(lambda i: sums_n[:, i % GT, :], g, bank(AGG[0])).then_inc(S("any_degree_turned"), 1)
                any_edges_tensor(pe, 1)
            pe.nop()

            def turn_sums(p, g, b, w):
                pe.wait_ge(S("sums_in"), 16 * g + 16 * (NG * p + 1))
                n = w // P
                pe.sem_inc(S("chunk_used"), NC - n)
                for i in range(n):
                    pe.transpose(bank(AGG[b])[:, i * P:(i + 1) * P], sums_n[:, i, :], ident[:, :]).then_inc(S("chunk_used"), 1)

            def aggregate(p, g, b, w):
                with pe.If(any_edges > 0):
                    turn_sums(p, g, b, w)
                with pe.Else():
                    multiply(p, g, b, w)
                pe.nop()

            def multiply(p, g, b, w):
                gq = NG * p + g
                for c in range(NC):
                    hold(pe, S("chunk_in", c), 16 * gq + 16)
                    if isinstance(g, int) and g == 0:
                        pe.wait_ge(S("parts_ready"), min(NG, (c * CI + CI - 1) // GT + 1) + NG * p)
                    for i in range(CI):
                        moving = ring[:, c, 0:w // P, i * P:(i + 1) * P].bitcast(fp8)
                        for s in range(PARTS):
                            t = c * CI + i
                            ins = pe.matmul(bank(AGG[b], w), parts[:, s, t, :], moving,
                                            start=(t == 0 and s == 0), stop=(t == NT - 1 and s == PARTS - 1))
                    ins.then_inc(S("chunk_used"), 1)

            def run_pass(p, project):
                in_lag = GT * P
                with pe.If(any_edges > 0):
                    any_edges_tensor(pe, 2 + p)
                pe.nop()
                aggregate(p, 0, 0, in_lag)
                aggregate(p, 1, 1, in_lag)
                lagged(p, 0, 0, in_lag, project)
                with pe.Fori(0, (NG - 3) // 2) as k:
                    aggregate(p, 2 * k + 2, 0, in_lag)
                    lagged(p, 2 * k + 1, 1, in_lag, project)
                    aggregate(p, 2 * k + 3, 1, in_lag)
                    lagged(p, 2 * k + 2, 0, in_lag, project)
                aggregate(p, NG - 1, 0, gw(NG - 1))
                lagged(p, NG - 2, 1, in_lag, project)
                lagged(p, NG - 1, 0, gw(NG - 1), project)

            def lagged(p, g, b, w, project):
                pe.wait_ge(S("agg_copied"), g + 1 + NG * p)
                if not isinstance(g, int) or g > 0:
                    pe.wait_ge(S("proj_used"), g + NG * p)
                project(g, b, w).then_inc(S("proj_done"), 1)

            def to_nodes(layer, buf, before):
                for g in range(NG):
                    before(g)
                    if g >= 2:
                        pe.wait_ge(S("h_taken", layer), g - 1)
                    transposes(lambda i: buf[:, i * P:(i + 1) * P], g, bank(TR[g % 2])).then_inc(S("h_in_psum", layer), 1)

            def to_features(layer):
                for g in range(NG):
                    pe.wait_ge(S("x_ready", layer), g + 1)
                    if g >= 2:
                        pe.wait_ge(S("xT_ready", layer), g - 1)
                    transposes(lambda i: x_nm[:, i, :], g, bank(TR[g % 2])).then_inc(S("xT_in_psum", layer), 1)

            for n in range(2):
                ins = pe.matmul(bank(SRC[n], T * D), ones[0:1, :], rvec[:, n, :], start=True, stop=True)
            ins.then_inc(S("biases_spread"), 1)
            pe.wait_ge(S("biases_taken"), 1)
            run_pass(0, lambda g, b, w: pe.matmul(bank(PROJ, w), mat("W"), agg_s[:, 0:w], start=True, stop=True))
            to_nodes(0, hT, lambda g: pe.wait_ge(S("relu_done", 0), g + 1))
            to_features(0)

            def node_update(t):
                def project(g, b, w):
                    if t == 0:
                        pe.wait_ge(S("self_ready"), g + 1)
                    terms = ([(0, tmp[:, b, :])] if t == 0 else []) + [(1 + t, agg_s)]
                    for n in range(w // P):
                        for j, (k, buf) in enumerate(terms):
                            m = MAT[f"Wn{k}0"]
                            ins = pe.matmul(ps[:, PROJ + n, 0:T * D], buf[:, n * P:(n + 1) * P],
                                            wts[:, m:m + T, :].rearrange("p m d -> p (m d)"),
                                            start=(j == 0), stop=(j == len(terms) - 1))
                    return ins
                return project
            for t in range(T):
                if t > 0:
                    pe.wait_ge(S("proj_used"), NG * (t + 1))
                for g in range(NG):
                    if g >= 2:
                        pe.wait_ge(S("bias_added", 1 + t), g - 1)
                    for n, i in enumerate(tiles_of(g)):
                        o = bank(SRC[g % 2])[:, n * P:(n + 1) * P]
                        ins = pe.matmul(o, xT[:, i * P:(i + 1) * P], mat(f"We{t}"), start=True, stop=True)
                    ins.then_inc(S("src_in_psum", 1 + t), 1)
                run_pass(1 + t, node_update(t))
            to_features(1)

            pe.wait_ge(S("late_mats_in"), 16)
            run_pass(4, lambda g, b, w: pe.matmul(bank(PROJ, w), mat("W1"), agg_s[:, 0:w], start=True, stop=True))
            for g in range(NG):
                pe.wait_ge(S("relu_done", 1), g + 1)
                if g >= 2:
                    pe.wait_ge(S("h2_ready"), g - 1)
                pe.matmul(bank(SRC[g % 2], gw(g)), mat("W2"), hT[:, cols_of(g)], start=True, stop=True).then_inc(S("lin2_done"), 1)
            to_nodes(2, hT, lambda g: pe.wait_ge(S("relu_done", 2), g + 1))
            to_features(2)

            def sage(p, terms):
                def project(g, b, w):
                    o = bank(PROJ, w)
                    c = bass.ds(g * (GT * P), w)
                    pe.matmul(o, mat(terms[0]), agg_s[:, 0:w], start=True, stop=False)
                    for n, (m, buf) in enumerate(terms[1:]):
                        ins = pe.matmul(o, mat(m), buf[:, c], start=False, stop=(n == len(terms) - 2))
                    return ins
                run_pass(p, project)
            pe.wait_ge(S("squares_ready"), 2)
            pe.matmul(bank(PROJ, 2 * D + 1), ones[:, :], square_l, start=True, stop=True).then_inc(S("squares_summed"), 1)
            pe.wait_ge(S("xT_ready", 2), NG)
            sage(5, ["f_lw", ("f_rw", xT)])
            pe.wait_ge(S("proj_used"), NG * 6)
            for g in range(NG):
                if g >= 2:
                    pe.wait_ge(S("src_ready", 6), g - 1)
                transposes(lambda i: hT[:, i * P:(i + 1) * P], g, bank(SRC[g % 2])).then_inc(S("src_in_psum", 6), 1)
            sage(6, ["n_lw", ("n_rw", hT), ("fc", xT)])
            to_nodes(3, z_row, lambda g: pe.wait_ge(S("proj_used"), NG * 7) if g == 0 else None)


def kernel(**inputs):
    import numpy as np
    import concourse.bacc as bacc
    from concourse.bass_utils import run_bass_kernel_spmd

    a = {k: np.asarray(v) for k, v in inputs.items()}
    t = lambda w: np.ascontiguousarray(w.T)
    we, wn = a["L1_gnn_W_e"], a["L1_gnn_W_n"]
    D = a["x"].shape[1]
    mats = [a["L0_gnn_W"]] + [we[i].T for i in range(3)]
    mats += [wn[i][:, k * D:(k + 1) * D].T for k in range(4) for i in range(3)]
    mats += [a[f"L2_gnn_{n}"].T for n in ("W1", "W2")]
    mats += [a[f"L3_gnn_{n}"].T for n in ("fc_w", "f_lw", "f_rw", "n_lw", "n_rw")]
    cols = [a[n] for n in ("L0_gnn_b", "L0_gnn_gamma", "L0_gnn_beta", "L2_gnn_b1", "L2_gnn_g1", "L2_gnn_beta1",
                           "L2_gnn_b2", "L2_gnn_g2", "L2_gnn_beta2", "L3_gnn_f_lb", "L3_gnn_n_lb", "L3_gnn_fc_b")]
    rows = [a["L1_gnn_b_e"].reshape(-1), a["L1_gnn_b_n"].reshape(-1)]
    arrays = {
        "x": a["x"],
        "edges": np.ascontiguousarray(np.stack([a["src"], a["dst"], a["edge_type_3"]], axis=1)),
        "dst": a["dst"],
        "node_type": a["node_type_3"],
        "mats": np.ascontiguousarray(np.concatenate(mats, axis=1)),
        "cols": np.ascontiguousarray(np.stack(cols, axis=1)),
        "rows": np.ascontiguousarray(np.stack(rows, axis=0)),
        "eps2": a["L2_gnn_eps"],
    }
    nc = bacc.Bacc("TRN2", target_bir_lowering=False, num_devices=1)
    args = [nc.dram_tensor(n, v.shape, mybir.dt.from_np(v.dtype), kind="ExternalInput").ap() for n, v in arrays.items()]
    out = nc.dram_tensor("out", a["x"].shape, mybir.dt.float32, kind="ExternalOutput").ap()
    gnn_resnorm_kernel(nc, *args, out)
    r = run_bass_kernel_spmd(nc, [arrays], core_ids=[0])
    return r.results[0]["out"]
```

```python
import concourse.bass as bass
from concourse import mybir
from contextlib import ExitStack


class Chain:

    def __init__(self, eng, sem):
        self.eng, self.sem, self.done, self.turn = eng, sem, 0, 0

    def link(self, ins):
        ins.then_inc(self.sem, 1)
        self.done += 1
        self.eng.wait_ge(self.sem, self.turn + self.done)

    def enter(self, i, per_turn):
        self.before, self.per, self.turn = self.done, per_turn, i * per_turn

    def leave(self, turns):
        assert self.done - self.before == self.per, (self.done - self.before, self.per)
        self.done, self.turn = self.before + turns * self.per, 0


def gnn_resnorm_kernel(nc, x, edges, dst, node_type, mats, cols, rows, eps2, out):
    fp32, fp16 = mybir.dt.float32, mybir.dt.float16
    fp8, u8, i16, i32 = mybir.dt.float8e4, mybir.dt.uint8, mybir.dt.int16, mybir.dt.int32
    ALU, ACT, AX = mybir.AluOpType, mybir.ActivationFunctionType, mybir.AxisListType

    N, D = x.shape
    E = edges.shape[0]
    T = 3
    P = 128
    NT = -(-N // P)
    NP = NT * P
    LASTN = N - (NT - 1) * P
    GT = 4
    NG = -(-NT // GT)
    WN = 2
    WE = 128
    SBW = P // WN
    NH = -(-NT // 2)
    KINDS = T + 1
    AC = KINDS * NT
    BW = 16
    NB = SBW // BW
    UW = 4
    UPB = SBW // UW
    FIELD = 256.0
    BYTE = 2.0 ** -9
    HEADS = 375
    HROW = E // HEADS
    ROWS_AT_ONCE = 5
    assert HEADS * HROW == E and NT % 2 == 1
    CI = 7
    NC = NT // CI
    PARTS = 2
    BN_EPS = LN_EPS = 1e-5
    XMAX = 11.5
    X_SCALE = 2.0 ** 11
    MAXCOUNT = 16.0

    EARLY = ["W"] + [f"We{t}" for t in range(T)] + [f"Wn{k}{t}" for k in range(T + 1) for t in range(T)]
    LATE = ["W1", "W2", "fc", "f_lw", "f_rw", "n_lw", "n_rw"]
    MAT = {n: i for i, n in enumerate(EARLY)} | {n: i for i, n in enumerate(LATE)}
    COL = {n: i for i, n in enumerate(
        ["b", "gamma", "beta", "b1", "g1", "beta1", "b2", "g2", "beta2", "f_lb", "n_lb", "fc_b"])}
    ALL = T
    PASSES = [ALL, 0, 1, 2, ALL, ALL, ALL]
    NPASS = len(PASSES)

    CH = 125
    NCH = E // CH
    assert NCH * CH == E
    table = nc.dram_tensor("table", (NP, PARTS, D), fp16, kind="Internal").ap()
    sums = nc.dram_tensor("sums", (NP, D), fp32, kind="Internal").ap()
    adj = nc.dram_tensor("adjacency", (KINDS, NT, P, NT * P), u8, kind="Internal").ap()

    ctx = ExitStack()
    with ctx:
        def sb(name, shape, dt):
            return ctx.enter_context(nc.sbuf_tensor(name, shape, dt))

        def sem(name):
            return ctx.enter_context(nc.semaphore(name))

        x_nm = sb("x_nm", [P, NT, D], fp32)
        feat = sb("feat", [P, 2, NP], fp32)
        xT, hT = feat[:, 0, :], feat[:, 1, :]
        stage = [feat[:, s, :].bitcast(fp8).rearrange("p (k i d) -> p k i d", k=KINDS, d=P) for s in range(2)]
        deg_pairs = sb("deg_pairs", [P, NH * 2 * P], fp32)
        deg_row = deg_pairs[:, 0:NP]
        z = sb("z", [P, NT, D], fp32)
        z_row = z[:, :, :].rearrange("p i d -> p (i d)")
        work = sb("work", [P, 10000], fp32)
        parts = work[:, 0:PARTS * NT * D // 2].bitcast(fp16).rearrange("p (s i d) -> p s i d", s=PARTS, d=D)
        scale = sb("scale", [P, T + 2, 2], fp32)
        bound = sb("bound", [P, 8], fp32)
        ring = sb("ring", [P, NC, GT, CI * P], u8)
        wts = sb("wts", [P, len(EARLY), D], fp32)
        cvec = sb("cvec", [P, len(COL)], fp32)
        rvec = sb("rvec", [1, 2, T * D], fp32)
        eps_c = sb("eps_c", [P, 1], fp32)
        ident = sb("ident", [P, P], fp32)
        ones = sb("ones", [P, P], fp32)
        ones_h = sb("ones_h", [P, P], fp16)
        probe = sb("probe", [P, int(MAXCOUNT)], u8)
        probe_i = sb("probe_i", [P, int(MAXCOUNT)], i32)
        probe_f = sb("probe_f", [P, int(MAXCOUNT)], fp32)
        agg_s = sb("agg_s", [P, GT * P], fp32)
        square_l = agg_s[:, 0:2 * D + 1]
        tmp = sb("tmp", [P, 2, GT * P], fp32)
        nt_i = sb("nt_i", [P, NT], i32)
        nt_m = sb("nt_m", [P, T, NT], fp32)
        deg_out = sb("deg_out", [P, NT], fp32)
        stats = sb("stats", [P, max(NG, GT), 6], fp32)
        mv = sb("mv", [P, NT, 2], fp32)
        mv_g = sb("mv_g", [P, GT, 2], fp32)
        bn_a = sb("bn_a", [P, 8], fp32)
        start_i = sb("start_i", [P, NH + 1], i32)
        next_i = sb("next_i", [P, 1], i32)

        flag = sb("flag", [1, 1], i32)
        ring_f = ring[:, :, :, :].rearrange("p c b n -> p (c b n)").bitcast(fp32)
        o = [0]

        def of_ring(words):
            o[0] += words
            assert o[0] <= ring_f.shape[1]
            return ring_f[:, o[0] - words:o[0]]
        c_edges = of_ring(3)[0:CH].bitcast(i32)
        c_rows = of_ring(PARTS * D // 2)[0:CH].bitcast(fp16)
        c_old, c_new = of_ring(D)[0:CH], of_ring(D)[0:CH]
        c_diag = of_ring(P)[0:CH, 0:CH]
        c_same = of_ring(P)[0:CH, 0:CH]
        c_sel = of_ring(P)[0:CH].bitcast(fp16)[:, 0:CH]
        c_tri = of_ring(P)[0:CH, 0:CH]
        c_idx = of_ring(1)[0:CH].bitcast(i32)
        c_dst, c_typ, c_dup, c_idf = (of_ring(1)[0:CH] for _ in range(4))
        zeros = of_ring(GT * P)
        sums_n = of_ring(GT * P).rearrange("p (i d) -> p i d", d=D)

        at = [0]

        def scratch(words):
            at[0] += words
            assert at[0] <= work.shape[1]
            return work[:, at[0] - words:at[0]]
        onehot = scratch(BW * (AC + P)).bitcast(fp16).rearrange("p (s n) -> p s n", s=2)
        OH_T, OH_A, OH_L = T * NT * BW, AC * BW, (AC + P) * BW
        keysT = scratch(4 * P // 2).bitcast(fp16).rearrange("p (a w) -> p a w", a=4)
        key_d = scratch(P)
        to_dst = scratch(P).bitcast(fp16).rearrange("p (w d) -> p w d", d=WN)
        g3 = scratch(3 * WE).bitcast(i32)
        deg_acc, deg_max, deg_b = (scratch(NT) for _ in range(3))
        deg_i = scratch(NT).bitcast(i32)
        bnd = scratch(NH)
        cnt, cnt2, row_f = (scratch(NH) for _ in range(3))
        bnd_i, row_i = scratch(NH).bitcast(i32), scratch(NH).bitcast(i32)
        g3v = g3.rearrange("p (e a) -> p a e", a=3)
        lo_i, hi_i, dl, ge0, valid, key = (scratch(WE) for _ in range(6))
        kw = scratch(3 * WE).rearrange("p (a e) -> p a e", a=3)
        iota_r = scratch(AC * BW // 2).bitcast(fp16)
        bias_b = work[:, PARTS * NT * D // 2:PARTS * NT * D // 2 + 2 * T * D].rearrange("p (a d) -> p a d", a=2)
        square = work[:, PARTS * NT * D // 2 + 2 * T * D:PARTS * NT * D // 2 + 3 * T * D]
        f_flat = feat[:, :, :].rearrange("p a n -> p (a n)")
        iota_i = f_flat[:, 0:AC * BW].bitcast(i32)
        NR = 8
        o = AC * BW
        rowg = f_flat[:, o:o + NR * HROW].bitcast(i32).rearrange("p (s n) -> p s n", s=NR)
        o += NR * HROW
        junk = f_flat[:, o:o + HROW]
        o += HROW
        head_i = f_flat[0:1, o:o + HEADS].bitcast(i32)
        head_f = f_flat[0:1, o + HEADS:o + 2 * HEADS]

        ps = ctx.enter_context(nc.psum_tensor("ps", [P, 8, 512], fp32))
        A_BANK, DEG_BANK, MISC = (0, 2, 4), 6, 7
        AGG, PROJ, SRC, XT, TR = (0, 1), 2, (2, 3), (4, 5), (6, 7)

        made = {}

        def S(signal, phase=""):
            name = f"{signal}{phase}"
            if name not in made:
                made[name] = ctx.enter_context(nc.semaphore(name))
            return made[name]

        block = ctx.enter_context(nc.Block())

        def gw(g):
            return min(GT * P, NP - g * GT * P)

        def cols_of(g):
            return slice(g * GT * P, g * GT * P + gw(g))

        def tiles_of(g):
            return range(GT * g, min(GT * (g + 1), NT))

        def banks_of(u):
            return A_BANK[u % 3 if u < UPB - 1 else 1]

        def bank(i, w=512):
            return ps[:, i, 0:w]

        def nodes(buf, g):
            return buf[:, GT * g:min(GT * (g + 1), NT), :].rearrange("p i d -> p (i d)")

        def in_turns(eng, one, then=None):
            one(0, 0, GT * P)
            one(1, 1, GT * P)
            if then:
                then()
            with eng.Fori(0, (NG - 3) // 2) as k:
                one(2 * k + 2, 0, GT * P)
                one(2 * k + 3, 1, GT * P)
            one(NG - 1, 0, gw(NG - 1))

        def hold(eng, signal, value):
            eng.wait_ge(signal, value)
            if not isinstance(value, int):
                eng.sem_inc(S("holds"), 1)

        def scale_of(p):
            k = {0: 0, 1: 1, 2: 2, 3: 3, 6: T + 1}.get(p)
            return (X_SCALE, 1.0 / (X_SCALE * BYTE)) if k is None else (scale[:, k, 0:1], scale[:, k, 1:2])

        def table_init(sp, n, ready, count):
            sp.wait_ge(ready, count)
            sp.wait_ge(S("zeros_ready"), 1)
            for k in range(PARTS):
                sp.dma_start(table[:, k, :].rearrange("(i p) d -> p i d", p=P), parts[:, k]).then_inc(S("init_done"), 16)
            for g in range(NG):
                sp.dma_start(sums[g * GT * P:g * GT * P + gw(g), :].rearrange("(i p) d -> p i d", p=P),
                             zeros[:, 0:gw(g)].rearrange("p (i d) -> p i d", d=D)).then_inc(S("init_done"), 16)
            sp.wait_ge(S("init_done"), 16 * (PARTS + NG) * (n + 1))

        def any_edges_sync(sp, n):
            sp.dma_start(c_edges, edges[0:CH, :]).then_inc(S("chunk_edges_in", n // 2), 16)
            with sp.Fori(1, NCH) as i:
                hold(sp, S("sums_put", n // 2), 16 * i + 16 * (n % 2 * NCH))
                sp.dma_start(c_edges, edges[bass.ds(i * CH, CH), :]).then_inc(S("chunk_edges_in", n // 2), 16)
            sp.wait_ge(S("sums_put", n // 2), 16 * (n % 2 + 1) * NCH)

        def any_edges_pool(pool, n, src, dst_col):
            with pool.Fori(0, NCH) as i:
                hold(pool, S("chunk_edges_in", n // 2), 16 * i + 16 * (n % 2 * NCH + 1))
                pool.indirect_dma_start(out=c_rows, out_offset=None, in_=table.rearrange("n s d -> n (s d)"),
                                        in_offset=bass.IndirectOffsetOnAxis(ap=c_edges[:, src:src + 1], axis=0)
                                        ).then_inc(S("chunk_rows_in", n // 2), 16)
                pool.indirect_dma_start(out=c_old, out_offset=None, in_=sums,
                                        in_offset=bass.IndirectOffsetOnAxis(ap=c_edges[:, dst_col:dst_col + 1], axis=0)
                                        ).then_inc(S("chunk_old_in", n // 2), 16)
                hold(pool, S("chunk_new"), i + (n * NCH + 1))
                pool.indirect_dma_start(out=sums, out_offset=bass.IndirectOffsetOnAxis(ap=c_idx[:, 0:1], axis=0),
                                        in_=c_new, in_offset=None, bounds_check=NP - 1, oob_is_err=False
                                        ).then_inc(S("sums_put", n // 2), 16)

        def any_edges_vector(dve, ch, n, kind, dst_col):
            with dve.Fori(0, NCH) as i:
                ch.enter(i, 7)
                dve.wait_ge(S("chunk_edges_in", n // 2), 16 * i + 16 * (n % 2 * NCH + 1))
                ch.link(dve.tensor_copy(c_dst, c_edges[:, dst_col:dst_col + 1]))
                dve.tensor_scalar(c_diag, ident[0:CH, 0:CH], c_dst, None, op0=ALU.mult).then_inc(S("chunk_diag"), 1)
                if kind == ALL:
                    ch.link(dve.memset(c_typ, BYTE))
                else:
                    ch.link(dve.tensor_scalar(c_typ, c_edges[:, 2:3], float(kind), BYTE, op0=ALU.is_equal, op1=ALU.mult))
                dve.wait_ge(S("chunk_spread"), i + (n * NCH + 1))
                ch.link(dve.tensor_scalar(c_same, bank(PROJ, CH)[0:CH], c_dst, None, op0=ALU.is_equal))
                dve.tensor_scalar(c_sel, c_same, c_typ, None, op0=ALU.mult).then_inc(S("chunk_sel"), 1)
                ch.link(dve.tensor_tensor(c_diag, c_same, c_tri, ALU.mult))
                ch.link(dve.tensor_reduce(c_dup, c_diag, axis=AX.X, op=ALU.add))
                ch.link(dve.scalar_tensor_tensor(c_idf, c_dup, float(NP), c_dst, op0=ALU.mult, op1=ALU.add))
                dve.tensor_copy(c_idx, c_idf)
                dve.wait_ge(S("chunk_old_in", n // 2), 16 * i + 16 * (n % 2 * NCH + 1))
                dve.wait_ge(S("chunk_sum"), i + (n * NCH + 1))
                ch.link(dve.tensor_tensor(c_new, c_old, bank(PROJ + 1)[0:CH, 0:D], ALU.add))
                dve.tensor_tensor(c_new, c_new, bank(PROJ + 1)[0:CH, D:2 * D], ALU.add).then_inc(S("chunk_new"), 1)
                dve.wait_ge(S("chunk_new"), i + (n * NCH + 1))
                ch.leave(NCH)

        def any_edges_tensor(pe, n):
            with pe.Fori(0, NCH) as i:
                pe.wait_ge(S("chunk_diag"), i + (n * NCH + 1))
                pe.matmul(bank(PROJ, CH)[0:CH], ones[0:CH, 0:CH], c_diag, start=True, stop=True).then_inc(S("chunk_spread"), 1)
                pe.wait_ge(S("chunk_sel"), i + (n * NCH + 1))
                pe.wait_ge(S("chunk_rows_in", n // 2), 16 * i + 16 * (n % 2 * NCH + 1))
                pe.matmul(bank(PROJ + 1)[0:CH, 0:PARTS * D], c_sel, c_rows, start=True, stop=True).then_inc(S("chunk_sum"), 1)

        def read_flag(eng):
            eng.wait_ge(S("flag_ready"), 1)
            return eng.value_load(flag[0:1, 0:1], min_val=0, max_val=1)

        def wait_sums(eng, p, g):
            eng.wait_ge(S("chunk_used"), NC * (NG * p + g + 1))

        @block.sync
        def _(sp):
            with nc.allow_non_contiguous_dma(reason="single integers"):
                sp.dma_start(head_i, dst.rearrange("(r c) -> c r", c=HROW)[0:1, :]).then_inc(S("heads_in"), 16)
            sp.dma_start(x_nm[:, 0:NT - 1, :], x[0:(NT - 1) * P, :].rearrange("(i p) d -> p i d", p=P)).then_inc(S("x_in"), 16)
            sp.wait_ge(S("consts"), 2)
            sp.dma_start(x_nm[0:LASTN, NT - 1, :], x[(NT - 1) * P:N, :]).then_inc(S("x_in"), 16)
            sp.dma_start(wts[:, :, :], mats[:, 0:len(EARLY) * D].rearrange("p (m d) -> p m d", d=D)).then_inc(S("mats_in"), 16)
            sp.dma_start(cvec[:, :], cols).then_inc(S("cols_in"), 16)
            sp.dma_start(rvec[:, :, :], rows.unsqueeze(0)).then_inc(S("rows_in"), 16)
            sp.dma_start(eps_c[:, :], eps2.unsqueeze(0).to_broadcast([P, 1])).then_inc(S("eps_in"), 16)
            with nc.allow_non_contiguous_dma(reason="single integers"):
                sp.dma_start(nt_i[:, 0:NT - 1], node_type[0:(NT - 1) * P].rearrange("(i p) -> p i", p=P)).then_inc(S("nt_in"), 16)
                sp.dma_start(nt_i[0:LASTN, NT - 1:NT], node_type[(NT - 1) * P:N].unsqueeze(1)).then_inc(S("nt_in"), 16)

            def store(s, block_i):
                hold(sp, S("evacuated"), (block_i + 1) * UPB)
                sp.dma_start(adj[:, bass.ds(block_i, 1), :, :].rearrange("k o p n -> p (k o) n"),
                             stage[s].rearrange("p k i d -> p k (i d)").bitcast(u8)).then_inc(S("stored", s), 16)
            store(0, 0)
            with sp.Fori(0, NH - 1) as k:
                store(1, 2 * k + 1)
                store(0, 2 * k + 2)
            sp.wait_ge(S("stored", 0), 16 * NH)
            sp.wait_ge(S("stored", 1), 16 * NH)

            any_edges = read_flag(sp)
            with sp.If(any_edges > 0):
                table_init(sp, 0, S("ones_ready"), 1)
                any_edges_sync(sp, 0)
                for g in range(NG):
                    if g > 0:
                        sp.wait_ge(S("any_degree_taken"), g)
                    sp.dma_start(sums_n[:, 0:gw(g) // P, :], sums[g * GT * P:g * GT * P + gw(g), :]
                                 .rearrange("(i p) d -> p i d", p=P)).then_inc(S("any_degree_in"), 16)
                sp.wait_ge(S("any_degree_taken"), NG)
                table_init(sp, 1, S("ones_ready"), 1)
                any_edges_sync(sp, 1)
                with nc.allow_non_contiguous_dma(reason="one number per node"):
                    sp.dma_start(deg_out[:, :], sums[:, 0:1].rearrange("(i p) d -> p (i d)", p=P)).then_inc(S("any_outdegree_in"), 16)
                sp.wait_ge(S("any_outdegree_in"), 16)
            sp.nop()

            def load_sums(p, g, width, first):
                if not first:
                    hold(sp, S("chunk_used"), NC * (NG * p + g))
                sp.dma_start(sums_n[:, 0:width, :], sums[bass.ds(g * (GT * P), width * P), :]
                             .rearrange("(i p) d -> p i d", p=P)).then_inc(S("sums_in"), 16)

            def load(p, g, width, first=False):
                if isinstance(g, int) and g == 0:
                    with sp.If(any_edges > 0):
                        table_init(sp, 2 + p, S("parts_ready"), NG * (p + 1))
                        any_edges_sync(sp, 2 + p)
                    sp.nop()
                with sp.If(any_edges > 0):
                    load_sums(p, g, width, first)
                with sp.Else():
                    load_chunks(p, g, width, first)
                sp.nop()

            def load_chunks(p, g, width, first):
                for c in range(NC):
                    if not first:
                        hold(sp, S("chunk_used"), NC * (NG * p + g - 1) + c + 1)
                    sp.dma_start(ring[:, c, 0:width, :],
                                 adj[PASSES[p], bass.ds(GT * g, width), :, c * CI * P:(c + 1) * CI * P]
                                 .rearrange("b p n -> p b n")).then_inc(S("chunk_in", c), 16)
            for p in range(NPASS):
                if p == T + 1:
                    sp.wait_ge(S("proj_used"), NG * (T + 1))
                    sp.dma_start(wts[:, 0:len(LATE), :], mats[:, len(EARLY) * D:].rearrange("p (m d) -> p m d", d=D)
                                 ).then_inc(S("late_mats_in"), 16)
                load(p, 0, GT, first=(p == 0))
                with sp.Fori(1, NG - 1) as g:
                    load(p, g, GT)
                load(p, NG - 1, NT - GT * (NG - 1))

            for g in range(NG):
                sp.wait_ge(S("x_ready", 3), g + 1)
                if g < NG - 1:
                    sp.dma_start(out[g * GT * P:(g + 1) * GT * P, :].rearrange("(i p) d -> p i d", p=P),
                                 x_nm[:, GT * g:GT * (g + 1), :]).then_inc(S("out_stored"), 16)
                else:
                    sp.dma_start(out[(NT - 1) * P:N, :], x_nm[0:LASTN, NT - 1, :]).then_inc(S("out_stored"), 16)
            sp.wait_ge(S("out_stored"), 16 * NG)

        @block.gpsimd
        def _(pool):
            consts = S("consts")
            pool.memset(x_nm[:, NT - 1, :], 0.0).then_inc(consts, 1)
            pool.memset(nt_i[:, NT - 1:NT], 0).then_inc(consts, 1)
            pool.iota(bnd_i[:, :], pattern=[[P * WN, NH]], base=0, channel_multiplier=WN).then_inc(consts, 1)
            pool.memset(ones[:, :], 1.0).then_inc(consts, 1)
            pool.iota(iota_i, pattern=[[1, AC], [0, BW]], base=1, channel_multiplier=0).then_inc(consts, 1)
            pool.iota(probe_i[:, :], pattern=[[1, int(MAXCOUNT)]], base=1, channel_multiplier=0).then_inc(consts, 1)
            pool.memset(ones_h[:, :], 1.0).then_inc(consts, 1)
            pool.memset(ident[:, :], 0.0).then_inc(consts, 1)
            pool.wait_ge(consts, 8)
            pool.affine_select(out=ident[:, :], in_=ident[:, :], compare_op=ALU.not_equal, fill=1.0,
                               base=0, pattern=[[-1, P]], channel_multiplier=1).then_inc(consts, 1)
            for h in range(NH):
                pool.wait_ge(S("rows_found"), h // ROWS_AT_ONCE + 1)
                if h >= NR:
                    pool.wait_ge(S("row_counted"), h - NR + 1)
                pool.indirect_dma_start(out=rowg[:, h % NR, :], out_offset=None,
                                        in_=dst.rearrange("(r c) -> r c", c=HROW),
                                        in_offset=bass.IndirectOffsetOnAxis(ap=row_i[:, h:h + 1], axis=0)
                                        ).then_inc(S("row_in", h % NR), 16)
            with pool.Fori(0, NH) as h:
                hold(pool, S("index_ready"), h + 1)
                pool.indirect_dma_start(out=g3, out_offset=None, in_=edges,
                                        in_offset=bass.IndirectOffsetOnAxis(ap=next_i[:, 0:1], axis=0)
                                        ).then_inc(S("edges_in"), 16)
            any_edges = read_flag(pool)
            with pool.If(any_edges > 0):
                pool.memset(zeros, 0.0).then_inc(S("zeros_ready"), 1)
                pool.memset(c_tri, 1.0).then_inc(S("tri_ready"), 1)
                pool.wait_ge(S("tri_ready"), 1)
                pool.affine_select(out=c_tri, in_=c_tri, compare_op=ALU.is_gt, fill=0.0, base=0,
                                   pattern=[[-1, CH]], channel_multiplier=1).then_inc(S("tri_ready"), 1)
                any_edges_pool(pool, 0, 0, 1)
                any_edges_pool(pool, 1, 1, 0)
                for p in range(NPASS):
                    any_edges_pool(pool, 2 + p, 0, 1)
            pool.nop()

        @block.scalar
        def _(act):
            act.sem_inc(S("stored", 1), 16)

            def evacuate(s, block_i, u):
                hold(act, S("counts_ready"), block_i * UPB + u + 1)
                act.activation(
                    stage[s].rearrange("p k i d -> p (k i) d").bitcast(i16)[:, :, u * UW:(u + 1) * UW].rearrange("p c (b w) -> p b w c", w=2),
                    ps[:, banks_of(u):banks_of(u) + UW // 2, 0:2 * AC].rearrange("p b (w c) -> p b w c", w=2),
                    ACT.Copy).then_inc(S("evacuated"), 1)

            def copy_degree(h):
                act.wait_ge(S("degree_ready"), h + 1)
                act.activation(deg_pairs[:, bass.ds(h * (2 * P), 2 * P)], bank(MISC, 2 * P),
                               ACT.Copy).then_inc(S("degree_copied"), 1)

            def block_of(s, block_i, stored_before, pair=None):
                if stored_before is not None:
                    act.wait_ge(S("stored", s), stored_before)
                for u in range(UPB):
                    evacuate(s, block_i, u)
                    if u == 5 and pair is not None:
                        copy_degree(pair)
            block_of(0, 0, None, 0)
            with act.Fori(0, NH - 1) as k:
                block_of(1, 2 * k + 1, 16 * k + 16)
                block_of(0, 2 * k + 2, 16 * k + 16, k + 1)

            act.wait_ge(S("degree_inverse"), 1)
            act.activation(deg_out[:, :], deg_out[:, :], ACT.Sqrt).then_inc(S("degree_norm"), 1)

            def split(p, source):
                if p > 0:
                    wait_sums(act, p - 1, NG - 1)
                for j in range(NG):
                    src = source(j)
                    act.activation(nodes(parts[:, 0], j), src, ACT.Copy, scale=scale_of(p)[0]).then_inc(S("hi_ready"), 1)

            def of_tmp(p):
                def source(j):
                    act.wait_ge(S("src_ready", p), j + 1)
                    return tmp[:, j % 2, 0:gw(j)]
                return source

            def of_x(layer):
                def source(j):
                    act.wait_ge(S("x_ready", layer), j + 1)
                    return nodes(x_nm, j)
                return source

            def of_message(p):
                def source(j):
                    m = tmp[:, j % 2, 0:gw(j)]
                    act.wait_ge(S("bias_added"), j + 1 + NG * (p - 1))
                    act.activation(m, m, ACT.Relu).then_inc(S("src_ready", p), 1)
                    act.wait_ge(S("src_ready", p), j + 1)
                    return m
                return source

            def relu_x(g, b, w):
                act.activation(tmp[:, b, 0:w], xT[:, bass.ds(g * (GT * P), w)], ACT.Relu).then_inc(S("self_ready"), 1)

            def of_psum(p, func):
                def source(j):
                    act.wait_ge(S("src_in_psum"), j + 1 + NG * T)
                    if j >= 2:
                        act.wait_ge(S("parts_ready"), j - 1 + NG * p)
                    act.activation(tmp[:, j % 2, 0:gw(j)], bank(SRC[j % 2], gw(j)), func).then_inc(S("src_ready", p), 1)
                    act.wait_ge(S("src_ready", p), j + 1)
                    return tmp[:, j % 2, 0:gw(j)]
                return source

            def copy_aggregates(p, first=None, then=None):
                def one(g, b, w):
                    if not isinstance(g, int) or g > 0:
                        act.wait_ge(S("proj_done"), g + NG * p)
                    if first:
                        first(g, b, w)
                    wait_sums(act, p, g)
                    act.activation(agg_s[:, 0:w], bank(AGG[b], w), ACT.Copy, scale=scale_of(p)[1]).then_inc(S("agg_copied"), 1)
                in_turns(act, one, then)

            def to_feat(p, to, func, bias, unscale=1.0):
                def one(g, b, w):
                    act.wait_ge(S("proj_done"), g + 1 + NG * p)
                    if to is None:
                        if not isinstance(g, int) or g >= 2:
                            act.wait_ge(S("h_in_psum", 3), g - 1)
                        dest = tmp[:, b, 0:w]
                    else:
                        dest = to[:, bass.ds(g * (GT * P), w)]
                    act.activation(dest, bank(PROJ, w), func, bias=bias, scale=unscale).then_inc(S("proj_used"), 1)
                in_turns(act, one)

            def std(v, kind, n, count=1):
                act.wait_ge(S(f"{kind}_var_ready", n), count)
                act.activation(v, v, ACT.Sqrt).then_inc(S(f"{kind}_std_ready", n), 1)

            def bn_std(n):
                std(bn_a[:, 1:2], "bn", n)

            def bn_relu(n):
                bn_std(n)
                act.wait_ge(S("bn_ready"), n + 1)
                for g in range(NG):
                    act.activation(hT[:, cols_of(g)], hT[:, cols_of(g)], ACT.Relu, bias=bn_a[:, 5:6],
                                   scale=bn_a[:, 4:5]).then_inc(S("relu_done"), 1)

            def copy_xT(layer, by_group):
                if not by_group:
                    std(mv[:, :, 1], "ln", layer)
                for s in range(NG + 2):
                    if by_group and s < NG:
                        std(mv[:, GT * s:GT * s + len(tiles_of(s)), 1], "ln", layer, s + 1)
                    if s >= 2:
                        g = s - 2
                        act.wait_ge(S("xT_in_psum"), g + 1 + NG * layer)
                        act.activation(xT[:, cols_of(g)], bank(XT[g % 2], gw(g)), ACT.Copy).then_inc(S("xT_ready"), 1)

            act.wait_ge(S("cols_in"), 16)
            split(0, of_tmp(0))

            def degree_and_norms():
                act.wait_ge(S("degree_inverse"), 2)
                act.activation(z_row, deg_row[:, :], ACT.Sqrt).then_inc(S("degree_norm"), 1)
                act.wait_ge(S("norms_ready"), 1)
                act.activation(bound[:, 1:1 + T], bound[:, 1:1 + T], ACT.Sqrt).then_inc(S("norms_rooted"), 1)
            copy_aggregates(0, then=degree_and_norms)
            bn_relu(0)
            copy_xT(0, True)
            for t in range(T):
                split(1 + t, of_message(1 + t))
                if t == 0:
                    act.wait_ge(S("xT_ready"), NG)
                    act.wait_ge(S("parts_ready"), NG * 2)
                copy_aggregates(1 + t, relu_x if t == 0 else None)
            copy_xT(1, False)
            split(4, of_x(1))
            to_feat(4, hT, ACT.Identity, cvec[:, COL["b1"]:COL["b1"] + 1], unscale=scale_of(4)[1])
            bn_relu(1)
            for g in range(NG):
                act.wait_ge(S("lin2_done"), g + 1)
                act.activation(hT[:, cols_of(g)], bank(SRC[g % 2], gw(g)), ACT.Identity,
                               bias=cvec[:, COL["b2"]:COL["b2"] + 1]).then_inc(S("h2_ready"), 1)
            bn_relu(2)
            copy_xT(2, True)
            act.wait_ge(S("norms_ready"), 2)
            act.activation(bound[:, 1:3], bound[:, 1:3], ACT.Sqrt).then_inc(S("norms_rooted"), 1)
            split(5, of_x(2))
            to_feat(5, hT, ACT.Relu, cvec[:, COL["f_lb"]:COL["f_lb"] + 1])
            split(6, of_psum(6, ACT.Copy))
            act.wait_ge(S("bias_ready"), 1)
            to_feat(6, None, ACT.Relu, bn_a[:, 6:7])
            std(mv[:, :, 1], "ln", 3)

        @block.vector
        def _(dve):
            ch = Chain(dve, S("vector_steps"))
            link = ch.link

            dve.wait_ge(S("consts"), 9)
            dve.tensor_copy(iota_r, iota_i)
            dve.tensor_copy(probe[:, :], probe_i[:, :]).then_inc(S("probe_ready"), 1)
            link(dve.tensor_copy(bnd[:, :], bnd_i[:, :]))
            def power_of_two(k):
                b, sc, inv = bound[:, 0:1], scale[:, k, 0:1], scale[:, k, 1:2]
                link(dve.tensor_scalar(b, b, 2.0 ** -80, None, op0=ALU.max))
                link(dve.tensor_scalar(inv.bitcast(i32), b.bitcast(i32), 0x7F800000, None, op0=ALU.bitwise_and))
                link(dve.tensor_scalar(sc.bitcast(i32), inv.bitcast(i32), -1.0, float(254 << 23), op0=ALU.mult, op1=ALU.add))
                link(dve.tensor_scalar(sc, sc, 2.0 ** 14, None, op0=ALU.mult))
                link(dve.tensor_scalar(inv, inv, 2.0 ** -14 / BYTE, None, op0=ALU.mult))

            dve.wait_ge(S("heads_in"), 16)
            dve.tensor_copy(head_f, head_i).then_inc(S("heads_ready"), 1)
            dve.wait_ge(S("heads_spread"), 1)
            for h0 in range(0, NH, ROWS_AT_ONCE):
                c = slice(h0, min(h0 + ROWS_AT_ONCE, NH))
                for h in range(c.start, c.stop):
                    link(dve.tensor_scalar(junk[:, 0:HEADS], bank(MISC, HEADS), bnd[:, h:h + 1], 0.0,
                                           op0=ALU.is_lt, op1=ALU.add, accum_out=cnt[:, h:h + 1]))
                link(dve.tensor_scalar(row_f[:, c], cnt[:, c], -1.0, 0.0, op0=ALU.add, op1=ALU.max))
                dve.tensor_copy(row_i[:, c], row_f[:, c]).then_inc(S("rows_found"), 1)

            dve.wait_ge(S("x_in"), 32)
            dve.tensor_reduce(bound[:, 1:2], x_nm[:, :, :].rearrange("p i d -> p (i d)"), axis=AX.X, op=ALU.max,
                              apply_absolute_value=True).then_inc(S("xmax_ready"), 1)
            dve.wait_ge(S("xmax_turned"), 1)
            dve.tensor_reduce(bound[0:1, 2:3], bank(0, P)[0:1, :], axis=AX.X, op=ALU.max).then_inc(S("xmax_ready"), 1)
            dve.wait_ge(S("xmax_spread"), 1)
            link(dve.tensor_copy(bound[:, 0:1], bank(1, 1)))
            power_of_two(0)
            for h in range(NH):
                dve.wait_ge(S("row_in", h % NR), 16 * (h // NR + 1))
                dve.tensor_scalar(junk, rowg[:, h % NR, :], bnd[:, h:h + 1], 0.0, op0=ALU.is_lt, op1=ALU.add,
                                  accum_out=cnt2[:, h:h + 1]).then_inc(S("row_counted"), 1)
                dve.wait_ge(S("row_counted"), h + 1)
            link(dve.scalar_tensor_tensor(cnt[:, :], row_f[:, :], float(HROW), cnt2[:, :], op0=ALU.mult, op1=ALU.add))
            dve.memset(start_i[:, NH:NH + 1], 0)
            link(dve.tensor_scalar(start_i[:, 0:NH], cnt[:, :], float(E - WE), None, op0=ALU.min))
            dve.wait_ge(S("probe_done"), 1)
            link(dve.scalar_tensor_tensor(probe_f[:, :], probe_i[:, :], float(P * BYTE), bank(DEG_BANK, int(MAXCOUNT)),
                                          op0=ALU.mult, op1=ALU.not_equal))
            dve.tensor_reduce(bound[:, 7:8], probe_f[:, :], axis=AX.X, op=ALU.max).then_inc(S("probe_done"), 1)
            link(dve.memset(deg_acc[:, :], 0.0))
            link(dve.memset(deg_max[:, :], 0.0))
            dve.tensor_copy(next_i[:, :], start_i[:, 0:1]).then_inc(S("index_ready"), 1)

            def window_keys(h, last=False):
                dve.wait_ge(S("edges_in"), 16 * h + 16)
                dve.tensor_scalar(lo_i.bitcast(i32), g3v[:, 0, :], P - 1, None, op0=ALU.bitwise_and)
                dve.tensor_scalar(hi_i.bitcast(i32), g3v[:, 0, :], 7, None, op0=ALU.logical_shift_right)
                link(dve.tensor_scalar(dl, g3v[:, 1, :], bnd[:, bass.ds(h, 1)], None, op0=ALU.subtract))
                dve.tensor_scalar(kw[:, 0, :], lo_i.bitcast(i32), 1.0, None, op0=ALU.add)
                dve.tensor_scalar(ge0, dl, 0.0, None, op0=ALU.is_ge)
                link(dve.scalar_tensor_tensor(key, g3v[:, 2, :], float(NT), hi_i.bitcast(i32), op0=ALU.mult, op1=ALU.add))
                link(dve.scalar_tensor_tensor(valid, dl, float(WN - 1), ge0, op0=ALU.is_le, op1=ALU.mult))
                link(dve.tensor_tensor(dl, dl, valid, ALU.mult))
                dve.scalar_tensor_tensor(kw[:, 0, :], dl, 2.0 * P, kw[:, 0, :], op0=ALU.mult, op1=ALU.add)
                dve.scalar_tensor_tensor(kw[:, 2, :], hi_i.bitcast(i32), 1.0, valid, op0=ALU.add, op1=ALU.mult)
                dve.scalar_tensor_tensor(kw[:, 1, :], key, 1.0, valid, op0=ALU.add, op1=ALU.mult).then_inc(S("keys_ready"), 1)

            def next_gather(h):
                dve.wait_ge(S("keys_ready"), h)
                dve.tensor_copy(next_i[:, :], start_i[:, bass.ds(h, 1)]).then_inc(S("index_ready"), 1)

            def take_keys(h):
                dve.wait_ge(S("keys_in_psum"), h + 1)
                link(dve.tensor_scalar(key_d, bank(MISC, P), 2.0 * P, None, op0=ALU.is_ge))
                dve.tensor_scalar(keysT[:, 3, :], key_d, FIELD - 1.0, 1.0, op0=ALU.mult, op1=ALU.add)
                dve.scalar_tensor_tensor(keysT[:, 2, :], key_d, -2.0 * P, bank(MISC, P), op0=ALU.mult, op1=ALU.add)
                dve.scalar_tensor_tensor(to_dst[:, :, 0], bank(MISC)[:, 2 * P:3 * P], 1.0, key_d, op0=ALU.is_ge, op1=ALU.subtract)
                dve.tensor_copy(to_dst[:, :, 1], key_d)
                dve.tensor_copy(keysT[:, 0:2, :], bank(MISC)[:, P:3 * P].rearrange("p (a w) -> p a w", a=2)).then_inc(S("keys_taken"), 1)
                dve.wait_ge(S("keys_taken"), h + 1)

            def onehots(block_i, half, b):
                s = b % 2
                B = NB * block_i + b
                if not (isinstance(B, int) and B < 2):
                    dve.wait_ge(S("onehots_used"), B - 1)
                w = half * SBW + b * BW
                def columns(c0, c1):
                    return onehot[:, s, c0:c1].rearrange("p (c w) -> p c w", w=BW)

                def key(a, c0, c1):
                    return keysT[:, a, w:w + BW].unsqueeze(1).to_broadcast([P, (c1 - c0) // BW, BW])
                for a, c0, c1 in ((2, OH_A, OH_L), (0, 0, OH_T), (1, OH_T, OH_A)):
                    dve.tensor_tensor(columns(c0, c1), iota_r[:, 0:c1 - c0].rearrange("p (c w) -> p c w", w=BW),
                                      key(a, c0, c1), ALU.is_equal).then_inc(S("onehot_steps"), 1)
                dve.wait_ge(S("onehot_steps"), 3 * B + 1)
                ins = dve.tensor_tensor(columns(OH_A, OH_L), columns(OH_A, OH_L), key(3, OH_A, OH_L), ALU.mult)
                ins.then_inc(S("onehots_ready"), 1)

            def take_outdegrees(block_i, step):
                dve.wait_ge(S("onehots_used"), NB * (block_i + 1))
                step(dve.tensor_copy(deg_i, bank(DEG_BANK, NT)))
                step(dve.tensor_scalar(deg_i, deg_i, 8, None, op0=ALU.logical_shift_right))
                step(dve.scalar_tensor_tensor(deg_b, deg_i, 1.0 - FIELD, bank(DEG_BANK, NT), op0=ALU.mult, op1=ALU.add))
                dve.tensor_tensor(deg_acc[:, :], deg_acc[:, :], deg_b, ALU.add)
                dve.tensor_tensor(deg_max[:, :], deg_max[:, :], deg_b, ALU.max).then_inc(S("outdegrees_taken"), 1)
                dve.wait_ge(S("outdegrees_taken"), block_i + 1)

            window_keys(0)
            next_gather(1)
            take_keys(0)
            for b in range(NB):
                onehots(0, 0, b)
            with dve.Fori(0, NH - 1) as k:
                ch.enter(k, 11)
                for b in range(NB):
                    onehots(2 * k + 1, 1, b)
                    if b == 0:
                        take_outdegrees(2 * k, link)
                    if b == 1:
                        window_keys(k + 1)
                dve.wait_ge(S("onehots_ready"), NB * (2 * k + 2))
                take_keys(k + 1)
                for b in range(NB):
                    onehots(2 * k + 2, 0, b)
                    if b == 0:
                        take_outdegrees(2 * k + 1, link)
                    if b == 1:
                        next_gather(k + 2)
                ch.leave(NH - 1)
            take_outdegrees(NT - 1, link)

            dve.tensor_copy(deg_out[:, :], deg_acc[:, :])
            dve.tensor_reduce(bound[:, 1:2], deg_acc, axis=AX.X, op=ALU.add)
            link(dve.tensor_reduce(bound[:, 2:3], deg_max, axis=AX.X, op=ALU.max))
            link(dve.tensor_scalar(bound[:, 2:3], bound[:, 2:3], MAXCOUNT, None, op0=ALU.is_gt))
            dve.tensor_tensor(bound[:, 2:3], bound[:, 2:3], bound[:, 7:8], ALU.add).then_inc(S("holds_counted"), 1)
            dve.wait_ge(S("holds_summed"), 1)
            link(dve.tensor_copy(bound[0:1, 4:6], bank(DEG_BANK, 2)[0:1, :]))
            link(dve.tensor_scalar(bound[0:1, 4:5], bound[0:1, 4:5], float(E), None, op0=ALU.not_equal))
            link(dve.tensor_tensor(bound[0:1, 4:5], bound[0:1, 4:5], bound[0:1, 5:6], ALU.add))
            dve.tensor_scalar(flag[0:1, 0:1], bound[0:1, 4:5], 1.0, None, op0=ALU.min).then_inc(S("flag_ready"), 1)
            dve.wait_ge(S("degree_copied"), NH)
            any_edges = read_flag(dve)
            ach = Chain(dve, S("any_steps"))
            with dve.If(any_edges > 0):
                dve.memset(parts[:, 0], 1.0)
                dve.memset(parts[:, 1], 0.0).then_inc(S("ones_ready"), 1)
                dve.wait_ge(S("tri_ready"), 2)
                any_edges_vector(dve, ach, 0, ALL, 1)
                for g in range(NG):
                    dve.wait_ge(S("any_degree_turned"), g + 1)
                    dve.tensor_scalar(deg_row[:, cols_of(g)], bank(AGG[0], gw(g)), 1.0 / BYTE, None, op0=ALU.mult).then_inc(S("any_degree_taken"), 1)
                any_edges_vector(dve, ach, 1, ALL, 0)
                dve.wait_ge(S("any_outdegree_in"), 16)
                ach.link(dve.tensor_scalar(deg_out[:, :], deg_out[:, :], 1.0 / BYTE, None, op0=ALU.mult))
                dve.wait_ge(S("any_degree_taken"), NG)
            dve.nop()
            link(dve.tensor_scalar(deg_out[:, :], deg_out[:, :], 1.0, None, op0=ALU.max))
            dve.reciprocal(deg_out[:, :], deg_out[:, :]).then_inc(S("degree_inverse"), 1)
            dve.wait_ge(S("nt_in"), 32)
            for t in range(T):
                link(dve.tensor_scalar(nt_m[:, t, :], nt_i[:, :], float(t), None, op0=ALU.is_equal))

            def subtract(p, source):
                for j in range(NG):
                    src = source(j)
                    dve.wait_ge(S("hi_ready"), j + 1 + NG * p)
                    dve.scalar_tensor_tensor(nodes(parts[:, 1], j), src, scale_of(p)[0], nodes(parts[:, 0], j),
                                             op0=ALU.mult, op1=ALU.subtract).then_inc(S("parts_ready"), 1)
                any_sums(p)

            def of_tmp(p):
                def source(j):
                    dve.wait_ge(S("src_ready", p), j + 1)
                    return tmp[:, j % 2, 0:gw(j)]
                return source

            def scaled(j):
                def scale_x(j):
                    for n, i in enumerate(tiles_of(j)):
                        ins = dve.tensor_scalar(tmp[:, j % 2, n * P:(n + 1) * P], x_nm[:, i, :], deg_out[:, i:i + 1], None, op0=ALU.mult)
                    ins.then_inc(S("src_ready", 0), 1)
                if j == 0:
                    scale_x(0)
                if j + 1 < NG:
                    if j > 0:
                        dve.wait_ge(S("parts_ready"), j)
                    scale_x(j + 1)
                dve.wait_ge(S("src_ready", 0), j + 1)
                return tmp[:, j % 2, 0:gw(j)]

            def stats_of(k, g, w):
                n = w if not isinstance(g, int) or g < NG - 1 else N - (NG - 1) * GT * P
                dve.bn_stats(stats[:, bass.ds(g, 1), :].rearrange("p o s -> p (o s)"),
                             hT[:, bass.ds(g * (GT * P), n)]).then_inc(S("stats_done", k), 1)

            def bn_scale(n, gamma, beta):
                dve.wait_ge(S("stats_done", n), NG)
                link(dve.bn_aggr(bn_a[:, 0:2], stats[:, 0:NG, :].rearrange("p g s -> p (g s)")))
                dve.tensor_scalar(bn_a[:, 1:2], bn_a[:, 1:2], BN_EPS, None, op0=ALU.add).then_inc(S("bn_var_ready", n), 1)
                dve.wait_ge(S("bn_std_ready", n), 1)
                link(dve.reciprocal(bn_a[:, 1:2], bn_a[:, 1:2]))
                link(dve.tensor_tensor(bn_a[:, 4:5], bn_a[:, 1:2], cvec[:, COL[gamma]:COL[gamma] + 1], ALU.mult))
                link(dve.tensor_tensor(bn_a[:, 3:4], bn_a[:, 0:1], bn_a[:, 4:5], ALU.mult))
                dve.tensor_tensor(bn_a[:, 5:6], cvec[:, COL[beta]:COL[beta] + 1], bn_a[:, 3:4], ALU.subtract).then_inc(S("bn_ready"), 1)

            def apart():
                dve.sem_inc(S("vector_holds"), 1)

            def tile(buf, i):
                return buf[:, i, :] if isinstance(i, int) else buf[:, bass.ds(i, 1), :].rearrange("p o d -> p (o d)")

            def node_stats(y, to, width):
                for n in range(width // P):
                    ins = dve.bn_stats(stats[:, n, :], y(n))
                link(ins)
                apart()
                for n in range(width // P):
                    ins = dve.bn_aggr(to(n), stats[:, n, :])
                link(ins)

            def normalize(layer, g):
                for i in tiles_of(g):
                    ins = dve.tensor_scalar(x_nm[:, i, :], x_nm[:, i, :], mv[:, i, 0:1], mv[:, i, 1:2],
                                            op0=ALU.subtract, op1=ALU.mult)
                ins.then_inc(S("x_ready", layer), 1)

            def layer_norm_by_group(layer, y):
                for s in range(NG + 1):
                    if s < NG:
                        y(s)
                    if s > 0:
                        v = mv[:, GT * (s - 1):GT * (s - 1) + len(tiles_of(s - 1)), 1]
                        dve.wait_ge(S("ln_std_ready", layer), s)
                        dve.reciprocal(v, v).then_inc(S("inverse_ready"), 1)
                    if s < NG:
                        dve.wait_ge(S("h_taken", layer), s + 1)
                        for n, i in enumerate(tiles_of(s)):
                            ins = dve.bn_stats(stats[:, n, :], x_nm[:, i, :])
                        ins.then_inc(S("node_stats_done"), 1)
                    if s > 0:
                        dve.wait_ge(S("inverse_ready"), s + NG * (layer // 2))
                        normalize(layer, s - 1)
                    if s < NG:
                        dve.wait_ge(S("node_stats_done"), s + 1 + NG * (layer // 2))
                        for n, i in enumerate(tiles_of(s)):
                            ins = dve.bn_aggr(mv[:, i, :], stats[:, n, :])
                        link(ins)
                        v = mv[:, GT * s:GT * s + len(tiles_of(s)), 1]
                        dve.tensor_scalar(v, v, LN_EPS, None, op0=ALU.add).then_inc(S("ln_var_ready", layer), 1)
                dve.wait_ge(S("x_ready", layer), NG)

            def layer_norm(layer):
                dve.tensor_scalar(mv[:, :, 1], mv[:, :, 1], LN_EPS, None, op0=ALU.add).then_inc(S("ln_var_ready", layer), 1)
                dve.wait_ge(S("ln_std_ready", layer), 1)
                link(dve.reciprocal(mv[:, :, 1], mv[:, :, 1]))
                for g in range(NG):
                    normalize(layer, g)
                dve.wait_ge(S("x_ready", layer), NG)

            def plus_transposed(layer, times):
                def y(g):
                    dve.wait_ge(S("h_in_psum", layer), g + 1)
                    dve.scalar_tensor_tensor(nodes(x_nm, g), nodes(x_nm, g), times, bank(TR[g % 2], gw(g)),
                                             op0=ALU.mult, op1=ALU.add).then_inc(S("h_taken", layer), 1)
                return y

            def any_sums(p):
                with dve.If(any_edges > 0):
                    any_edges_vector(dve, ach, 2 + p, PASSES[p], 1)
                dve.nop()

            dve.wait_ge(S("mats_in"), 16)
            we = wts[:, MAT["We0"]:MAT["We0"] + T, :].rearrange("p m d -> p (m d)")
            dve.tensor_tensor(square, we, we, ALU.mult).then_inc(S("squares_ready"), 1)
            dve.wait_ge(S("biases_spread"), 1)
            for n in range(2):
                ins = dve.tensor_copy(bias_b[:, n, :], bank(XT[n], T * D))
            ins.then_inc(S("biases_taken"), 1)
            dve.wait_ge(S("degree_norm"), 1)
            subtract(0, scaled)
            link(dve.tensor_scalar(deg_row[:, :], deg_row[:, :], 1.0, None, op0=ALU.max))
            dve.reciprocal(deg_row[:, :], deg_row[:, :]).then_inc(S("degree_inverse"), 1)

            dve.wait_ge(S("squares_summed"), 1)
            dve.wait_ge(S("biases_taken"), 1)
            link(dve.tensor_reduce(bound[:, 1:1 + T], bank(TR[0], T * D).rearrange("p (t d) -> p t d", t=T), axis=AX.X, op=ALU.max))
            link(dve.tensor_reduce(bound[:, 4:4 + T], bias_b[:, 0, :].rearrange("p (t d) -> p t d", t=T), axis=AX.X,
                                   op=ALU.max, apply_absolute_value=True))
            dve.sem_inc(S("norms_ready"), 1)
            dve.wait_ge(S("norms_rooted"), 1)
            for t in range(T):
                link(dve.scalar_tensor_tensor(bound[:, 0:1], bound[:, 1 + t:2 + t], XMAX, bound[:, 4 + t:5 + t],
                                              op0=ALU.mult, op1=ALU.add))
                power_of_two(1 + t)
            dve.wait_ge(S("degree_norm"), 2)
            dve.wait_ge(S("cols_in"), 16)

            def layer0_h(g, b, w):
                dve.wait_ge(S("proj_done"), g + 1)
                c = bass.ds(g * (GT * P), w)
                dve.tensor_tensor(hT[:, c], bank(PROJ, w), z_row[:, c], ALU.mult).then_inc(S("proj_used"), 1)
                dve.wait_ge(S("proj_used"), g + 1)
                dve.tensor_scalar(hT[:, c], hT[:, c], cvec[:, 0:1], None, op0=ALU.add).then_inc(S("h_ready", 0), 1)
                dve.wait_ge(S("h_ready", 0), g + 1)
                stats_of(0, g, w)
            in_turns(dve, layer0_h)
            bn_scale(0, "gamma", "beta")
            layer_norm_by_group(0, plus_transposed(0, 2.0))

            def update(g, width, first):
                terms = [(t, b) for b in ([True] if first else []) + [False] for t in range(T)]
                for k, (t, is_bias) in enumerate(terms):
                    for n in range(width // P):
                        i = GT * g + n if isinstance(g, int) else g * GT + n
                        m = nt_m[:, t, i:i + 1] if isinstance(i, int) else nt_m[:, t, bass.ds(i, 1)]
                        part = bias_b[:, 1, t * D:(t + 1) * D] if is_bias else ps[:, PROJ + n, t * D:(t + 1) * D]
                        if first and k == 0:
                            ins = dve.tensor_scalar(tile(z, i), part, m, None, op0=ALU.mult)
                        else:
                            ins = dve.scalar_tensor_tensor(tile(z, i), part, m, tile(z, i), op0=ALU.mult, op1=ALU.add)
                    if k < len(terms) - 1:
                        link(ins)
                ins.then_inc(S("proj_used"), 1)

            def message(t):
                def add_bias(j):
                    n = gw(j) // P
                    dve.wait_ge(S("src_in_psum"), j + 1 + NG * t)
                    dve.tensor_tensor(tmp[:, j % 2, 0:gw(j)].rearrange("p (n d) -> p n d", d=D),
                                      bank(SRC[j % 2], gw(j)).rearrange("p (n d) -> p n d", d=D),
                                      bias_b[:, 0, t * D:(t + 1) * D].unsqueeze(1).to_broadcast([P, n, D]),
                                      ALU.add).then_inc(S("bias_added"), 1)

                def source(j):
                    if j == 0:
                        add_bias(0)
                    if j + 1 < NG:
                        if j > 0:
                            dve.wait_ge(S("parts_ready"), NG * (1 + t) + j)
                        add_bias(j + 1)
                    dve.wait_ge(S("src_ready", 1 + t), j + 1)
                    return tmp[:, j % 2, 0:gw(j)]
                return source

            for t in range(T):
                subtract(1 + t, message(t))

                def take(g, b, w):
                    dve.wait_ge(S("proj_done"), g + 1 + NG * (1 + t))
                    update(g, w, t == 0)
                    if t == T - 1:
                        c = slice(GT * g, GT * g + w // P) if isinstance(g, int) else bass.ds(g * GT, w // P)
                        dve.wait_ge(S("proj_used"), g + 1 + NG * (1 + t))
                        x_g, z_g = (v[:, c, :].rearrange("p i d -> p (i d)") for v in (x_nm, z))
                        y = tmp[:, b, 0:w]
                        link(dve.scalar_tensor_tensor(y, x_g, 2.0, z_g, op0=ALU.mult, op1=ALU.add))
                        apart()
                        dve.tensor_copy(x_g, y)
                        node_stats(lambda n: tmp[:, b, n * P:(n + 1) * P], lambda n: mv_g[:, n, :], w)
                        link(dve.tensor_copy(mv[:, c, :], mv_g[:, 0:w // P, :]))
                take(0, 0, GT * P)
                take(1, 1, GT * P)
                with dve.Fori(0, (NG - 3) // 2) as k:
                    ch.enter(k, 2 * {0: 2 * T - 1, T - 1: T - 1 + 4}.get(t, T - 1))
                    take(2 * k + 2, 0, GT * P)
                    take(2 * k + 3, 1, GT * P)
                    ch.leave((NG - 3) // 2)
                take(NG - 1, 0, gw(NG - 1))
                dve.wait_ge(S("proj_used"), NG * (t + 2))

            layer_norm(1)

            def of_x(j):
                return nodes(x_nm, j)
            dve.wait_ge(S("eps_in"), 16)
            link(dve.tensor_scalar(bn_a[:, 7:8], eps_c[:, :], 1.0, X_SCALE * BYTE, op0=ALU.add, op1=ALU.mult))
            subtract(4, of_x)

            def plus_self(g, b, w):
                wait_sums(dve, 4, g)
                if not isinstance(g, int) or g > 0:
                    dve.wait_ge(S("proj_done"), g + NG * 4)
                dve.scalar_tensor_tensor(agg_s[:, 0:w], xT[:, bass.ds(g * (GT * P), w)], bn_a[:, 7:8], bank(AGG[b], w),
                                         op0=ALU.mult, op1=ALU.add).then_inc(S("agg_copied"), 1)

            def layer2(g, b, w):
                plus_self(g, b, w)
                if isinstance(g, int) and g == 0:
                    return
                dve.wait_ge(S("proj_used"), g + NG * 4)
                stats_of(1, g - 1, GT * P)
            dve.wait_ge(S("xT_ready"), NG * 2)
            in_turns(dve, layer2)
            dve.wait_ge(S("proj_used"), NG * 5)
            stats_of(1, NG - 1, gw(NG - 1))
            bn_scale(1, "g1", "beta1")
            for g in range(NG):
                dve.wait_ge(S("h2_ready"), g + 1)
                stats_of(2, g, gw(g))
            bn_scale(2, "g2", "beta2")
            layer_norm_by_group(2, plus_transposed(2, 1.0))

            fl, fr = wts[:, MAT["f_lw"], :], wts[:, MAT["f_rw"], :]
            dve.wait_ge(S("late_mats_in"), 16)
            dve.tensor_tensor(square_l[:, 0:D], fl, fl, ALU.mult)
            lb = cvec[:, COL["f_lb"]:COL["f_lb"] + 1]
            dve.scalar_tensor_tensor(square_l[:, 2 * D:2 * D + 1], lb, -1.0, lb, op0=ALU.mult, op1=ALU.max)
            dve.tensor_tensor(square_l[:, D:2 * D], fr, fr, ALU.mult).then_inc(S("squares_ready"), 1)
            dve.wait_ge(S("squares_summed"), 2)
            link(dve.tensor_reduce(bound[:, 1:3], bank(PROJ, 2 * D).rearrange("p (t d) -> p t d", t=2), axis=AX.X, op=ALU.max))
            link(dve.tensor_copy(bound[:, 4:5], bank(PROJ)[:, 2 * D:2 * D + 1]))
            dve.sem_inc(S("norms_ready"), 1)
            dve.wait_ge(S("norms_rooted"), 2)
            for n in range(2):
                link(dve.scalar_tensor_tensor(bound[:, 4:5], bound[:, 1 + n:2 + n], XMAX, bound[:, 4:5], op0=ALU.mult, op1=ALU.add))
            link(dve.tensor_copy(bound[:, 0:1], bound[:, 4:5]))
            power_of_two(T + 1)
            dve.tensor_tensor(bn_a[:, 6:7], cvec[:, COL["n_lb"]:COL["n_lb"] + 1], cvec[:, COL["fc_b"]:COL["fc_b"] + 1], ALU.add).then_inc(S("bias_ready"), 1)
            for p in (5, 6):
                subtract(p, of_x if p == 5 else of_tmp(p))

                def mean(g, b, w):
                    wait_sums(dve, p, g)
                    if not isinstance(g, int) or g > 0:
                        dve.wait_ge(S("proj_done"), g + NG * p)
                    dve.scalar_tensor_tensor(agg_s[:, 0:w], bank(AGG[b], w), scale_of(p)[1],
                                             deg_row[:, bass.ds(g * (GT * P), w)],
                                             op0=ALU.mult, op1=ALU.mult).then_inc(S("agg_copied"), 1)

                def result(g, b, w):
                    dve.wait_ge(S("h_in_psum", 3), g + 1)
                    c = slice(GT * g, GT * g + w // P) if isinstance(g, int) else bass.ds(g * GT, w // P)
                    x_g = x_nm[:, c, :].rearrange("p i d -> p (i d)")
                    y = z_row[:, b * GT * P:b * GT * P + w]
                    dve.tensor_tensor(y, x_g, bank(TR[b], w), ALU.add).then_inc(S("h_taken", 3), 1)
                    dve.wait_ge(S("h_taken", 3), g + 3)
                    apart()
                    dve.tensor_copy(x_g, y)
                    node_stats(lambda n: y[:, n * P:(n + 1) * P], lambda n: mv_g[:, n, :], w)
                    link(dve.tensor_copy(mv[:, c, :], mv_g[:, 0:w // P, :]))
                if p == 5:
                    in_turns(dve, mean)
            dve.sem_inc(S("h_taken", 3), 2)
            mean(0, 0, GT * P)
            mean(1, 1, GT * P)
            with dve.Fori(0, (NG - 3) // 2) as k:
                ch.enter(k, 2 * 3)
                mean(2 * k + 2, 0, GT * P)
                result(2 * k, 0, GT * P)
                mean(2 * k + 3, 1, GT * P)
                result(2 * k + 1, 1, GT * P)
                ch.leave((NG - 3) // 2)
            mean(NG - 1, 0, gw(NG - 1))
            for g in (NG - 3, NG - 2, NG - 1):
                result(g, g % 2, gw(g))
            layer_norm(3)

        @block.tensor
        def _(pe):
            def mat(name):
                return wts[:, MAT[name], :]

            pe.wait_ge(S("consts"), 9)

            def transposes(buf, g, to):
                for n, i in enumerate(tiles_of(g)):
                    ins = pe.transpose(to[:, n * P:(n + 1) * P], buf(i), ident[:, :])
                return ins

            pe.wait_ge(S("heads_ready"), 1)
            pe.matmul(bank(MISC, HEADS), ones[0:1, :], head_f, start=True, stop=True).then_inc(S("heads_spread"), 1)
            pe.wait_ge(S("xmax_ready"), 1)
            pe.transpose(bank(0)[0:1, 0:P], bound[:, 1:2], ident[:, :]).then_inc(S("xmax_turned"), 1)
            pe.wait_ge(S("xmax_ready"), 2)
            pe.matmul(bank(1, 1), ones[0:1, :], bound[0:1, 2:3], start=True, stop=True).then_inc(S("xmax_spread"), 1)

            def turn_keys(h):
                pe.wait_ge(S("keys_ready"), h + 1)
                for a in range(3):
                    ins = pe.transpose(bank(MISC)[:, a * P:(a + 1) * P], kw[:, a, :], ident[:, :])
                ins.then_inc(S("keys_in_psum"), 1)

            def count(block_i, b):
                s = b % 2
                pe.wait_ge(S("onehots_ready"), NB * block_i + b + 1)
                place = onehot[:, s, 0:OH_A].rearrange("p (c w) -> p c w", w=BW)
                source = onehot[:, s, OH_A:OH_L].rearrange("p (c w) -> p c w", w=BW)
                for j in range(BW // UW):
                    u = b * (BW // UW) + j
                    if not (isinstance(block_i, int) and u < 3):
                        pe.wait_ge(S("evacuated"), block_i * UPB + {0: -3, 1: 0, 2: -1, UPB - 1: UPB - 2}.get(u, u - 2))
                    for w in range(UW):
                        o = ps[:, banks_of(u) + w // 2, w % 2 * AC:(w % 2 + 1) * AC]
                        ins = pe.matmul(o, source[:, :, j * UW + w], place[:, :, j * UW + w], start=True, stop=True)
                    ins.then_inc(S("counts_ready"), 1)
                    if b == 0 and j == 0 and not isinstance(block_i, int):
                        pe.wait_ge(S("outdegrees_taken"), block_i)
                    for w in range(j * UW, (j + 1) * UW):
                        last = pe.matmul(bank(DEG_BANK, NT), source[:, :, w], place[:, T * NT:, w],
                                         start=(b == 0 and w == 0), stop=(b == NB - 1 and w == BW - 1))
                last.then_inc(S("onehots_used"), 1)

            def indegree(h):
                pe.wait_ge(S("keys_taken"), h + 1)
                pe.matmul(bank(MISC, 2 * P), ones_h[:, :], to_dst.rearrange("p w d -> p (w d)"),
                          start=True, stop=True).then_inc(S("degree_ready"), 1)

            pe.wait_ge(S("probe_ready"), 1)
            pe.matmul(bank(DEG_BANK, int(MAXCOUNT)), ones_h[:, :], probe[:, :].bitcast(fp8), start=True, stop=True).then_inc(S("probe_done"), 1)

            turn_keys(0)
            pe.wait_ge(S("probe_done"), 2)
            for b in range(NB):
                count(0, b)
                if b == 0:
                    indegree(0)
            with pe.Fori(0, NH - 1) as k:
                for b in range(NB):
                    count(2 * k + 1, b)
                    if b == 2:
                        pe.wait_ge(S("degree_copied"), k + 1)
                        turn_keys(k + 1)
                for b in range(NB):
                    count(2 * k + 2, b)
                    if b == 0:
                        indegree(k + 1)

            pe.wait_ge(S("holds_counted"), 1)
            pe.matmul(bank(DEG_BANK, 2), ones[:, :], bound[:, 1:3], start=True, stop=True).then_inc(S("holds_summed"), 1)
            any_edges = read_flag(pe)
            with pe.If(any_edges > 0):
                any_edges_tensor(pe, 0)
                for g in range(NG):
                    pe.wait_ge(S("any_degree_in"), 16 * g + 16)
                    if g > 0:
                        pe.wait_ge(S("any_degree_taken"), g)
                    transposes(lambda i: sums_n[:, i % GT, :], g, bank(AGG[0])).then_inc(S("any_degree_turned"), 1)
                any_edges_tensor(pe, 1)
            pe.nop()

            def turn_sums(p, g, b, w):
                pe.wait_ge(S("sums_in"), 16 * g + 16 * (NG * p + 1))
                n = w // P
                pe.sem_inc(S("chunk_used"), NC - n)
                for i in range(n):
                    pe.transpose(bank(AGG[b])[:, i * P:(i + 1) * P], sums_n[:, i, :], ident[:, :]).then_inc(S("chunk_used"), 1)

            def aggregate(p, g, b, w):
                with pe.If(any_edges > 0):
                    turn_sums(p, g, b, w)
                with pe.Else():
                    multiply(p, g, b, w)
                pe.nop()

            def multiply(p, g, b, w):
                gq = NG * p + g
                for c in range(NC):
                    hold(pe, S("chunk_in", c), 16 * gq + 16)
                    if isinstance(g, int) and g == 0:
                        pe.wait_ge(S("parts_ready"), min(NG, (c * CI + CI - 1) // GT + 1) + NG * p)
                    for i in range(CI):
                        moving = ring[:, c, 0:w // P, i * P:(i + 1) * P].bitcast(fp8)
                        for s in range(PARTS):
                            t = c * CI + i
                            ins = pe.matmul(bank(AGG[b], w), parts[:, s, t, :], moving,
                                            start=(t == 0 and s == 0), stop=(t == NT - 1 and s == PARTS - 1))
                    ins.then_inc(S("chunk_used"), 1)

            def turn_result(g, b, w):
                pe.wait_ge(S("proj_used"), g + 1 + NG * 6)
                pe.wait_ge(S("h_taken", 3), g + 1)
                for n in range(w // P):
                    ins = pe.transpose(bank(TR[b])[:, n * P:(n + 1) * P], tmp[:, b, n * P:(n + 1) * P], ident[:, :])
                ins.then_inc(S("h_in_psum", 3), 1)

            def run_pass(p, project, then=None):
                in_lag = GT * P
                with pe.If(any_edges > 0):
                    any_edges_tensor(pe, 2 + p)
                pe.nop()
                def follow(g, b, w):
                    if then:
                        then(g, b, w)
                aggregate(p, 0, 0, in_lag)
                aggregate(p, 1, 1, in_lag)
                lagged(p, 0, 0, in_lag, project)
                with pe.Fori(0, (NG - 3) // 2) as k:
                    aggregate(p, 2 * k + 2, 0, in_lag)
                    follow(2 * k, 0, in_lag)
                    lagged(p, 2 * k + 1, 1, in_lag, project)
                    aggregate(p, 2 * k + 3, 1, in_lag)
                    follow(2 * k + 1, 1, in_lag)
                    lagged(p, 2 * k + 2, 0, in_lag, project)
                aggregate(p, NG - 1, 0, gw(NG - 1))
                follow(NG - 3, 0, in_lag)
                lagged(p, NG - 2, 1, in_lag, project)
                follow(NG - 2, 1, in_lag)
                lagged(p, NG - 1, 0, gw(NG - 1), project)
                follow(NG - 1, 0, gw(NG - 1))

            def lagged(p, g, b, w, project):
                pe.wait_ge(S("agg_copied"), g + 1 + NG * p)
                if not isinstance(g, int) or g > 0:
                    pe.wait_ge(S("proj_used"), g + NG * p)
                project(g, b, w).then_inc(S("proj_done"), 1)

            def features_of(layer, g):
                pe.wait_ge(S("x_ready", layer), g + 1)
                if g >= 2:
                    pe.wait_ge(S("xT_ready"), g - 1 + NG * layer)
                transposes(lambda i: x_nm[:, i, :], g, bank(XT[g % 2])).then_inc(S("xT_in_psum"), 1)

            def turn_both(layer):
                for s in range(NG + 2):
                    if s < NG:
                        pe.wait_ge(S("relu_done"), s + 1 + NG * layer)
                        if s >= 2:
                            pe.wait_ge(S("h_taken", layer), s - 1)
                        transposes(lambda i: hT[:, i * P:(i + 1) * P], s, bank(TR[s % 2])).then_inc(S("h_in_psum", layer), 1)
                    if s >= 2:
                        features_of(layer, s - 2)

            pe.wait_ge(S("mats_in"), 16)
            pe.wait_ge(S("rows_in"), 16)
            pe.wait_ge(S("evacuated"), NT * UPB)
            for n in range(2):
                ins = pe.matmul(bank(XT[n], T * D), ones[0:1, :], rvec[:, n, :], start=True, stop=True)
            ins.then_inc(S("biases_spread"), 1)
            pe.wait_ge(S("squares_ready"), 1)
            pe.matmul(bank(TR[0], T * D), ones[:, :], square, start=True, stop=True).then_inc(S("squares_summed"), 1)
            pe.wait_ge(S("biases_taken"), 1)
            run_pass(0, lambda g, b, w: pe.matmul(bank(PROJ, w), mat("W"), agg_s[:, 0:w], start=True, stop=True))
            turn_both(0)

            def node_update(t):
                def project(g, b, w):
                    if t == 0:
                        pe.wait_ge(S("self_ready"), g + 1)
                    terms = ([(0, tmp[:, b, :])] if t == 0 else []) + [(1 + t, agg_s)]
                    for n in range(w // P):
                        for j, (k, buf) in enumerate(terms):
                            m = MAT[f"Wn{k}0"]
                            ins = pe.matmul(ps[:, PROJ + n, 0:T * D], buf[:, n * P:(n + 1) * P],
                                            wts[:, m:m + T, :].rearrange("p m d -> p (m d)"),
                                            start=(j == 0), stop=(j == len(terms) - 1))
                    return ins
                return project
            for t in range(T):
                if t > 0:
                    pe.wait_ge(S("proj_used"), NG * (t + 1))
                for g in range(NG):
                    if g >= 2:
                        pe.wait_ge(S("bias_added"), g - 1 + NG * t)
                    for n, i in enumerate(tiles_of(g)):
                        o = bank(SRC[g % 2])[:, n * P:(n + 1) * P]
                        ins = pe.matmul(o, xT[:, i * P:(i + 1) * P], mat(f"We{t}"), start=True, stop=True)
                    ins.then_inc(S("src_in_psum"), 1)
                run_pass(1 + t, node_update(t))
            for g in range(NG):
                features_of(1, g)

            pe.wait_ge(S("late_mats_in"), 16)
            run_pass(4, lambda g, b, w: pe.matmul(bank(PROJ, w), mat("W1"), agg_s[:, 0:w], start=True, stop=True))
            for g in range(NG):
                pe.wait_ge(S("relu_done"), g + 1 + NG)
                if g >= 2:
                    pe.wait_ge(S("h2_ready"), g - 1)
                pe.matmul(bank(SRC[g % 2], gw(g)), mat("W2"), hT[:, cols_of(g)], start=True, stop=True).then_inc(S("lin2_done"), 1)
            turn_both(2)

            def sage(p, terms, then=None):
                def project(g, b, w):
                    o = bank(PROJ, w)
                    c = bass.ds(g * (GT * P), w)
                    pe.matmul(o, mat(terms[0]), agg_s[:, 0:w], start=True, stop=False)
                    for n, (m, buf) in enumerate(terms[1:]):
                        ins = pe.matmul(o, mat(m), buf[:, c], start=False, stop=(n == len(terms) - 2))
                    return ins
                run_pass(p, project, then)
            pe.wait_ge(S("squares_ready"), 2)
            pe.matmul(bank(PROJ, 2 * D + 1), ones[:, :], square_l, start=True, stop=True).then_inc(S("squares_summed"), 1)
            pe.wait_ge(S("xT_ready"), NG * 3)
            sage(5, ["f_lw", ("f_rw", xT)])
            pe.wait_ge(S("proj_used"), NG * 6)
            for g in range(NG):
                if g >= 2:
                    pe.wait_ge(S("src_ready", 6), g - 1)
                transposes(lambda i: hT[:, i * P:(i + 1) * P], g, bank(SRC[g % 2])).then_inc(S("src_in_psum"), 1)
            sage(6, ["n_lw", ("n_rw", hT), ("fc", xT)], turn_result)


def kernel(**inputs):
    import numpy as np
    import concourse.bacc as bacc
    from concourse.bass_utils import run_bass_kernel_spmd

    a = {k: np.asarray(v) for k, v in inputs.items()}
    t = lambda w: np.ascontiguousarray(w.T)
    we, wn = a["L1_gnn_W_e"], a["L1_gnn_W_n"]
    D = a["x"].shape[1]
    mats = [a["L0_gnn_W"]] + [we[i].T for i in range(3)]
    mats += [wn[i][:, k * D:(k + 1) * D].T for k in range(4) for i in range(3)]
    mats += [a[f"L2_gnn_{n}"].T for n in ("W1", "W2")]
    mats += [a[f"L3_gnn_{n}"].T for n in ("fc_w", "f_lw", "f_rw", "n_lw", "n_rw")]
    cols = [a[n] for n in ("L0_gnn_b", "L0_gnn_gamma", "L0_gnn_beta", "L2_gnn_b1", "L2_gnn_g1", "L2_gnn_beta1",
                           "L2_gnn_b2", "L2_gnn_g2", "L2_gnn_beta2", "L3_gnn_f_lb", "L3_gnn_n_lb", "L3_gnn_fc_b")]
    rows = [a["L1_gnn_b_e"].reshape(-1), a["L1_gnn_b_n"].reshape(-1)]
    arrays = {
        "x": a["x"],
        "edges": np.ascontiguousarray(np.stack([a["src"], a["dst"], a["edge_type_3"]], axis=1)),
        "dst": a["dst"],
        "node_type": a["node_type_3"],
        "mats": np.ascontiguousarray(np.concatenate(mats, axis=1)),
        "cols": np.ascontiguousarray(np.stack(cols, axis=1)),
        "rows": np.ascontiguousarray(np.stack(rows, axis=0)),
        "eps2": a["L2_gnn_eps"],
    }
    nc = bacc.Bacc("TRN2", target_bir_lowering=False, num_devices=1)
    args = [nc.dram_tensor(n, v.shape, mybir.dt.from_np(v.dtype), kind="ExternalInput").ap() for n, v in arrays.items()]
    out = nc.dram_tensor("out", a["x"].shape, mybir.dt.float32, kind="ExternalOutput").ap()
    gnn_resnorm_kernel(nc, *args, out)
    r = run_bass_kernel_spmd(nc, [arrays], core_ids=[0])
    return r.results[0]["out"]
```
